# Optimizing a Trainium2 kernel written in Bass

```python
import numpy as np
import jax
import jax.numpy as jnp

def _softmax(x, axis=-1):
    return jax.nn.softmax(x, axis=axis)

def _gelu(x):
    return jax.nn.gelu(x, approximate=True)

def _silu(x):
    return jax.nn.silu(x)

def _sigmoid(x):
    return jax.nn.sigmoid(x)

def _layernorm(x, axis=-1, eps=1e-05):
    m = jnp.mean(x, axis=axis, keepdims=True)
    v = jnp.var(x, axis=axis, keepdims=True)
    return (x - m) / jnp.sqrt(v + eps)

def _scatter_add(tgt, idx, src, axis=0):
    return tgt.at[idx].add(src)

def _segment_sum(src, seg, n):
    return jax.ops.segment_sum(src, seg, n)
kernel_name = 'mk_gps_d1_gnn_r8_e0ec76'

def setup_inputs(seed: int=0):
    np.random.seed(seed)
    _w = jnp.asarray

    def _rec_inputs():
        import jax
        import jax.numpy as jnp
        _gk = jax.random.key(seed)
        x = -0.0003713 + 1 * jax.random.normal(jax.random.fold_in(_gk, 1), (6250, 256), jnp.float32)
        src = jax.random.randint(jax.random.fold_in(_gk, 2), (200000,), 0, 6250, jnp.int32)
        dst = jnp.minimum((6250 * jax.random.uniform(jax.random.fold_in(_gk, 3), (200000,)) ** 2.0).astype(jnp.int32), 49999)
        _o = jnp.argsort(dst, stable=True)
        src = src[_o]
        dst = dst[_o]
        return (x, src, dst)
    x, src, dst = _rec_inputs()

    def _L0_gnn_setup():
        import jax, jax.numpy as jnp
        import numpy as np
        N = 6250
        E = 200000
        DIN = 256
        DOUT = 64
        HEADS = 4
        SLOPE = 0.2
        key = jax.random.key(seed)
        k = jax.random.split(key, 7)
        h = jax.random.normal(k[0], (N, DIN), dtype=jnp.float32)
        W = jax.random.normal(k[1], (DIN, DOUT), dtype=jnp.float32) * 0.05
        b = jnp.zeros((DOUT,), dtype=jnp.float32)
        a_src = jax.random.normal(k[2], (HEADS, DOUT), dtype=jnp.float32) * 0.05
        a_dst = jax.random.normal(k[3], (HEADS, DOUT), dtype=jnp.float32) * 0.05
        row = jnp.sort(jax.random.randint(k[4], (E,), 0, N, dtype=jnp.int32))
        col = jax.random.randint(k[5], (E,), 0, N, dtype=jnp.int32)
        return {'h': h, 'W': W, 'b': b, 'a_src': a_src, 'a_dst': a_dst, 'row': row, 'col': col}
    _L0_gnn_all = _L0_gnn_setup()
    _L0_gnn_in = {k: v for k, v in _L0_gnn_all.items() if k in ('W', 'b', 'a_src', 'a_dst')}
    del _L0_gnn_all

    def _L0_mix_setup():
        import jax, jax.numpy as jnp
        import numpy as np
        NHEAD = 8
        ATT_EPS = 1e-06
        LN_EPS = 1e-05

        def _layernorm(x, g, b):
            mu = jnp.mean(x, axis=-1, keepdims=True)
            var = jnp.mean(jnp.square(x - mu), axis=-1, keepdims=True)
            return (x - mu) * jax.lax.rsqrt(var + LN_EPS) * g + b
        key = jax.random.key(seed)
        ks = jax.random.split(key, 7)
        N, L, C = (4, 2048, 256)
        s = 1.0 / np.sqrt(C)
        return {'x': jax.random.normal(ks[0], (N, L, C), jnp.float32), 'Wq': jax.random.normal(ks[1], (C, C), jnp.float32) * s, 'Wk': jax.random.normal(ks[2], (C, C), jnp.float32) * s, 'Wv': jax.random.normal(ks[3], (C, C), jnp.float32) * s, 'Wm': jax.random.normal(ks[4], (C, C), jnp.float32) * s, 'W1': jax.random.normal(ks[5], (2 * C, 2 * C), jnp.float32) * (1.0 / np.sqrt(2 * C)), 'W2': jax.random.normal(ks[6], (2 * C, C), jnp.float32) * (1.0 / np.sqrt(2 * C)), 'g1': jnp.ones((C,), jnp.float32), 'b1': jnp.zeros((C,), jnp.float32), 'g2': jnp.ones((C,), jnp.float32), 'b2': jnp.zeros((C,), jnp.float32)}
    _L0_mix_all = _L0_mix_setup()
    _L0_mix_in = {k: v for k, v in _L0_mix_all.items() if k in ('Wq', 'Wk', 'Wv', 'Wm', 'W1', 'W2', 'g1', 'b1', 'g2', 'b2')}
    del _L0_mix_all

    def _L0_ffn_setup():
        import jax, jax.numpy as jnp
        import numpy as np
        B, K, D = (512, 16, 256)
        E = 32
        H = int(D * 0.25)
        key = jax.random.key(seed)
        ks = jax.random.split(key, 7)
        d_rs = D ** (-0.5)
        h_rs = H ** (-0.5)
        x = jax.random.normal(ks[0], (B, K, D), dtype=jnp.float32)
        router_w = jax.random.uniform(ks[1], (E, D), jnp.float32, -d_rs, d_rs)
        router_b = jax.random.uniform(ks[2], (E,), jnp.float32, -d_rs, d_rs)
        W1 = jax.random.uniform(ks[3], (E, D, H), jnp.float32, -h_rs, h_rs)
        b1 = jax.random.uniform(ks[4], (E, H), jnp.float32, -h_rs, h_rs)
        W2 = jax.random.uniform(ks[5], (E, H, D), jnp.float32, -d_rs, d_rs)
        b2 = jax.random.uniform(ks[6], (E, D), jnp.float32, -d_rs, d_rs)
        return {'x': x, 'router_w': router_w, 'router_b': router_b, 'W1': W1, 'b1': b1, 'W2': W2, 'b2': b2}
    _L0_ffn_all = _L0_ffn_setup()
    _L0_ffn_in = {k: v for k, v in _L0_ffn_all.items() if k in ('router_w', 'router_b', 'W1', 'b1', 'W2', 'b2')}
    del _L0_ffn_all
    return {'x': x, 'src': src, 'dst': dst, 'L0_gnn_W': _L0_gnn_in['W'], 'L0_gnn_b': _L0_gnn_in['b'], 'L0_gnn_a_src': _L0_gnn_in['a_src'], 'L0_gnn_a_dst': _L0_gnn_in['a_dst'], 'L0_mix_Wq': _L0_mix_in['Wq'], 'L0_mix_Wk': _L0_mix_in['Wk'], 'L0_mix_Wv': _L0_mix_in['Wv'], 'L0_mix_Wm': _L0_mix_in['Wm'], 'L0_mix_W1': _L0_mix_in['W1'], 'L0_mix_W2': _L0_mix_in['W2'], 'L0_mix_g1': _L0_mix_in['g1'], 'L0_mix_b1': _L0_mix_in['b1'], 'L0_mix_g2': _L0_mix_in['g2'], 'L0_mix_b2': _L0_mix_in['b2'], 'L0_ffn_router_w': _L0_ffn_in['router_w'], 'L0_ffn_router_b': _L0_ffn_in['router_b'], 'L0_ffn_W1': _L0_ffn_in['W1'], 'L0_ffn_b1': _L0_ffn_in['b1'], 'L0_ffn_W2': _L0_ffn_in['W2'], 'L0_ffn_b2': _L0_ffn_in['b2']}

def reference(x, src, dst, L0_gnn_W, L0_gnn_b, L0_gnn_a_src, L0_gnn_a_dst, L0_mix_Wq, L0_mix_Wk, L0_mix_Wv, L0_mix_Wm, L0_mix_W1, L0_mix_W2, L0_mix_g1, L0_mix_b1, L0_mix_g2, L0_mix_b2, L0_ffn_router_w, L0_ffn_router_b, L0_ffn_W1, L0_ffn_b1, L0_ffn_W2, L0_ffn_b2):
    import jax
    import jax.numpy as jnp

    def _L0_gnn_ref(h, W, b, a_src, a_dst, row, col):
        import jax, jax.numpy as jnp
        import numpy as np
        N = 6250
        E = 200000
        DIN = 256
        DOUT = 64
        HEADS = 4
        SLOPE = 0.2
        hW = h @ W + b
        s = hW @ a_src.T
        d = hW @ a_dst.T
        outs = []
        for head in range(HEADS):
            e = jax.nn.leaky_relu(s[row, head] + d[col, head], negative_slope=SLOPE)
            m = jax.lax.stop_gradient(jax.ops.segment_max(e, row, num_segments=N))
            ex = jnp.exp(e - m[row])
            den = jax.ops.segment_sum(ex, row, num_segments=N)
            alpha = ex / den[row]
            outs.append(jax.ops.segment_sum(alpha[:, None] * hW[col], row, num_segments=N))
        return jnp.concatenate(outs, axis=1)

    def _L0_mix_ref(x, Wq, Wk, Wv, Wm, W1, W2, g1, b1, g2, b2):
        import jax, jax.numpy as jnp
        import numpy as np
        NHEAD = 8
        ATT_EPS = 1e-06
        LN_EPS = 1e-05

        def _layernorm(x, g, b):
            mu = jnp.mean(x, axis=-1, keepdims=True)
            var = jnp.mean(jnp.square(x - mu), axis=-1, keepdims=True)
            return (x - mu) * jax.lax.rsqrt(var + LN_EPS) * g + b
        N, L, C = x.shape
        H = NHEAD
        D = C // H
        q = (x @ Wq).reshape(N, L, H, D)
        k = (x @ Wk).reshape(N, L, H, D)
        v = (x @ Wv).reshape(N, L, H, D)
        Q = jax.nn.elu(q) + 1.0
        K = jax.nn.elu(k) + 1.0
        v = v / L
        KV = jnp.einsum('nshd,nshv->nhdv', K, v)
        Z = 1.0 / (jnp.einsum('nlhd,nhd->nlh', Q, K.sum(axis=1)) + ATT_EPS)
        msg = jnp.einsum('nlhd,nhdv,nlh->nlhv', Q, KV, Z) * L
        msg = msg.reshape(N, L, C) @ Wm
        msg = _layernorm(msg, g1, b1)
        h = jnp.concatenate([x, msg], axis=-1) @ W1
        h = jax.nn.relu(h) @ W2
        msg = _layernorm(h, g2, b2)
        return x + msg

    def _L0_ffn_ref(x, router_w, router_b, W1, b1, W2, b2):
        import jax, jax.numpy as jnp
        import numpy as np
        B, K, D = (512, 16, 256)
        E = 32
        H = int(D * 0.25)
        xf = x.reshape(-1, D)
        logits = xf @ router_w.T + router_b
        idx = jnp.argmax(logits, axis=-1)
        w1t = jnp.take(W1, idx, axis=0)
        h = jnp.einsum('nd,ndh->nh', xf, w1t) + jnp.take(b1, idx, axis=0)
        h = jax.nn.relu(h)
        w2t = jnp.take(W2, idx, axis=0)
        out = jnp.einsum('nh,nhd->nd', h, w2t) + jnp.take(b2, idx, axis=0)
        out = jax.nn.relu(out)
        return out.reshape(x.shape)
    xn = _layernorm(x, axis=-1)
    x = x + _L0_gnn_ref(xn, L0_gnn_W, L0_gnn_b, L0_gnn_a_src, L0_gnn_a_dst, src, dst) + _L0_mix_ref(xn[None], L0_mix_Wq, L0_mix_Wk, L0_mix_Wv, L0_mix_Wm, L0_mix_W1, L0_mix_W2, L0_mix_g1, L0_mix_b1, L0_mix_g2, L0_mix_b2)[0]
    x = x + _L0_ffn_ref(_layernorm(x, axis=-1)[None], L0_ffn_router_w, L0_ffn_router_b, L0_ffn_W1, L0_ffn_b1, L0_ffn_W2, L0_ffn_b2)[0]
    return x

_drawn_inputs = setup_inputs


def setup_inputs(seed=0):
    import zlib

    import numpy as np

    out = dict(_drawn_inputs(seed))
    spreads = {'L0_gnn_b': (0.0, 0.1),
     'L0_mix_g1': (1.0, 0.2),
     'L0_mix_b1': (0.0, 0.1),
     'L0_mix_g2': (1.0, 0.2),
     'L0_mix_b2': (0.0, 0.1)}
    factors = {'L0_gnn_a_src': 6.278,
     'L0_gnn_a_dst': 2.909,
     'L0_ffn_router_b': 2.674,
     'L0_ffn_b1': 8.0,
     'L0_ffn_b2': 5.165}
    for name, (base, spread) in spreads.items():
        noise = np.random.default_rng([zlib.crc32(name.encode()), seed]).standard_normal(out[name].shape)
        drawn = base * np.exp(spread * noise) if base else spread * noise
        out[name] = jnp.asarray(drawn.astype(out[name].dtype))
    for name, factor in factors.items():
        out[name] = (out[name] * factor).astype(out[name].dtype)
    return out
```

```python
import concourse.bass as bass
from concourse import mybir
from contextlib import ExitStack

N, C, E = 6250, 256, 200000
P = 128
TOK = -(-N // P)
NP = TOK * P
HEADS, DOUT = 4, 64
SLOPE = 0.2
TABW = 72
DCOL = DOUT + 1
AGG = HEADS * (DOUT + 1)
STAGE = 32
EC = -(-E // (P * STAGE)) * STAGE
TURNS = EC // STAGE
BT = 4
BE = BT * P
NB = (P * EC - TOK) // BE + TOK
GB = 2
NB = -(-NB // (2 * GB)) * (2 * GB)
GT = GB * BT
GROUPS = NB // GB
ET = NB * BT
NONE = 255
FAR = -1e30
MH, MD = 8, 32
HID = 512
EXP, EH = 32, 64
ATT_EPS, LN_EPS = 1e-6, 1e-5

fp32 = mybir.dt.float32
bf16 = mybir.dt.bfloat16
i32 = mybir.dt.int32
u32 = mybir.dt.uint32
ALU = mybir.AluOpType
ACT = mybir.ActivationFunctionType
AX = mybir.AxisListType


class Link:

    def __init__(self, eng, sem, pause):
        self.eng, self.sem, self.pause, self.base, self.n = eng, sem, pause, 0, 0

    def settle(self):
        self.eng.sem_inc(self.pause, 1)

    def loop(self, i, per):
        self.base, self.n = self.base0 + i * per, 0

    def enter(self):
        self.base0 = self.base + self.n

    def leave(self, total):
        self.base, self.n = self.base0 + total, 0

    def __call__(self, ins):
        self.n += 1
        ins.then_inc(self.sem, 1)
        self.eng.wait_ge(self.sem, self.base + self.n)


def build(nc, x, row, col, W, WT, b, a, Wqkv, Wm, W1, W2, lnp, rwT, rb, E1, b1, E2, b2, out, dbg=None):
    table = nc.dram_tensor("table", (NP, TABW), fp32).ap()
    slots = nc.dram_tensor("slots", (P * ET, 1), i32).ap()
    spill = nc.dram_tensor("spill", (GROUPS, P, GT * TABW), fp32).ap()
    ctx = ExitStack()
    with ctx:
        def sb(name, shape, dt, c=ctx):
            return c.enter_context(nc.sbuf_tensor(name, shape, dt))

        def ps(name, shape, c=ctx, dt=fp32):
            return c.enter_context(nc.psum_tensor(name, shape, dt))

        def sem(name):
            return ctx.enter_context(nc.semaphore(name))

        pause = {e: sem("pause_" + e) for e in ("dve", "act", "pool", "pe")}

        x2 = sb("x2", [P, TOK, C], fp32)
        s_res = sb("s_res", [P, TOK, HEADS], fp32)
        ident = sb("ident", [P, P], fp32)
        iota_f = sb("iota_f", [P, P], fp32)
        pcol = sb("pcol", [P, 1], fp32)
        ones = sb("ones", [P, P], fp32)
        bid_i = sb("bid_i", [1, NB], i32)
        lnb = sb("lnb", [P, 4, C], fp32)

        phase1(nc, ctx, locals())
        phase2(nc, locals())
        phase3(nc, locals())


NEWTON = 3
RSQRT_STEPS = 2 + 3 * NEWTON


def rsqrt(V, link, y, var, t):
    link(V.tensor_scalar(var, var, LN_EPS, None, ALU.add))
    link(V.tensor_scalar(y.bitcast(i32), var.bitcast(i32), -0.5, float(0x5F3759DF), ALU.mult, ALU.add))
    for _ in range(NEWTON):
        link(V.scalar_tensor_tensor(t, y, y, var, ALU.mult, ALU.mult))
        link(V.tensor_scalar(t, t, -0.5, 1.5, ALU.mult, ALU.add))
        link(V.tensor_tensor(y, y, t, ALU.mult))


def phase1(nc, octx, v):
    x, row, col, W, WT, b, a = (v[k] for k in ("x", "row", "col", "W", "WT", "b", "a"))
    Wqkv, Wm, W1, W2, lnp = (v[k] for k in ("Wqkv", "Wm", "W1", "W2", "lnp"))
    table, slots = v["table"], v["slots"]
    x2, s_res, ident, iota_f, pcol, ones, bid_i, lnb = (v[k] for k in (
        "x2", "s_res", "ident", "iota_f", "pcol", "ones", "bid_i", "lnb"))
    pause, sem = v["pause"], v["sem"]
    ctx = ExitStack()
    with ctx:
        def sb(name, shape, dt):
            return ctx.enter_context(nc.sbuf_tensor(name, shape, dt))

        def ps(name, shape):
            return ctx.enter_context(nc.psum_tensor(name, shape, fp32))

        rec = sb("rec", [P, EC], i32)
        addr = sb("addr", [P, EC], i32)
        blk = sb("blk", [P, EC], fp32)
        pos = sb("pos", [P, EC], fp32)
        eq = sb("eq", [P, EC], fp32)
        cum = sb("cum", [P, EC], fp32)
        cnt = sb("cnt", [P, TOK], fp32)
        base = sb("base", [P, TOK], fp32)
        tot = sb("tot", [P, TOK], fp32)
        tot_i = sb("tot_i", [P, TOK], i32)
        ends = sb("ends", [P, TOK], fp32)
        before = sb("before", [P, P], fp32)
        rec_s = sb("rec_s", [P, STAGE], i32)
        addr_s = sb("addr_s", [P, STAGE], i32)
        biota = sb("biota", [1, NB], fp32)
        bidf = sb("bidf", [1, NB], fp32)
        wcat = sb("wcat", [P, 2, TABW + 1], fp32)
        brow = sb("brow", [1, TABW + 1], fp32)
        wT = sb("wT", [DOUT, C], fp32)
        aT = sb("aT", [DOUT, 2 * HEADS], fp32)
        bcol = sb("bcol", [DOUT, 1], fp32)
        wqkv = sb("wqkv", [P, 2, 3 * C], fp32)
        wm = sb("wm", [P, 2, C], fp32)
        w1 = sb("w1", [P, 4, HID], fp32)
        w2 = sb("w2", [P, 4, C], fp32)
        blockm = sb("blockm", [P, P], fp32)
        valid = sb("valid", [P, TOK], fp32)
        kvb = sb("kvb", [P, 2, P], fp32)
        ksb = sb("ksb", [P, 2, P], fp32)
        kvacc = sb("kvacc", [P, 2, P + 1], fp32)
        xnT = sb("xnT", [P, 2, NP], fp32)
        xt = sb("xt", [P, C], fp32)
        xn = sb("xn", [P, C], fp32)
        st = sb("st", [P, 6], fp32)
        mv = sb("mv", [P, 2], fp32)
        rstd = sb("rstd", [P, 1], fp32)
        rt = sb("rt", [P, 1], fp32)
        xTs = sb("xTs", [P, 2, P], fp32)
        tab = sb("tab", [P, TABW], fp32)
        kmin = sb("kmin", [P, C], fp32)
        kexp = sb("kexp", [P, C], fp32)
        kk = sb("kk", [P, C], fp32)
        va = sb("va", [P, 2, P + 1], fp32)
        rec_d = sb("rec_d", [P, C], fp32)
        msgT = sb("msgT", [P, C], fp32)
        m1 = sb("m1", [P, C], fp32)
        m1T = sb("m1T", [P, 2, P], fp32)
        hT = sb("hT", [P, 4, P], fp32)

        ps_cnt = ps("ps_cnt", [P, 2, P])
        psT = ps("psT", [P, 2, P])
        ps_kv = ps("ps_kv", [P, 512])
        ps_h = ps("ps_h", [P, 512])
        ps_KV = ps("ps_KV", [P, 2, 256])
        ps_dm = ps("ps_dm", [P, 512])
        ps_o = ps("ps_o", [P, C])

        rows_in, w_in, ln_in, filled, consts = (sem(k) for k in ("rows_in", "w_in", "ln_in", "filled", "consts"))
        edges_ready, fill_ready, counted, ranked, based = (sem(k) for k in (
            "edges_ready", "fill_ready", "counted", "ranked", "based"))
        wa_ready, wa_done, bid_ready = sem("wa_ready"), sem("wa_done"), sem("bid_ready")
        staged, scattered, stage_free = sem("staged"), sem("scattered"), sem("stage_free")
        x_in, x_used, xn_ready, xT_ready, xTs_ready, kv_ready, kmin_ready, kexp_ready, k_ready, KV_ready = (
            sem(k) for k in ("x_in", "x_used", "xn_ready", "xT_ready", "xTs_ready", "kv_ready", "kmin_ready",
                             "kexp_ready", "k_ready", "KV_ready"))
        tab_ready, tab_out, tab_free = sem("tab_ready"), sem("tab_out"), sem("tab_free")
        xT_stored, va_ready = sem("xT_stored"), sem("va_ready")
        kvb_ready, q_ready, qmin_ready, qexp_ready, q_done, dm_ready, msg_ready, m_ready, m1_ready, m1T_ps, m1T_ready, \
            h_ready, hT_ready, o_ready, mixed = (sem(k) for k in (
                "kvb_ready", "q_ready", "qmin_ready", "qexp_ready", "q_done", "dm_ready", "msg_ready", "m_ready",
                "m1_ready", "m1T_ps", "m1T_ready", "h_ready", "hT_ready", "o_ready", "mixed"))
        KV_used, o_used = sem("KV_used"), sem("o_used")
        dve_chain = sem("dve_chain")
        pool_const = sem("pool_const")

        block = ctx.enter_context(nc.Block())

        @block.sync
        def _(sp):
            sp.dma_start(rec[:, :], row).then_inc(rows_in, 16)
            sp.dma_start(addr[:, :], col).then_inc(rows_in, 16)
            for dst, src in ((wcat[:, :, 0:DOUT], W.rearrange("(k p) n -> p k n", p=P)), (wT[:, :], WT), (aT[:, :], a),
                             (bcol[:, :], b), (brow[:, 0:DOUT], b.rearrange("n o -> o n")),
                             (wqkv[:, :, :], Wqkv.rearrange("(k p) n -> p k n", p=P)),
                             (wm[:, :, :], Wm.rearrange("(k p) n -> p k n", p=P)),
                             (w1[:, :, :], W1.rearrange("(k p) n -> p k n", p=P)),
                             (w2[:, :, :], W2.rearrange("(k p) n -> p k n", p=P))):
                sp.dma_start(dst, src).then_inc(w_in, 16)
            sp.wait_ge(fill_ready, 1)
            sp.dma_start(slots.rearrange("(p e) o -> p (e o)", p=P), xnT[:, 0, 0:ET].bitcast(i32)).then_inc(filled, 16)
            with sp.Fori(0, TOK) as i:
                sp.wait_ge(x_used, i + 1)
                sp.dma_start(xt[:, :], x[bass.ds(i * P, P), :]).then_inc(x_in, 16)
                sp.wait_ge(tab_ready, i + 1)
                sp.dma_start(table[bass.ds(i * P, P), :], tab[:, :]).then_inc(tab_out, 16)
                sp.wait_ge(tab_out, i * 16 + 16)
                sp.sem_inc(tab_free, 1)

        @block.gpsimd
        def _(pool):
            pool.memset(ones[:, :], 1.0).then_inc(consts, 1)
            pool.memset(ident[:, :], 1.0).then_inc(pool_const, 1)
            pool.memset(before[:, :], 1.0).then_inc(pool_const, 1)
            pool.memset(blockm[:, :], 1.0).then_inc(pool_const, 1)
            pool.wait_ge(pool_const, 3)
            pool.affine_select(out=ident[:, :], in_=ident[:, :], compare_op=ALU.is_equal, fill=0.0, base=0,
                               pattern=[[-1, P]], channel_multiplier=1).then_inc(consts, 1)
            pool.affine_select(out=before[:, :], in_=before[:, :], compare_op=ALU.is_gt, fill=0.0, base=0,
                               pattern=[[1, P]], channel_multiplier=-1).then_inc(consts, 1)
            bm = blockm[:, :].rearrange("p (a c) -> p a c", c=MD)
            pool.affine_select(out=bm, in_=bm, compare_op=ALU.is_ge, fill=0.0, base=0,
                               pattern=[[-MD, P // MD], [0, MD]], channel_multiplier=1).then_inc(pool_const, 1)
            pool.wait_ge(pool_const, 4)
            pool.affine_select(out=bm, in_=bm, compare_op=ALU.is_ge, fill=0.0, base=MD - 1,
                               pattern=[[MD, P // MD], [0, MD]], channel_multiplier=-1).then_inc(consts, 1)
            for t, pattern, up in ((iota_f, [[1, P]], 0), (pcol, [[0, 1]], 1), (valid, [[P, TOK]], 1),
                                   (biota, [[1, NB]], 0)):
                pool.iota(t[:, :], pattern, base=0, channel_multiplier=up,
                          allow_small_or_imprecise_dtypes=True).then_inc(consts, 1)
            for c in range(4):
                pool.dma_start(lnb[:, c, :], lnp[c:c + 1, :].to_broadcast([P, C])).then_inc(ln_in, 16)
            pool.wait_ge(ln_in, 64)
            pool.wait_ge(filled, 16)
            assert TURNS == TOK
            with pool.Fori(0, TURNS) as i:
                pool.wait_ge(staged, i + 1)
                pool.sem_inc(pause["pool"], 1)
                for k in range(STAGE):
                    pool.indirect_dma_start(slots, bass.IndirectOffsetOnAxis(ap=addr_s[:, k:k + 1].bitcast(u32), axis=0),
                                            rec_s[:, k:k + 1], None).then_inc(scattered, 16)
                pool.wait_ge(scattered, i * (16 * STAGE) + 16 * STAGE)
                pool.sem_inc(stage_free, 1)

        @block.scalar
        def _(act):
            act.wait_ge(wa_ready, 1)
            nc.scalar.copy(wcat[:, :, DCOL:TABW + 1], ps_h[:, 0:16].rearrange("p (k n) -> p k n", k=2)).then_inc(wa_done, 1)
            nc.scalar.copy(brow[:, DCOL:TABW + 1], ps_h[0:1, 16:24]).then_inc(wa_done, 1)
            with act.Fori(0, TOK) as i:
                act.wait_ge(xT_ready, i + 1)
                nc.scalar.copy(xTs[:, :, :], psT[:, :, :]).then_inc(xTs_ready, 1)
                act.wait_ge(kmin_ready, i + 1)
                nc.scalar.activation(kexp[:, :], kmin[:, :], ACT.Exp).then_inc(kexp_ready, 1)
                act.wait_ge(tab_free, i + 1)
                nc.scalar.copy(tab[:, :], ps_h[:, 0:TABW]).then_inc(tab_ready, 1)
            with act.Fori(0, TOK) as i:
                act.wait_ge(qmin_ready, i + 1)
                nc.scalar.activation(kexp[:, :], kmin[:, :], ACT.Exp).then_inc(qexp_ready, 1)
                act.wait_ge(m1T_ps, i + 1)
                nc.scalar.copy(m1T[:, :, :], psT[:, :, :]).then_inc(m1T_ready, 1)
                act.wait_ge(h_ready, i + 1)
                nc.scalar.activation(hT[:, :, :], ps_h[:, :].rearrange("p (m t) -> p m t", m=4), ACT.Relu).then_inc(hT_ready, 1)

        @block.vector
        def _(dve):
            link = Link(dve, dve_chain, pause["dve"])
            V = nc.vector
            dve.sem_inc(x_used, 1)
            dve.sem_inc(tab_free, 1)
            V.memset(xnT[:, 0, 0:ET].bitcast(i32), NONE).then_inc(fill_ready, 1)
            V.memset(wcat[:, :, DOUT:DCOL], 0.0)
            V.memset(brow[:, DOUT:DCOL], 1.0).then_inc(wa_done, 1)
            dve.wait_ge(rows_in, 32)
            link(V.tensor_scalar(cum[:, :].bitcast(i32), rec[:, :], 7, None, ALU.arith_shift_right))
            link(V.tensor_copy(blk[:, :], cum[:, :].bitcast(i32)))
            link(V.tensor_scalar(eq[:, :].bitcast(i32), rec[:, :], P - 1, None, ALU.bitwise_and))
            link(V.tensor_scalar(cum[:, :].bitcast(i32), addr[:, :], 8, None, ALU.logical_shift_left))
            link(V.tensor_tensor(rec[:, :], cum[:, :].bitcast(i32), eq[:, :].bitcast(i32), ALU.bitwise_or))
            link(V.memset(pos[:, :], 0.0))
            link(V.memset(bidf[:, :], 0.0))
            dve.wait_ge(consts, 8)
            link(V.tensor_scalar(valid[:, :], valid[:, :], float(N), None, ALU.is_lt))
            link.enter()
            with dve.Fori(0, TOK) as b_:
                link.loop(b_, 1)
                link(V.tensor_scalar(eq[:, :], blk[:, :], iota_f[:, bass.ds(b_, 1)], 0.0, ALU.is_equal, ALU.add,
                                     accum_out=cnt[:, bass.ds(b_, 1)]))
                link.settle()
            link.leave(TOK)
            dve.sem_inc(counted, 1)
            dve.wait_ge(ranked, 1)
            link(V.tensor_scalar(tot_i[:, :], ps_cnt[:, 1, 0:TOK], float(BE - 1), None, ALU.add))
            link(V.tensor_scalar(tot_i[:, :], tot_i[:, :], BE.bit_length() - 1, None, ALU.arith_shift_right))
            link(V.tensor_copy(tot[:, :], tot_i[:, :]))
            link(V.tensor_tensor_scan(ends[:, :], ones[:, 0:TOK], tot[:, :], 0.0, ALU.mult, ALU.add))
            link(V.tensor_tensor(base[:, :], ends[:, :], tot[:, :], ALU.subtract))
            link(V.scalar_tensor_tensor(base[:, :], base[:, :], float(BE), ps_cnt[:, 0, 0:TOK], ALU.mult, ALU.add))
            link(V.tensor_scalar(base[:, :], base[:, :], -1.0, None, ALU.add))
            link.enter()
            with dve.Fori(0, TOK) as b_:
                link.loop(b_, 5)
                link(V.tensor_scalar(eq[:, :], blk[:, :], iota_f[:, bass.ds(b_, 1)], None, ALU.is_equal))
                link(V.tensor_tensor_scan(cum[:, :], ones[:, 0:1].to_broadcast([P, EC]), eq[:, :], 0.0, ALU.mult, ALU.add))
                link(V.scalar_tensor_tensor(cum[:, :], cum[:, :], base[:, bass.ds(b_, 1)], eq[:, :], ALU.add, ALU.mult))
                link(V.tensor_tensor(pos[:, :], pos[:, :], cum[:, :], ALU.add))
                link(V.scalar_tensor_tensor(bidf[:, :], biota[:, :], ends[0:1, bass.ds(b_, 1)], bidf[:, :], ALU.is_ge, ALU.add))
                link.settle()
            link.leave(5 * TOK)
            link(V.tensor_scalar(bidf[:, :], bidf[:, :], float(TOK - 1), None, ALU.min))
            link(V.tensor_copy(bid_i[:, :], bidf[:, :]))
            link(V.tensor_copy(addr[:, :], pos[:, :]))
            link(V.tensor_scalar(eq[:, :].bitcast(i32), addr[:, :], P - 1, None, ALU.bitwise_and))
            link(V.tensor_scalar(cum[:, :].bitcast(i32), addr[:, :], 7, None, ALU.arith_shift_right))
            link(V.scalar_tensor_tensor(addr[:, :], eq[:, :].bitcast(i32), float(ET), cum[:, :].bitcast(i32), ALU.mult, ALU.add))
            dve.sem_inc(stage_free, 1)
            dve.wait_ge(filled, 16)

            def turn(i):
                dve.wait_ge(stage_free, i + 1)
                link(V.tensor_copy(rec_s[:, :], rec[:, bass.ds(i * STAGE, STAGE)]))
                link(V.tensor_copy(addr_s[:, :], addr[:, bass.ds(i * STAGE, STAGE)]))
                dve.sem_inc(staged, 1)

            def norm(src, dst):
                link(V.bn_stats(st[:, :], src))
                link.settle()
                link(V.bn_aggr(mv[:, :], st[:, :]))
                rsqrt(V, link, rstd[:, :], mv[:, 1:2], rt[:, :])
                link(V.tensor_scalar(dst, src, mv[:, 0:1], rstd[:, :], ALU.subtract, ALU.mult))

            link(V.memset(kvacc[:, :, :], 0.0))
            link.enter()
            with dve.Fori(0, TOK) as i:
                link.loop(i, 11 + RSQRT_STEPS)
                dve.wait_ge(x_in, i * 16 + 16)
                norm(xt[:, :], xn[:, :])
                dve.sem_inc(xn_ready, 1)
                link(V.tensor_tensor(x2[:, bass.ds(i, 1), :], xt[:, :].unsqueeze(1), xn[:, :].unsqueeze(1), ALU.add))
                dve.sem_inc(x_used, 1)
                dve.wait_ge(xTs_ready, i + 1)
                link(V.tensor_copy(xnT[:, :, bass.ds(i * P, P)], xTs[:, :, :]))
                dve.wait_ge(kv_ready, i + 1)
                link(V.tensor_scalar(kmin[:, :], ps_kv[:, 0:C], 0.0, None, ALU.min))
                dve.sem_inc(kmin_ready, 1)
                link(V.tensor_copy(va[:, :, 0:P], ps_kv[:, C:2 * C].rearrange("p (g n) -> p g n", g=2)))
                link(V.tensor_copy(va[:, :, P:P + 1], valid[:, bass.ds(i, 1)].unsqueeze(1).to_broadcast([P, 2, 1])))
                dve.wait_ge(kexp_ready, i + 1)
                link(V.scalar_tensor_tensor(kk[:, :], ps_kv[:, 0:C], 0.0, kexp[:, :], ALU.max, ALU.add))
                dve.sem_inc(k_ready, 1)
                dve.wait_ge(KV_ready, i + 1)
                link(V.tensor_tensor(kvacc[:, :, :], kvacc[:, :, :], ps_KV[:, :, 0:P + 1], ALU.add))
                dve.wait_ge(tab_ready, i + 1)
                link(V.tensor_copy(s_res[:, bass.ds(i, 1), :], ps_h[:, DCOL + HEADS:TABW + 1].unsqueeze(1)))
                dve.sem_inc(KV_used, 1)
                assert link.n == 11 + RSQRT_STEPS
            link.leave((11 + RSQRT_STEPS) * TOK)
            for g in range(2):
                link(V.tensor_tensor(kvb[:, g, :], kvacc[:, g, 0:P], blockm[:, :], ALU.mult))
                link(V.tensor_scalar(ksb[:, g, :], blockm[:, :], kvacc[:, g, P:P + 1], None, ALU.mult))
            dve.sem_inc(kvb_ready, 1)
            dve.wait_ge(ln_in, 64)
            link.enter()
            with dve.Fori(0, TOK) as i:
                link.loop(i, 18 + 2 * RSQRT_STEPS)
                turn(i)
                dve.wait_ge(q_ready, i + 1)
                link(V.tensor_scalar(kmin[:, :], ps_kv[:, 0:C], 0.0, None, ALU.min))
                dve.sem_inc(qmin_ready, 1)
                dve.wait_ge(qexp_ready, i + 1)
                link(V.scalar_tensor_tensor(kk[:, :], ps_kv[:, 0:C], 0.0, kexp[:, :], ALU.max, ALU.add))
                dve.sem_inc(q_done, 1)
                dve.wait_ge(dm_ready, i + 1)
                link(V.tensor_scalar(rec_d[:, :], ps_dm[:, 0:C], ATT_EPS, None, ALU.add))
                link(V.reciprocal(rec_d[:, :], rec_d[:, :]))
                link(V.tensor_tensor(msgT[:, :], ps_dm[:, C:2 * C], rec_d[:, :], ALU.mult))
                dve.sem_inc(msg_ready, 1)
                dve.wait_ge(m_ready, i + 1)
                norm(ps_o[:, :], m1[:, :])
                link(V.tensor_tensor(m1[:, :], m1[:, :], lnb[:, 0, :], ALU.mult))
                link(V.tensor_tensor(m1[:, :], m1[:, :], lnb[:, 1, :], ALU.add))
                dve.sem_inc(m1_ready, 1)
                dve.wait_ge(o_ready, i + 1)
                norm(ps_o[:, :], m1[:, :])
                dve.sem_inc(o_used, 1)
                link(V.tensor_tensor(m1[:, :], m1[:, :], lnb[:, 2, :], ALU.mult))
                link(V.tensor_tensor(m1[:, :], m1[:, :], lnb[:, 3, :], ALU.add))
                link(V.tensor_tensor(x2[:, bass.ds(i, 1), :], x2[:, bass.ds(i, 1), :], m1[:, :].unsqueeze(1), ALU.add))
                link.settle()
                assert link.n == 18 + 2 * RSQRT_STEPS, link.n
            link.leave((18 + 2 * RSQRT_STEPS) * TOK)

        @block.tensor
        def _(pe):
            T = nc.tensor
            pe.sem_inc(pause["pe"], 1)
            pe.wait_ge(w_in, 16 * 9)
            for k in range(2):
                T.matmul(ps_h[:, 8 * k:8 * k + 8], wT[:, k * P:(k + 1) * P], aT[:, :], start=True, stop=True)
            T.matmul(ps_h[0:1, 16:24], bcol[:, :], aT[:, :], start=True, stop=True).then_inc(wa_ready, 1)
            pe.wait_ge(counted, 1)
            T.matmul(ps_cnt[:, 0, 0:TOK], before[:, :], cnt[:, :], start=True, stop=True)
            T.matmul(ps_cnt[:, 1, 0:TOK], ones[:, :], cnt[:, :], start=True, stop=True).then_inc(ranked, 1)
            pe.wait_ge(wa_done, 3)
            with pe.Fori(0, TOK) as i:
                pe.wait_ge(xn_ready, i + 1)
                for k in range(2):
                    last = T.transpose(psT[:, k, :], xn[:, k * P:(k + 1) * P], ident[:, :])
                last.then_inc(xT_ready, 1)
                pe.wait_ge(xTs_ready, i + 1)
                for k in range(2):
                    T.matmul(ps_kv[:, :], xTs[:, k, :], wqkv[:, k, C:3 * C], start=(k == 0), stop=(k == 1))
                for k in range(2):
                    T.matmul(ps_h[:, 0:TABW + 1], xTs[:, k, :], wcat[:, k, :], start=(k == 0), stop=False)
                T.matmul(ps_h[:, 0:TABW + 1], ones[0:1, :], brow[:, :], start=False, stop=True).then_inc(kv_ready, 1)
                pe.wait_ge(k_ready, i + 1)
                for g in range(2):
                    last = T.matmul(ps_KV[:, g, 0:P + 1], kk[:, g * P:(g + 1) * P], va[:, g, :], start=True, stop=True)
                last.then_inc(KV_ready, 1)
                pe.wait_ge(KV_used, i + 1)
                pe.sem_inc(pause["pe"], 1)
            pe.wait_ge(kvb_ready, 1)
            with pe.Fori(0, TOK) as i:
                tok = bass.ds(i * P, P)
                for m in range(2):
                    for k in range(2):
                        last = T.matmul(ps_kv[:, m * P:(m + 1) * P], wqkv[:, k, m * P:(m + 1) * P], xnT[:, k, tok],
                                        start=(k == 0), stop=(k == 1))
                last.then_inc(q_ready, 1)
                pe.wait_ge(q_done, i + 1)
                for g in range(2):
                    qg = kk[:, g * P:(g + 1) * P]
                    T.matmul(ps_dm[:, g * P:(g + 1) * P], ksb[:, g, :], qg, start=True, stop=True)
                    last = T.matmul(ps_dm[:, C + g * P:C + (g + 1) * P], kvb[:, g, :], qg, start=True, stop=True)
                last.then_inc(dm_ready, 1)
                pe.wait_ge(msg_ready, i + 1)
                for g in range(2):
                    last = T.matmul(ps_o[:, :], msgT[:, g * P:(g + 1) * P], wm[:, g, :], start=(g == 0), stop=(g == 1))
                last.then_inc(m_ready, 1)
                pe.wait_ge(m1_ready, i + 1)
                for k in range(2):
                    last = T.transpose(psT[:, k, :], m1[:, k * P:(k + 1) * P], ident[:, :])
                last.then_inc(m1T_ps, 1)
                pe.wait_ge(m1T_ready, i + 1)
                for m in range(4):
                    for k in range(4):
                        src = xnT[:, k, tok] if k < 2 else m1T[:, k - 2, :]
                        last = T.matmul(ps_h[:, m * P:(m + 1) * P], w1[:, k, m * P:(m + 1) * P], src,
                                        start=(k == 0), stop=(k == 3))
                last.then_inc(h_ready, 1)
                pe.wait_ge(hT_ready, i + 1)
                for k in range(4):
                    last = T.matmul(ps_o[:, :], hT[:, k, :], w2[:, k, :], start=(k == 0), stop=(k == 3))
                last.then_inc(o_ready, 1)
                pe.wait_ge(o_used, i + 1)
                pe.sem_inc(pause["pe"], 1)


def phase2(nc, v):
    table, slots, spill = v["table"], v["slots"], v["spill"]
    x2, s_res, ident, iota_f, ones, bid_i = (v[k] for k in ("x2", "s_res", "ident", "iota_f", "ones", "bid_i"))
    pause, sem = v["pause"], v["sem"]
    ctx = ExitStack()
    with ctx:
        def sb(name, shape, dt, c=ctx):
            return c.enter_context(nc.sbuf_tensor(name, shape, dt))

        def ps(name, shape, dt=fp32):
            return ctx.enter_context(nc.psum_tensor(name, shape, dt))

        rec2 = sb("rec2", [P, ET], i32)
        lo = sb("lo", [P, ET], fp32)
        colx = sb("colx", [P, ET], i32)
        mx = sb("mx", [P, TOK, HEADS], fp32)
        sm = sb("sm", [P, TOK, 3, 2 * HEADS], bf16)
        smf = sb("smf", [P, TOK, 2 * HEADS], fp32)
        smr = sb("smr", [P, TOK, 2 * HEADS], fp32)
        acc = sb("acc", [P, TOK, AGG], fp32)
        ix = [sb(f"ix{n}", [P, GT], i32) for n in range(2)]
        G = [sb(f"G{n}", [P, GT, TABW], fp32) for n in range(2)]
        miss = sb("miss", [P, P], fp32)
        best = sb("best", [P, HEADS, P], fp32)
        bm = sb("bm", [P, HEADS], fp32)
        oh = sb("oh", [P, GT, P], fp32)
        ohT = sb("ohT", [P, GT, P], bf16)
        se = sb("se", [P, GT, 2 * HEADS], fp32)
        z = sb("z", [P, GT, HEADS], fp32)
        w = sb("w", [P, GT, HEADS], fp32)
        wv = sb("wv", [P, GT, HEADS, DOUT + 1], fp32)

        psb = [ps(f"psb{n}", [P, HEADS, P]) for n in range(2)]
        pst = [ps(f"pst{n}", [P, BT, P]) for n in range(2)]
        pss = ps("pss", [P, GT, 3, 2 * HEADS])
        psa = [ps(f"psa{n}", [P, 512]) for n in range(GB)]

        slots_in, colx_ready = sem("slots_in"), sem("colx_ready")
        ix_ready = [sem(f"ix_ready{n}") for n in range(2)]
        gathered = [sem(f"gathered{n}") for n in range(2)]
        G_seen = [sem(f"G_seen{n}") for n in range(2)]
        spilled = [sem(f"spilled{n}") for n in range(2)]
        G_free = [sem(f"G_free{n}") for n in range(2)]
        best_ready, bestT_ready, sm_ready = sem("best_ready"), sem("bestT_ready"), sem("sm_ready")
        chain2 = sem("chain2")

        block = nc.Block()
        block.__enter__()

        @block.sync
        def _(sp):
            sp.dma_start(rec2[:, :], slots.rearrange("(p e) o -> p (e o)", p=P)).then_inc(slots_in, 16)
            with sp.Fori(0, GROUPS // 2) as i:
                for n in range(2):
                    sp.wait_ge(gathered[n], i * (16 * GT) + 16 * GT)
                    sp.dma_start(spill[bass.ds(i * 2 + n, 1), :, :].rearrange("a p c -> (a p) c"),
                                 G[n][:, :, :].rearrange("p t c -> p (t c)")).then_inc(spilled[n], 16)
                    sp.wait_ge(spilled[n], i * 16 + 16)
                    sp.sem_inc(G_free[n], 1)

        @block.gpsimd
        def _(pool):
            with pool.Fori(0, GROUPS // 2) as i:
                for n in range(2):
                    pool.wait_ge(ix_ready[n], i + 1)
                    pool.wait_ge(G_free[n], i + 1)
                    pool.wait_ge(G_seen[n], i + 1)
                    pool.sem_inc(pause["pool"], 1)
                    for k in range(GT):
                        pool.indirect_dma_start(G[n][:, k, :], None, table, bass.IndirectOffsetOnAxis(
                            ap=ix[n][:, k:k + 1].bitcast(u32), axis=0)).then_inc(gathered[n], 16)

        @block.scalar
        def _(act):
            act.wait_ge(colx_ready, 1)
            with act.Fori(0, GROUPS // 2) as i:
                for n in range(2):
                    act.wait_ge(G_seen[n], i + 1)
                    act.sem_inc(pause["act"], 1)
                    nc.scalar.copy(ix[n][:, :], colx[:, bass.ds(i * (2 * GT) + n * GT, GT)]).then_inc(ix_ready[n], 1)

        @block.vector
        def _(dve):
            V = nc.vector
            link = Link(dve, chain2, pause["dve"])
            for n in range(2):
                dve.sem_inc(G_free[n], 1)
                dve.sem_inc(G_seen[n], 1)
            dve.wait_ge(slots_in, 16)
            link(V.tensor_scalar(colx[:, :], rec2[:, :], NONE, None, ALU.bitwise_and))
            link(V.tensor_copy(lo[:, :], colx[:, :]))
            link(V.tensor_scalar(colx[:, :], rec2[:, :], 8, None, ALU.logical_shift_right))
            dve.sem_inc(colx_ready, 1)
            link(V.memset(mx[:, :, :], 2 * FAR))
            link(V.memset(acc[:, :, :], 0.0))
            per = 2 * GB * (BT * (1 + HEADS) + 2)
            link.enter()
            with dve.Fori(0, GROUPS // 2) as i:
                link.loop(i, per)
                for n in range(2):
                    dve.wait_ge(gathered[n], i * (16 * GT) + 16 * GT)
                    for q in range(GB):
                        bid = dve.value_load(bid_i[0:1, bass.ds(i * (2 * GB) + n * GB + q, 1)], min_val=0, max_val=TOK - 1)
                        for k in range(BT):
                            t = i * (2 * GT) + n * GT + q * BT + k
                            link(V.tensor_scalar(miss[:, :], iota_f[:, :], lo[:, bass.ds(t, 1)], FAR, ALU.not_equal, ALU.mult))
                            for h in range(HEADS):
                                d = G[n][:, q * BT + k, DCOL + h:DCOL + h + 1]
                                if k == 0:
                                    link(V.tensor_scalar(best[:, h, :], miss[:, :], d, None, ALU.add))
                                else:
                                    link(V.scalar_tensor_tensor(best[:, h, :], miss[:, :], d, best[:, h, :], ALU.add, ALU.max))
                        if q == GB - 1:
                            dve.sem_inc(G_seen[n], 1)
                        dve.sem_inc(best_ready, 1)
                        dve.wait_ge(bestT_ready, i * (2 * GB) + n * GB + q + 1)
                        link(V.tensor_reduce(bm[:, :], psb[0][:, :, :], AX.X, ALU.max))
                        link(V.tensor_tensor(mx[:, bass.ds(bid, 1), :], mx[:, bass.ds(bid, 1), :], bm[:, :].unsqueeze(1), ALU.max))
                        link.settle()
                assert link.n == per, link.n
            link.leave(per * GROUPS // 2)
            link(V.tensor_copy(smf[:, :, 0:HEADS], s_res[:, :, :]))
            link(V.tensor_tensor(mx[:, :, :], mx[:, :, :], s_res[:, :, :], ALU.add))
            link(V.scalar_tensor_tensor(smf[:, :, HEADS:], mx[:, :, :], SLOPE, mx[:, :, :], ALU.mult, ALU.max))
            link(V.tensor_copy(sm[:, :, 0, :], smf[:, :, :]))
            link(V.tensor_tensor(smr[:, :, :], smf[:, :, :], sm[:, :, 0, :], ALU.subtract))
            link(V.tensor_copy(sm[:, :, 1, :], smr[:, :, :]))
            link(V.tensor_tensor(smr[:, :, :], smr[:, :, :], sm[:, :, 1, :], ALU.subtract))
            link(V.tensor_copy(sm[:, :, 2, :], smr[:, :, :]))
            dve.sem_inc(sm_ready, 1)

        @block.tensor
        def _(pe):
            with pe.Fori(0, NB) as i:
                pe.wait_ge(best_ready, i + 1)
                for h in range(HEADS):
                    last = nc.tensor.transpose(psb[0][:, h, :], best[:, h, :], ident[:, :])
                last.then_inc(bestT_ready, 1)

        block.__exit__(None, None, None)

        loaded = [sem(f"loaded{n}") for n in range(2)]
        G_used = [sem(f"G_used{n}") for n in range(2)]
        oh_ready, oh_ps, ohT_ready, se_ready, z_ready, w_ready, wv_ready, sums_ready, sums_used = (sem(k) for k in (
            "oh_ready", "oh_ps", "ohT_ready", "se_ready", "z_ready", "w_ready", "wv_ready", "sums_ready", "sums_used"))
        chain3 = sem("chain3")
        with nc.Block() as block:
            @block.sync
            def _(sp):
                with sp.Fori(0, GROUPS // 2) as i:
                    for n in range(2):
                        sp.wait_ge(G_used[n], i + 1)
                        sp.dma_start(G[n][:, :, :].rearrange("p t c -> p (t c)"),
                                     spill[bass.ds(i * 2 + n, 1), :, :].rearrange("a p c -> (a p) c")).then_inc(loaded[n], 16)

            @block.scalar
            def _(act):
                with act.Fori(0, GROUPS) as i:
                    act.wait_ge(oh_ps, i + 1)
                    for q in range(GB):
                        last = nc.scalar.copy(ohT[:, q * BT:(q + 1) * BT, :], pst[q][:, :, :])
                    last.then_inc(ohT_ready, 1)
                    act.wait_ge(z_ready, i + 1)
                    nc.scalar.activation(w[:, :, :], z[:, :, :], ACT.Exp).then_inc(w_ready, 1)

            @block.vector
            def _(dve):
                V = nc.vector
                link = Link(dve, chain3, pause["dve"])
                for n in range(2):
                    dve.sem_inc(G_used[n], 1)
                dve.sem_inc(sums_used, 1)
                per = 2 * (6 + GB)
                link.enter()
                with dve.Fori(0, GROUPS // 2) as i:
                    link.loop(i, per)
                    for n in range(2):
                        g = i * 2 + n + 1
                        link(V.tensor_tensor(oh[:, :, :], iota_f[:, :].unsqueeze(1).to_broadcast([P, GT, P]),
                                             lo[:, bass.ds(i * (2 * GT) + n * GT, GT)].unsqueeze(2).to_broadcast([P, GT, P]),
                                             ALU.is_equal))
                        dve.sem_inc(oh_ready, 1)
                        dve.wait_ge(se_ready, g)
                        link(V.tensor_reduce(se[:, :, :], pss[:, :, :, :].rearrange("p t k c -> p t c k"), AX.X, ALU.add))
                        dve.wait_ge(loaded[n], i * 16 + 16)
                        d = G[n][:, :, DCOL:DCOL + HEADS]
                        link(V.tensor_tensor(z[:, :, :], se[:, :, 0:HEADS], d, ALU.add))
                        link(V.scalar_tensor_tensor(z[:, :, :], z[:, :, :], SLOPE, z[:, :, :], ALU.mult, ALU.max))
                        link(V.tensor_tensor(z[:, :, :], z[:, :, :], se[:, :, HEADS:], ALU.subtract))
                        dve.sem_inc(z_ready, 1)
                        dve.wait_ge(w_ready, g)
                        link(V.tensor_tensor(wv[:, :, :, :],
                                             G[n][:, :, 0:DOUT + 1].unsqueeze(2).to_broadcast([P, GT, HEADS, DOUT + 1]),
                                             w[:, :, :].unsqueeze(3).to_broadcast([P, GT, HEADS, DOUT + 1]), ALU.mult))
                        dve.sem_inc(G_used[n], 1)
                        dve.sem_inc(wv_ready, 1)
                        for q in range(GB):
                            dve.wait_ge(sums_ready, i * (2 * GB) + n * GB + q + 1)
                            bid = dve.value_load(bid_i[0:1, bass.ds(i * (2 * GB) + n * GB + q, 1)], min_val=0, max_val=TOK - 1)
                            a_ = acc[:, bass.ds(bid, 1), :]
                            link(V.tensor_tensor(a_, a_, psa[q][:, 0:AGG].unsqueeze(1), ALU.add))
                        link.settle()
                    assert link.n == per
                link.leave(per * GROUPS // 2)
                for h in range(HEADS):
                    den = acc[:, :, h * (DOUT + 1) + DOUT]
                    link(V.tensor_scalar(smr[:, :, h], den, 1e-30, None, ALU.max))
                    link(V.reciprocal(smf[:, :, h], smr[:, :, h]))
                    val = acc[:, :, h * (DOUT + 1):h * (DOUT + 1) + DOUT]
                    link(V.tensor_tensor(val, val, smf[:, :, h].unsqueeze(2).to_broadcast([P, TOK, DOUT]), ALU.mult))
                    xs = x2[:, :, h * DOUT:(h + 1) * DOUT]
                    link(V.tensor_tensor(xs, xs, val, ALU.add))
                link.settle()

            @block.tensor
            def _(pe):
                with pe.Fori(0, GROUPS) as i:
                    pe.wait_ge(oh_ready, i + 1)
                    for t in range(GT):
                        last = nc.tensor.transpose(pst[t // BT][:, t % BT, :], oh[:, t, :], ident[:, :])
                    last.then_inc(oh_ps, 1)
                    pe.wait_ge(ohT_ready, i + 1)
                    for q in range(GB):
                        bid = pe.value_load(bid_i[0:1, bass.ds(i * GB + q, 1)], min_val=0, max_val=TOK - 1)
                        for t in range(q * BT, (q + 1) * BT):
                            last = nc.tensor.matmul(pss[:, t, :, :], ohT[:, t, :],
                                                    sm[:, bass.ds(bid, 1), :, :].rearrange("p a k c -> p (a k c)"),
                                                    start=True, stop=True)
                    last.then_inc(se_ready, 1)
                    pe.wait_ge(wv_ready, i + 1)
                    for q in range(GB):
                        for t in range(q * BT, (q + 1) * BT):
                            last = nc.tensor.matmul(psa[q][:, 0:AGG], oh[:, t, :],
                                                    wv[:, t, :, :].rearrange("p h c -> p (h c)"),
                                                    start=(t % BT == 0), stop=(t % BT == BT - 1))
                        last.then_inc(sums_ready, 1)


def phase3(nc, v):
    x2, ident, iota_f, pcol, ones = (v[k] for k in ("x2", "ident", "iota_f", "pcol", "ones"))
    rwT, rb, E1, b1, E2, b2, out = (v[k] for k in ("rwT", "rb", "E1", "b1", "E2", "b2", "out"))
    pause, sem = v["pause"], v["sem"]
    HT = EXP * EH // P
    ctx = ExitStack()
    with ctx:
        def sb(name, shape, dt):
            return ctx.enter_context(nc.sbuf_tensor(name, shape, dt))

        def ps(name, shape):
            return ctx.enter_context(nc.psum_tensor(name, shape, fp32))

        e1 = sb("e1", [P, 2, EXP, EH], fp32)
        e2 = sb("e2", [P, HT, C], fp32)
        eb1 = sb("eb1", [P, HT], fp32)
        eb2 = sb("eb2", [EXP, C], fp32)
        rw = sb("rw", [P, 2, EXP], fp32)
        rbr = sb("rbr", [1, EXP], fp32)
        eid = sb("eid", [P, HT], fp32)
        st = sb("st3", [P, 6], fp32)
        mv = sb("mv3", [P, 2], fp32)
        rstd = sb("rstd3", [P, 1], fp32)
        rt = sb("rt3", [P, 1], fp32)
        yn = sb("yn", [P, C], fp32)
        ynT = sb("ynT", [P, 2, P], fp32)
        lg = sb("lg", [P, EXP], fp32)
        top = sb("top", [P, 8], fp32)
        topi = sb("topi", [P, 8], u32)
        idx = sb("idx", [P, 1], fp32)
        idxw = sb("idxw", [P, P], fp32)
        idxb = sb("idxb", [P, P], fp32)
        pick = sb("pick", [EXP, P], fp32)
        hs = sb("hs", [P, HT, P], fp32)
        ot = sb("ot", [P, 1, C], fp32)
        psT = ps("psT3", [P, 2, P])
        psl = ps("psl", [P, 512])
        psh = [ps(f"psh{n}", [P, 4, P]) for n in range(4)]
        psy = ps("psy", [P, 512])

        w3_in, eid_ready = sem("w3_in"), sem("eid_ready")
        yn_ready, yT_ready, ynT_ready, l_ready, idxw_ready, idx_ps, pick_ready, h_ready, relu_ready, masked, y_ready, \
            out_ready, out_sent, out_free = (sem(k + "3") for k in (
                "yn_ready", "yT_ready", "ynT_ready", "l_ready", "idxw_ready", "idx_ps", "pick_ready", "h_ready",
                "relu_ready", "masked", "y_ready", "out_ready", "out_sent", "out_free"))
        chain = sem("chain4")
        with nc.Block() as block:
            @block.sync
            def _(sp):
                for k in range(2):
                    sp.dma_start(e1[:, k, :, :], E1[:, k * P:(k + 1) * P, :].rearrange("e p h -> p e h")).then_inc(w3_in, 16)
                for dst, src in ((e2[:, :, :], E2.rearrange("(m p) c -> p m c", p=P)),
                                 (eb1[:, :], b1), (eb2[:, :], b2),
                                 (rw[:, :, :], rwT.rearrange("(k p) e -> p k e", p=P)), (rbr[:, :], rb)):
                    sp.dma_start(dst, src).then_inc(w3_in, 16)
                with sp.Fori(0, TOK) as i:
                    sp.wait_ge(out_ready, i + 1)
                    sp.dma_start(out[bass.ds(i * P, P), :], ot[:, 0, :]).then_inc(out_sent, 16)
                    sp.wait_ge(out_sent, i * 16 + 16)
                    sp.sem_inc(out_free, 1)
                sp.wait_ge(out_sent, 16 * TOK)

            @block.scalar
            def _(act):
                act.wait_ge(w3_in, 16 * 7)
                with act.Fori(0, TOK) as i:
                    act.wait_ge(yT_ready, i + 1)
                    nc.scalar.copy(ynT[:, :, :], psT[:, :, :]).then_inc(ynT_ready, 1)
                    for q in range(4):
                        act.wait_ge(h_ready, i * 4 + q + 1)
                        for m in range(4):
                            last = nc.scalar.activation(hs[:, 4 * q + m, :], psh[q][:, m, :], ACT.Relu,
                                                        bias=eb1[:, 4 * q + m:4 * q + m + 1])
                        last.then_inc(relu_ready, 1)

            @block.vector
            def _(dve):
                V = nc.vector
                link = Link(dve, chain, pause["dve"])
                dve.sem_inc(out_free, 1)
                link(V.tensor_scalar(eid[:, :], iota_f[:, 0:HT], 2.0, None, ALU.mult))
                link(V.tensor_scalar(idx[:, :], pcol[:, :], float(EH), None, ALU.is_ge))
                link(V.tensor_scalar(eid[:, :], eid[:, :], idx[:, :], None, ALU.add))
                link.enter()
                per = 3 + RSQRT_STEPS + 7 + HT + 1
                with dve.Fori(0, TOK) as i:
                    link.loop(i, per)
                    xi = x2[:, bass.ds(i, 1), :].rearrange("p a c -> p (a c)")
                    link(V.bn_stats(st[:, :], xi))
                    link.settle()
                    link(V.bn_aggr(mv[:, :], st[:, :]))
                    rsqrt(V, link, rstd[:, :], mv[:, 1:2], rt[:, :])
                    link(V.tensor_scalar(yn[:, :], xi, mv[:, 0:1], rstd[:, :], ALU.subtract, ALU.mult))
                    dve.sem_inc(yn_ready, 1)
                    dve.wait_ge(l_ready, i + 1)
                    link(V.tensor_copy(lg[:, :], psl[:, 0:EXP]))
                    link.settle()
                    link(V.max(top[:, :], lg[:, :]))
                    link.settle()
                    link(V.max_index(topi[:, :], top[:, :], lg[:, :]))
                    link(V.tensor_copy(idx[:, :], topi[:, 0:1]))
                    link(V.tensor_scalar(idxw[:, :], ones[:, :], idx[:, :], None, ALU.mult))
                    dve.sem_inc(idxw_ready, 1)
                    dve.wait_ge(idx_ps, i + 1)
                    link(V.tensor_copy(idxb[:, :], psl[:, P:2 * P]))
                    link(V.tensor_scalar(pick[:, :], idxb[0:EXP, :], pcol[0:EXP, :], None, ALU.is_equal))
                    dve.sem_inc(pick_ready, 1)
                    for q in range(4):
                        dve.wait_ge(relu_ready, i * 4 + q + 1)
                        for m in range(4 * q, 4 * q + 4):
                            link(V.scalar_tensor_tensor(hs[:, m, :], idxb[:, :], eid[:, m:m + 1], hs[:, m, :],
                                                        ALU.is_equal, ALU.mult))
                    dve.sem_inc(masked, 1)
                    dve.wait_ge(y_ready, i + 1)
                    dve.wait_ge(out_free, i + 1)
                    link(V.scalar_tensor_tensor(ot[:, :, :], psy[:, 0:C].unsqueeze(1), 0.0, x2[:, bass.ds(i, 1), :],
                                                ALU.max, ALU.add))
                    dve.sem_inc(out_ready, 1)
                    assert link.n == per, link.n
                link.leave(per * TOK)

            @block.tensor
            def _(pe):
                T = nc.tensor
                pe.wait_ge(w3_in, 16 * 7)
                with pe.Fori(0, TOK) as i:
                    pe.wait_ge(yn_ready, i + 1)
                    for k in range(2):
                        last = T.transpose(psT[:, k, :], yn[:, k * P:(k + 1) * P], ident[:, :])
                    last.then_inc(yT_ready, 1)
                    pe.wait_ge(ynT_ready, i + 1)
                    for k in range(2):
                        T.matmul(psl[:, 0:EXP], ynT[:, k, :], rw[:, k, :], start=(k == 0), stop=False)
                    T.matmul(psl[:, 0:EXP], ones[0:1, :], rbr[:, :], start=False, stop=True).then_inc(l_ready, 1)
                    for q in range(4):
                        for m in range(4):
                            e = 2 * (4 * q + m)
                            for k in range(2):
                                last = T.matmul(psh[q][:, m, :], e1[:, k, e:e + 2, :].rearrange("p e h -> p (e h)"),
                                                ynT[:, k, :], start=(k == 0), stop=(k == 1))
                        last.then_inc(h_ready, 1)
                    pe.wait_ge(idxw_ready, i + 1)
                    T.matmul(psl[:, P:2 * P], idxw[:, :], ident[:, :], start=True, stop=True).then_inc(idx_ps, 1)
                    pe.wait_ge(masked, i + 1)
                    T.matmul(psy[:, 0:C], pick[:, :], eb2[:, :], start=True, stop=False)
                    for m in range(HT):
                        last = T.matmul(psy[:, 0:C], hs[:, m, :], e2[:, m, :], start=False, stop=(m == HT - 1))
                    last.then_inc(y_ready, 1)


_INS = ["x", "row", "col", "W", "WT", "b", "a", "Wqkv", "Wm", "W1", "W2", "lnp", "rwT", "rb", "E1", "b1", "E2", "b2"]


def kernel(**inputs):
    import numpy as _np
    import concourse.bacc as _bacc
    from concourse import mybir as _mybir
    from concourse.bass_utils import run_bass_kernel_spmd as _run

    g = {k: _np.asarray(v) for k, v in inputs.items()}

    def edges(v, fill):
        return _np.concatenate([v, _np.full(P * EC - E, fill, v.dtype)]).reshape(P, EC)

    host = {
        "x": _np.concatenate([g["x"], _np.zeros((NP - N, C), g["x"].dtype)]),
        "row": edges(g["src"], NP - 1), "col": edges(g["dst"], 0),
        "W": g["L0_gnn_W"], "WT": g["L0_gnn_W"].T, "b": g["L0_gnn_b"].reshape(DOUT, 1),
        "a": _np.concatenate([g["L0_gnn_a_dst"], g["L0_gnn_a_src"]]).T,
        "Wqkv": _np.concatenate([g["L0_mix_Wq"], g["L0_mix_Wk"], g["L0_mix_Wv"]], axis=1),
        "Wm": g["L0_mix_Wm"], "W1": g["L0_mix_W1"], "W2": g["L0_mix_W2"],
        "lnp": _np.stack([g["L0_mix_g1"], g["L0_mix_b1"], g["L0_mix_g2"], g["L0_mix_b2"]]),
        "rwT": g["L0_ffn_router_w"].T, "rb": g["L0_ffn_router_b"].reshape(1, EXP),
        "E1": g["L0_ffn_W1"], "b1": g["L0_ffn_b1"].reshape(EXP * EH // P, P).T,
        "E2": g["L0_ffn_W2"].reshape(EXP * EH, C), "b2": g["L0_ffn_b2"],
    }
    nc = _bacc.Bacc("TRN2", target_bir_lowering=False, num_devices=1)
    arrays, args = {}, []
    for name in _INS:
        arr = _np.ascontiguousarray(host[name])
        arrays[f"in_{name}_dram"] = arr
        args.append(nc.dram_tensor(f"in_{name}_dram", arr.shape, _mybir.dt.from_np(arr.dtype), kind="ExternalInput").ap())
    args.append(nc.dram_tensor("out_0_dram", (NP, C), fp32, kind="ExternalOutput").ap())
    build(nc, *args)
    r = _run(nc, [arrays], core_ids=[0])
    return r.results[0]["out_0_dram"][:N]
```

```python
import concourse.bass as bass
from concourse import mybir
from contextlib import ExitStack

N, C, E = 6250, 256, 200000
P = 128
TOK = -(-N // P)
NP = TOK * P
HEADS, DOUT = 4, 64
SLOPE = 0.2
TABW = 72
DCOL = DOUT + 1
AGG = HEADS * (DOUT + 1)
STAGE = 28
EC = -(-E // (2 * P * STAGE)) * 2 * STAGE
TURNS = EC // STAGE
BT = 4
BE = BT * P
NB = (P * EC - TOK) // BE + TOK
RING = 4
TURN = 2 * RING
NB = -(-NB // TURN) * TURN
ET = NB * BT
XT = 3
NONE = 255
FAR_ROOT = 1e15
MH, MD = 8, 32
HID = 512
EXP, EH = 32, 64
ATT_EPS, LN_EPS = 1e-6, 1e-5

fp32 = mybir.dt.float32
bf16 = mybir.dt.bfloat16
i32 = mybir.dt.int32
u32 = mybir.dt.uint32
ALU = mybir.AluOpType
ACT = mybir.ActivationFunctionType
AX = mybir.AxisListType


class Link:

    def __init__(self, eng, sem, pause):
        self.eng, self.sem, self.pause, self.base, self.n = eng, sem, pause, 0, 0

    def loop(self, i, per):
        self.base, self.n = self.base0 + i * per, 0

    def enter(self):
        self.base0 = self.base + self.n

    def leave(self, total):
        self.base, self.n = self.base0 + total, 0

    def put(self, ins, sem=None, value=None):
        if sem is None:
            self.n += 1
            sem, value = self.sem, self.base + self.n
        ins.then_inc(sem, 1)
        self.last = sem, value

    def need(self, back=1):
        if back == 1:
            self.eng.wait_ge(*self.last)
        else:
            self.eng.wait_ge(self.sem, self.base + self.n + 1 - back)

    def settle(self):
        self.eng.sem_inc(self.pause, 1)

    def __call__(self, ins, sem=None, value=None):
        self.put(ins, sem, value)
        self.need()


def build(nc, x, row, col, W, WT, b, a, Wqkv, Wm, W1, W2, lnp, rwT, rb, E1, b1, E2, b2, out, dbg=None):
    table = nc.dram_tensor("table", (NP, TABW), fp32).ap()
    slots = nc.dram_tensor("slots", (P * ET, 1), i32).ap()
    ctx = ExitStack()
    with ctx:
        def sb(name, shape, dt, c=ctx):
            return c.enter_context(nc.sbuf_tensor(name, shape, dt))

        def ps(name, shape, c=ctx, dt=fp32):
            return c.enter_context(nc.psum_tensor(name, shape, dt))

        def sem(name):
            return ctx.enter_context(nc.semaphore(name))

        pause = {e: sem("pause_" + e) for e in ("dve", "act", "pool", "pe")}

        x2 = sb("x2", [P, TOK, C], fp32)
        s_res = sb("s_res", [P, TOK, HEADS], fp32)
        ident = sb("ident", [P, P], fp32)
        iota_f = sb("iota_f", [P, P], fp32)
        pcol = sb("pcol", [P, 1], fp32)
        ones = sb("ones", [P, P], fp32)
        bid_i = sb("bid_i", [1, NB + 2], i32)
        lnb = sb("lnb", [P, 4, C], fp32)

        phase1(nc, ctx, locals())
        phase2(nc, locals())
        phase3(nc, locals())


NEWTON = 3
RSQRT_STEPS = 2 + 3 * NEWTON
P1_STEPS = 6 + RSQRT_STEPS
P2_STEPS = 11 + 2 * RSQRT_STEPS


def rsqrt(V, link, y, var, t):
    link(V.tensor_scalar(var, var, LN_EPS, None, ALU.add))
    link(V.tensor_scalar(y.bitcast(i32), var.bitcast(i32), -0.5, float(0x5F3759DF), ALU.mult, ALU.add))
    for _ in range(NEWTON):
        link(V.scalar_tensor_tensor(t, y, y, var, ALU.mult, ALU.mult))
        link(V.tensor_scalar(t, t, -0.5, 1.5, ALU.mult, ALU.add))
        link(V.tensor_tensor(y, y, t, ALU.mult))


def phase1(nc, octx, v):
    x, row, col, W, WT, b, a = (v[k] for k in ("x", "row", "col", "W", "WT", "b", "a"))
    Wqkv, Wm, W1, W2, lnp = (v[k] for k in ("Wqkv", "Wm", "W1", "W2", "lnp"))
    table, slots = v["table"], v["slots"]
    x2, s_res, ident, iota_f, pcol, ones, bid_i, lnb = (v[k] for k in (
        "x2", "s_res", "ident", "iota_f", "pcol", "ones", "bid_i", "lnb"))
    pause, sem = v["pause"], v["sem"]
    ctx = ExitStack()
    with ctx:
        def sb(name, shape, dt):
            return ctx.enter_context(nc.sbuf_tensor(name, shape, dt))

        def ps(name, shape):
            return ctx.enter_context(nc.psum_tensor(name, shape, fp32))

        rec = sb("rec", [P, EC], i32)
        addr = sb("addr", [P, EC], i32)
        blk = sb("blk", [P, EC], fp32)
        pos = sb("pos", [P, EC], fp32)
        eq = sb("eq", [P, EC], fp32)
        cum = sb("cum", [P, EC], fp32)
        cnt = sb("cnt", [P, TOK], fp32)
        base = sb("base", [P, TOK], fp32)
        tot = sb("tot", [P, TOK], fp32)
        tot_i = sb("tot_i", [P, TOK], i32)
        ends = sb("ends", [P, TOK], fp32)
        before = sb("before", [P, P], fp32)
        rec_s = [sb(f"rec_s{n}", [P, STAGE], i32) for n in range(2)]
        addr_s = [sb(f"addr_s{n}", [P, STAGE], i32) for n in range(2)]
        biota = sb("biota", [1, NB], fp32)
        bidf = sb("bidf", [1, NB], fp32)
        wcat = sb("wcat", [P, 2, TABW + 1], fp32)
        brow = sb("brow", [1, TABW + 1], fp32)
        wT = sb("wT", [DOUT, C], fp32)
        aT = sb("aT", [DOUT, 2 * HEADS], fp32)
        bcol = sb("bcol", [DOUT, 1], fp32)
        wqkv = sb("wqkv", [P, 2, 3 * C], fp32)
        wm = sb("wm", [P, 2, C], fp32)
        w1 = sb("w1", [P, 4, HID], fp32)
        w2 = sb("w2", [P, 4, C], fp32)
        blockm = sb("blockm", [P, P], fp32)
        valid = sb("valid", [P, TOK], fp32)
        kvb = sb("kvb", [P, 2, P], fp32)
        ksb = sb("ksb", [P, 2, P], fp32)
        kvacc = sb("kvacc", [P, 2, P + 1], fp32)
        xnT = sb("xnT", [P, 2, NP], fp32)
        xt = sb("xt", [P, C], fp32)
        xn = sb("xn", [P, C], fp32)
        st = sb("st", [P, 6], fp32)
        mv = sb("mv", [P, 2], fp32)
        rstd = sb("rstd", [P, 1], fp32)
        rt = sb("rt", [P, 1], fp32)
        xTs = sb("xTs", [P, 2, P], fp32)
        tab = sb("tab", [P, TABW], fp32)
        kmin = sb("kmin", [P, C], fp32)
        kexp = sb("kexp", [P, C], fp32)
        kk = sb("kk", [P, C], fp32)
        va = sb("va", [P, 2, P + 1], fp32)
        rec_d = sb("rec_d", [P, C], fp32)
        msgT = sb("msgT", [P, C], fp32)
        m1 = sb("m1", [P, C], fp32)
        m1T = sb("m1T", [P, 2, P], fp32)
        hT = sb("hT", [P, 4, P], fp32)

        ps_cnt = ps("ps_cnt", [P, 2, P])
        psT = ps("psT", [P, 2, P])
        ps_kv = ps("ps_kv", [P, 512])
        ps_h = ps("ps_h", [P, 512])
        ps_KV = ps("ps_KV", [P, 2, 256])
        ps_dm = ps("ps_dm", [P, 512])
        ps_o = ps("ps_o", [P, C])

        rows_in, w_in, ln_in, filled, consts = (sem(k) for k in ("rows_in", "w_in", "ln_in", "filled", "consts"))
        edges_ready, fill_ready, counted, ranked, based = (sem(k) for k in (
            "edges_ready", "fill_ready", "counted", "ranked", "based"))
        wa_ready, wa_done, bid_ready = sem("wa_ready"), sem("wa_done"), sem("bid_ready")
        placed, staged, scattered = sem("placed"), sem("staged"), [sem(f"scattered{n}") for n in range(2)]
        x_in, x_used, xn_ready, xT_ready, xTs_ready, kv_ready, kmin_ready, kexp_ready, k_ready, KV_ready = (
            sem(k) for k in ("x_in", "x_used", "xn_ready", "xT_ready", "xTs_ready", "kv_ready", "kmin_ready",
                             "kexp_ready", "k_ready", "KV_ready"))
        tab_ready, tab_out, tab_free = sem("tab_ready"), sem("tab_out"), sem("tab_free")
        xT_stored, va_ready = sem("xT_stored"), sem("va_ready")
        kvb_ready, q_ready, qmin_ready, qexp_ready, q_done, dm_ready, msg_ready, m_ready, m1_ready, m1T_ps, m1T_ready, \
            h_ready, hT_ready, o_ready, mixed = (sem(k) for k in (
                "kvb_ready", "q_ready", "qmin_ready", "qexp_ready", "q_done", "dm_ready", "msg_ready", "m_ready",
                "m1_ready", "m1T_ps", "m1T_ready", "h_ready", "hT_ready", "o_ready", "mixed"))
        KV_used, o_used = sem("KV_used"), sem("o_used")
        dve_chain = sem("dve_chain")
        pool_const = sem("pool_const")

        block = ctx.enter_context(nc.Block())

        @block.sync
        def _(sp):
            sp.dma_start(rec[:, :], row).then_inc(rows_in, 16)
            sp.dma_start(addr[:, :], col).then_inc(rows_in, 16)
            for dst, src in ((wcat[:, :, 0:DOUT], W.rearrange("(k p) n -> p k n", p=P)), (wT[:, :], WT), (aT[:, :], a),
                             (bcol[:, :], b), (brow[:, 0:DOUT], b.rearrange("n o -> o n")),
                             (wqkv[:, :, :], Wqkv.rearrange("(k p) n -> p k n", p=P)),
                             (wm[:, :, :], Wm.rearrange("(k p) n -> p k n", p=P)),
                             (w1[:, :, :], W1.rearrange("(k p) n -> p k n", p=P)),
                             (w2[:, :, :], W2.rearrange("(k p) n -> p k n", p=P))):
                sp.dma_start(dst, src).then_inc(w_in, 16)
            sp.wait_ge(fill_ready, 1)
            sp.dma_start(slots.rearrange("(p e) o -> p (e o)", p=P), xnT[:, 0, 0:ET].bitcast(i32)).then_inc(filled, 16)
            with sp.Fori(0, TOK) as i:
                sp.wait_ge(x_used, i + 1)
                sp.dma_start(xt[:, :], x[bass.ds(i * P, P), :]).then_inc(x_in, 16)
                sp.wait_ge(tab_ready, i + 1)
                sp.dma_start(table[bass.ds(i * P, P), :], tab[:, :]).then_inc(tab_out, 16)
                sp.wait_ge(tab_out, i * 16 + 16)
                sp.sem_inc(tab_free, 1)

        @block.gpsimd
        def _(pool):
            pool.memset(ones[:, :], 1.0).then_inc(consts, 1)
            pool.memset(ident[:, :], 1.0).then_inc(pool_const, 1)
            pool.memset(before[:, :], 1.0).then_inc(pool_const, 1)
            pool.memset(blockm[:, :], 1.0).then_inc(pool_const, 1)
            pool.wait_ge(pool_const, 3)
            pool.affine_select(out=ident[:, :], in_=ident[:, :], compare_op=ALU.is_equal, fill=0.0, base=0,
                               pattern=[[-1, P]], channel_multiplier=1).then_inc(consts, 1)
            pool.affine_select(out=before[:, :], in_=before[:, :], compare_op=ALU.is_gt, fill=0.0, base=0,
                               pattern=[[1, P]], channel_multiplier=-1).then_inc(consts, 1)
            bm = blockm[:, :].rearrange("p (a c) -> p a c", c=MD)
            pool.affine_select(out=bm, in_=bm, compare_op=ALU.is_ge, fill=0.0, base=0,
                               pattern=[[-MD, P // MD], [0, MD]], channel_multiplier=1).then_inc(pool_const, 1)
            pool.wait_ge(pool_const, 4)
            pool.affine_select(out=bm, in_=bm, compare_op=ALU.is_ge, fill=0.0, base=MD - 1,
                               pattern=[[MD, P // MD], [0, MD]], channel_multiplier=-1).then_inc(consts, 1)
            for t, pattern, up in ((iota_f, [[1, P]], 0), (pcol, [[0, 1]], 1), (valid, [[P, TOK]], 1),
                                   (biota, [[1, NB]], 0)):
                pool.iota(t[:, :], pattern, base=0, channel_multiplier=up,
                          allow_small_or_imprecise_dtypes=True).then_inc(consts, 1)
            for c in range(4):
                pool.dma_start(lnb[:, c, :], lnp[c:c + 1, :].to_broadcast([P, C])).then_inc(ln_in, 16)
            pool.wait_ge(ln_in, 64)
            pool.wait_ge(filled, 16)
            pool.wait_ge(placed, 1)
            pool.sem_inc(pause["pool"], 1)

            def turn(i, n, wait):
                if wait:
                    pool.wait_ge(scattered[n], i * (16 * STAGE))
                    pool.sem_inc(pause["pool"], 1)
                cols = bass.ds(i * (2 * STAGE) + n * STAGE, STAGE)
                pool.tensor_copy(rec_s[n][:, :], rec[:, cols]).then_inc(staged, 1)
                pool.tensor_copy(addr_s[n][:, :], addr[:, cols]).then_inc(staged, 1)
                pool.wait_ge(staged, i * 4 + 2 * n + 2)
                pool.sem_inc(pause["pool"], 1)
                for k in range(STAGE):
                    pool.indirect_dma_start(slots, bass.IndirectOffsetOnAxis(ap=addr_s[n][:, k:k + 1].bitcast(u32), axis=0),
                                            rec_s[n][:, k:k + 1], None).then_inc(scattered[n], 16)

            for n in range(2):
                turn(0, n, False)
            with pool.Fori(1, TURNS // 2) as i:
                for n in range(2):
                    turn(i, n, True)
            for n in range(2):
                pool.wait_ge(scattered[n], 16 * STAGE * TURNS // 2)

        @block.scalar
        def _(act):
            act.wait_ge(wa_ready, 1)
            wa = ps_h[:, 0:16].rearrange("p (k n) -> p k n", k=2)
            nc.scalar.mul(wcat[:, :, DCOL:DCOL + HEADS], wa[:, :, 0:HEADS], -1.0)
            nc.scalar.copy(wcat[:, :, DCOL + HEADS:], wa[:, :, HEADS:]).then_inc(wa_done, 1)
            nc.scalar.mul(brow[:, DCOL:DCOL + HEADS], ps_h[0:1, 16:16 + HEADS], -1.0)
            nc.scalar.copy(brow[:, DCOL + HEADS:], ps_h[0:1, 16 + HEADS:16 + 2 * HEADS]).then_inc(wa_done, 1)
            with act.Fori(0, TOK) as i:
                act.wait_ge(xT_ready, i + 1)
                nc.scalar.copy(xTs[:, :, :], psT[:, :, :]).then_inc(xTs_ready, 1)
                act.wait_ge(kmin_ready, i + 1)
                nc.scalar.activation(kexp[:, :], kmin[:, :], ACT.Exp).then_inc(kexp_ready, 1)
                act.wait_ge(tab_free, i + 1)
                nc.scalar.copy(tab[:, :], ps_h[:, 0:TABW]).then_inc(tab_ready, 1)
            with act.Fori(0, TOK) as i:
                act.wait_ge(qmin_ready, i + 1)
                nc.scalar.activation(kexp[:, :], kmin[:, :], ACT.Exp).then_inc(qexp_ready, 1)
                act.wait_ge(m1T_ps, i + 1)
                nc.scalar.copy(m1T[:, :, :], psT[:, :, :]).then_inc(m1T_ready, 1)
                act.wait_ge(h_ready, i + 1)
                nc.scalar.activation(hT[:, :, :], ps_h[:, :].rearrange("p (m t) -> p m t", m=4), ACT.Relu).then_inc(hT_ready, 1)

        @block.vector
        def _(dve):
            link = Link(dve, dve_chain, pause["dve"])
            V = nc.vector
            dve.sem_inc(x_used, 1)
            dve.sem_inc(tab_free, 1)
            V.memset(xnT[:, 0, 0:ET].bitcast(i32), NONE).then_inc(fill_ready, 1)
            V.memset(wcat[:, :, DOUT:DCOL], 0.0)
            V.memset(brow[:, DOUT:DCOL], 1.0).then_inc(wa_done, 1)
            dve.wait_ge(rows_in, 32)
            link(V.tensor_scalar(cum[:, :].bitcast(i32), rec[:, :], 7, None, ALU.arith_shift_right))
            link(V.tensor_copy(blk[:, :], cum[:, :].bitcast(i32)))
            link(V.tensor_scalar(eq[:, :].bitcast(i32), rec[:, :], P - 1, None, ALU.bitwise_and))
            link(V.tensor_scalar(cum[:, :].bitcast(i32), addr[:, :], 8, None, ALU.logical_shift_left))
            link(V.tensor_tensor(rec[:, :], cum[:, :].bitcast(i32), eq[:, :].bitcast(i32), ALU.bitwise_or))
            link(V.memset(pos[:, :], 0.0))
            link(V.memset(bidf[:, :], 0.0))
            dve.wait_ge(consts, 8)
            link(V.tensor_scalar(valid[:, :], valid[:, :], float(N), None, ALU.is_lt))
            link.enter()
            with dve.Fori(0, TOK) as b_:
                link.loop(b_, 1)
                link(V.tensor_scalar(eq[:, :], blk[:, :], iota_f[:, bass.ds(b_, 1)], 0.0, ALU.is_equal, ALU.add,
                                     accum_out=cnt[:, bass.ds(b_, 1)]))
                link.settle()
            link.leave(TOK)
            dve.sem_inc(counted, 1)
            dve.wait_ge(ranked, 1)
            link(V.tensor_scalar(tot_i[:, :], ps_cnt[:, 1, 0:TOK], float(BE - 1), None, ALU.add))
            link(V.tensor_scalar(tot_i[:, :], tot_i[:, :], BE.bit_length() - 1, None, ALU.arith_shift_right))
            link(V.tensor_copy(tot[:, :], tot_i[:, :]))
            link(V.tensor_tensor_scan(ends[:, :], ones[:, 0:TOK], tot[:, :], 0.0, ALU.mult, ALU.add))
            link(V.tensor_tensor(base[:, :], ends[:, :], tot[:, :], ALU.subtract))
            link(V.scalar_tensor_tensor(base[:, :], base[:, :], float(BE), ps_cnt[:, 0, 0:TOK], ALU.mult, ALU.add))
            link(V.tensor_scalar(base[:, :], base[:, :], -1.0, None, ALU.add))
            link.enter()
            with dve.Fori(0, TOK) as b_:
                link.loop(b_, 5)
                link(V.tensor_scalar(eq[:, :], blk[:, :], iota_f[:, bass.ds(b_, 1)], None, ALU.is_equal))
                link(V.tensor_tensor_scan(cum[:, :], ones[:, 0:1].to_broadcast([P, EC]), eq[:, :], 0.0, ALU.mult, ALU.add))
                link(V.scalar_tensor_tensor(cum[:, :], cum[:, :], base[:, bass.ds(b_, 1)], eq[:, :], ALU.add, ALU.mult))
                link(V.tensor_tensor(pos[:, :], pos[:, :], cum[:, :], ALU.add))
                link(V.scalar_tensor_tensor(bidf[:, :], biota[:, :], ends[0:1, bass.ds(b_, 1)], bidf[:, :], ALU.is_ge, ALU.add))
                link.settle()
            link.leave(5 * TOK)
            link(V.tensor_scalar(bidf[:, :], bidf[:, :], float(TOK - 1), None, ALU.min))
            link(V.memset(bid_i[:, 0:2], 0))
            link(V.tensor_copy(bid_i[:, 2:], bidf[:, :]))
            link(V.tensor_copy(addr[:, :], pos[:, :]))
            link(V.tensor_scalar(eq[:, :].bitcast(i32), addr[:, :], P - 1, None, ALU.bitwise_and))
            link(V.tensor_scalar(cum[:, :].bitcast(i32), addr[:, :], 7, None, ALU.arith_shift_right))
            link(V.scalar_tensor_tensor(addr[:, :], eq[:, :].bitcast(i32), float(ET), cum[:, :].bitcast(i32), ALU.mult, ALU.add), placed, 1)
            dve.wait_ge(filled, 16)

            def norm(src, dst, sem=None, value=None):
                link(V.bn_stats(st[:, :], src))
                link.settle()
                link(V.bn_aggr(mv[:, :], st[:, :]))
                rsqrt(V, link, rstd[:, :], mv[:, 1:2], rt[:, :])
                link(V.tensor_scalar(dst, src, mv[:, 0:1], rstd[:, :], ALU.subtract, ALU.mult), sem, value)

            link(V.memset(kvacc[:, :, :], 0.0))
            link.enter()
            with dve.Fori(0, TOK) as i:
                link.loop(i, P1_STEPS)
                dve.wait_ge(x_in, i * 16 + 16)
                norm(xt[:, :], xn[:, :], xn_ready, i + 1)
                link(V.tensor_tensor(x2[:, bass.ds(i, 1), :], xt[:, :].unsqueeze(1), xn[:, :].unsqueeze(1), ALU.add), x_used, i + 2)
                dve.wait_ge(xTs_ready, i + 1)
                link(V.tensor_copy(xnT[:, :, bass.ds(i * P, P)], xTs[:, :, :]))
                dve.wait_ge(kv_ready, i + 1)
                link(V.tensor_scalar(kmin[:, :], ps_kv[:, 0:C], 0.0, None, ALU.min), kmin_ready, i + 1)
                link(V.tensor_copy(va[:, :, 0:P], ps_kv[:, C:2 * C].rearrange("p (g n) -> p g n", g=2)))
                link(V.tensor_copy(va[:, :, P:P + 1], valid[:, bass.ds(i, 1)].unsqueeze(1).to_broadcast([P, 2, 1])))
                dve.wait_ge(kexp_ready, i + 1)
                link(V.scalar_tensor_tensor(kk[:, :], ps_kv[:, 0:C], 0.0, kexp[:, :], ALU.max, ALU.add), k_ready, i + 1)
                dve.wait_ge(KV_ready, i + 1)
                link(V.tensor_tensor(kvacc[:, :, :], kvacc[:, :, :], ps_KV[:, :, 0:P + 1], ALU.add))
                dve.wait_ge(tab_ready, i + 1)
                link(V.tensor_copy(s_res[:, bass.ds(i, 1), :], ps_h[:, DCOL + HEADS:TABW + 1].unsqueeze(1)), KV_used, i + 1)
                assert link.n == P1_STEPS, link.n
            link.leave(P1_STEPS * TOK)
            for g in range(2):
                link(V.tensor_tensor(kvb[:, g, :], kvacc[:, g, 0:P], blockm[:, :], ALU.mult))
                link(V.tensor_scalar(ksb[:, g, :], blockm[:, :], kvacc[:, g, P:P + 1], None, ALU.mult))
            dve.sem_inc(kvb_ready, 1)
            dve.wait_ge(ln_in, 64)
            link.enter()
            with dve.Fori(0, TOK) as i:
                link.loop(i, P2_STEPS)
                dve.wait_ge(q_ready, i + 1)
                link(V.tensor_scalar(kmin[:, :], ps_kv[:, 0:C], 0.0, None, ALU.min), qmin_ready, i + 1)
                dve.wait_ge(qexp_ready, i + 1)
                link(V.scalar_tensor_tensor(kk[:, :], ps_kv[:, 0:C], 0.0, kexp[:, :], ALU.max, ALU.add), q_done, i + 1)
                dve.wait_ge(dm_ready, i + 1)
                link(V.tensor_scalar(rec_d[:, :], ps_dm[:, 0:C], ATT_EPS, None, ALU.add))
                link(V.reciprocal(rec_d[:, :], rec_d[:, :]))
                link(V.tensor_tensor(msgT[:, :], ps_dm[:, C:2 * C], rec_d[:, :], ALU.mult), msg_ready, i + 1)
                dve.wait_ge(m_ready, i + 1)
                norm(ps_o[:, :], m1[:, :])
                link(V.tensor_tensor(m1[:, :], m1[:, :], lnb[:, 0, :], ALU.mult))
                link(V.tensor_tensor(m1[:, :], m1[:, :], lnb[:, 1, :], ALU.add), m1_ready, i + 1)
                dve.wait_ge(o_ready, i + 1)
                norm(ps_o[:, :], m1[:, :], o_used, i + 1)
                link(V.tensor_tensor(m1[:, :], m1[:, :], lnb[:, 2, :], ALU.mult))
                link(V.tensor_tensor(m1[:, :], m1[:, :], lnb[:, 3, :], ALU.add))
                link(V.tensor_tensor(x2[:, bass.ds(i, 1), :], x2[:, bass.ds(i, 1), :], m1[:, :].unsqueeze(1), ALU.add))
                link.settle()
                assert link.n == P2_STEPS, link.n
            link.leave(P2_STEPS * TOK)

        @block.tensor
        def _(pe):
            T = nc.tensor
            pe.sem_inc(pause["pe"], 1)
            pe.wait_ge(w_in, 16 * 9)
            for k in range(2):
                T.matmul(ps_h[:, 8 * k:8 * k + 8], wT[:, k * P:(k + 1) * P], aT[:, :], start=True, stop=True)
            T.matmul(ps_h[0:1, 16:24], bcol[:, :], aT[:, :], start=True, stop=True).then_inc(wa_ready, 1)
            pe.wait_ge(counted, 1)
            T.matmul(ps_cnt[:, 0, 0:TOK], before[:, :], cnt[:, :], start=True, stop=True)
            T.matmul(ps_cnt[:, 1, 0:TOK], ones[:, :], cnt[:, :], start=True, stop=True).then_inc(ranked, 1)
            pe.wait_ge(wa_done, 3)
            with pe.Fori(0, TOK) as i:
                pe.wait_ge(xn_ready, i + 1)
                for k in range(2):
                    last = T.transpose(psT[:, k, :], xn[:, k * P:(k + 1) * P], ident[:, :])
                last.then_inc(xT_ready, 1)
                pe.wait_ge(xTs_ready, i + 1)
                for k in range(2):
                    T.matmul(ps_kv[:, :], xTs[:, k, :], wqkv[:, k, C:3 * C], start=(k == 0), stop=(k == 1))
                for k in range(2):
                    T.matmul(ps_h[:, 0:TABW + 1], xTs[:, k, :], wcat[:, k, :], start=(k == 0), stop=False)
                T.matmul(ps_h[:, 0:TABW + 1], ones[0:1, :], brow[:, :], start=False, stop=True).then_inc(kv_ready, 1)
                pe.wait_ge(k_ready, i + 1)
                for g in range(2):
                    last = T.matmul(ps_KV[:, g, 0:P + 1], kk[:, g * P:(g + 1) * P], va[:, g, :], start=True, stop=True)
                last.then_inc(KV_ready, 1)
                pe.wait_ge(KV_used, i + 1)
                pe.sem_inc(pause["pe"], 1)
            pe.wait_ge(kvb_ready, 1)
            with pe.Fori(0, TOK) as i:
                tok = bass.ds(i * P, P)
                for m in range(2):
                    for k in range(2):
                        last = T.matmul(ps_kv[:, m * P:(m + 1) * P], wqkv[:, k, m * P:(m + 1) * P], xnT[:, k, tok],
                                        start=(k == 0), stop=(k == 1))
                last.then_inc(q_ready, 1)
                pe.wait_ge(q_done, i + 1)
                for g in range(2):
                    qg = kk[:, g * P:(g + 1) * P]
                    T.matmul(ps_dm[:, g * P:(g + 1) * P], ksb[:, g, :], qg, start=True, stop=True)
                    last = T.matmul(ps_dm[:, C + g * P:C + (g + 1) * P], kvb[:, g, :], qg, start=True, stop=True)
                last.then_inc(dm_ready, 1)
                pe.wait_ge(msg_ready, i + 1)
                for g in range(2):
                    last = T.matmul(ps_o[:, :], msgT[:, g * P:(g + 1) * P], wm[:, g, :], start=(g == 0), stop=(g == 1))
                last.then_inc(m_ready, 1)
                pe.wait_ge(m1_ready, i + 1)
                for k in range(2):
                    last = T.transpose(psT[:, k, :], m1[:, k * P:(k + 1) * P], ident[:, :])
                last.then_inc(m1T_ps, 1)
                pe.wait_ge(m1T_ready, i + 1)
                for m in range(4):
                    for k in range(4):
                        src = xnT[:, k, tok] if k < 2 else m1T[:, k - 2, :]
                        last = T.matmul(ps_h[:, m * P:(m + 1) * P], w1[:, k, m * P:(m + 1) * P], src,
                                        start=(k == 0), stop=(k == 3))
                last.then_inc(h_ready, 1)
                pe.wait_ge(hT_ready, i + 1)
                for k in range(4):
                    last = T.matmul(ps_o[:, :], hT[:, k, :], w2[:, k, :], start=(k == 0), stop=(k == 3))
                last.then_inc(o_ready, 1)
                pe.wait_ge(o_used, i + 1)
                pe.sem_inc(pause["pe"], 1)


def phase2(nc, v):
    table, slots = v["table"], v["slots"]
    x2, s_res, ident, iota_f, bid_i = (v[k] for k in ("x2", "s_res", "ident", "iota_f", "bid_i"))
    pause, sem = v["pause"], v["sem"]
    ctx = ExitStack()
    with ctx:
        def sb(name, shape, dt):
            return ctx.enter_context(nc.sbuf_tensor(name, shape, dt))

        def ps(name, shape):
            return ctx.enter_context(nc.psum_tensor(name, shape, fp32))

        rec2 = sb("rec2", [P, ET], i32)
        lo = sb("lo", [P, ET], fp32)
        colx = sb("colx", [P, ET], i32)
        mx = sb("mx", [P, TOK, HEADS], fp32)
        acc = sb("acc", [P, TOK, AGG], fp32)
        ix = [sb(f"ix{n}", [P, BT], i32) for n in range(RING)]
        G = [sb(f"G{n}", [P, BT, TABW], fp32) for n in range(RING)]
        miss = [sb(f"miss{n}", [P, BT, P], fp32) for n in range(RING)]
        oh = [sb(f"oh{n}", [P, BT, P], fp32) for n in range(RING)]
        cc = [sb(f"cc{n}", [P, HEADS], fp32) for n in range(RING)]
        ohT = [sb(f"ohT{n}", [P, BT, P], fp32) for n in range(2)]
        wv = [sb(f"wv{n}", [P, BT, HEADS, DOUT + 1], fp32) for n in range(2)]
        far = [sb(f"far{n}", [P, XT, HEADS, P], fp32) for n in range(2)]
        best = sb("best", [P, HEADS, P], fp32)
        one = sb("one", [P, 1], fp32)
        bm = sb("bm", [P, HEADS], fp32)
        sd = sb("sd", [P, 2 * HEADS], fp32)
        smb = sb("smb", [P, 3 * HEADS], fp32)
        cdiff = sb("cdiff", [P, HEADS], fp32)
        z = sb("z", [P, BT, HEADS], fp32)
        w = sb("w", [P, BT, HEADS], fp32)
        rden = sb("rden", [P, TOK, HEADS], fp32)

        psb = ps("psb", [P, HEADS, P])
        pst = [ps(f"pst{n}", [P, BT, P]) for n in range(2)]
        pss = ps("pss", [P, 512])
        psa = [ps(f"psa{n}", [P, 512]) for n in range(2)]

        slots_in, lo_ready = sem("slots_in"), sem("lo_ready")
        gathered = [sem(f"gathered{n}") for n in range(RING)]
        ix_ready, miss_ready, oh_ready, oh_ps, ohT_ready = (sem(k) for k in (
            "ix_ready", "miss_ready", "oh_ready", "oh_ps", "ohT_ready"))
        best_ready, bestT_ready, smb_ready, cdiff_ready, c_ready, se_ready, z_ready, w_ready, sums_ready = (
            sem(k) for k in ("best_ready", "bestT_ready", "smb_ready", "cdiff_ready", "c_ready", "se_ready", "z_ready",
                             "w_ready", "sums_ready"))
        off_ready = sem("off_ready")
        far_ready = sem("far_ready")
        rows_used, summed = sem("rows_used"), sem("summed")
        chain2 = sem("chain2")

        block = ctx.enter_context(nc.Block())

        @block.sync
        def _(sp):
            sp.dma_start(rec2[:, :], slots.rearrange("(p e) o -> p (e o)", p=P)).then_inc(slots_in, 16)

        @block.gpsimd
        def _(pool):
            pool.wait_ge(lo_ready, 2)
            with pool.Fori(0, NB // RING) as i:
                for k in range(RING):
                    j = i * RING + k
                    pool.wait_ge(rows_used, j + 1)
                    pool.sem_inc(pause["pool"], 1)
                    pool.tensor_tensor(miss[k][:, :, :], iota_f[:, :].unsqueeze(1).to_broadcast([P, BT, P]),
                                       lo[:, bass.ds(j * BT, BT)].unsqueeze(2).to_broadcast([P, BT, P]),
                                       ALU.subtract).then_inc(off_ready, 1)
                    pool.wait_ge(ix_ready, j + 1)
                    pool.sem_inc(pause["pool"], 1)
                    for t in range(BT):
                        pool.indirect_dma_start(G[k][:, t, :], None, table, bass.IndirectOffsetOnAxis(
                            ap=ix[k][:, t:t + 1].bitcast(u32), axis=0)).then_inc(gathered[k], 16)

        @block.scalar
        def _(act):
            def targets(j, k):
                act.wait_ge(rows_used, j + 1)
                act.sem_inc(pause["act"], 1)
                nc.scalar.copy(ix[k][:, :], colx[:, bass.ds(j * BT, BT)]).then_inc(ix_ready, 1)

            def match(j, k, nth):
                act.wait_ge(off_ready, j + 1)
                nc.scalar.activation(miss[k][:, :, :], miss[k][:, :, :], ACT.Square, scale=FAR_ROOT).then_inc(miss_ready, 1)
                act.wait_ge(miss_ready, j + 1)
                act.wait_ge(summed, j + 1)
                nc.scalar.activation(oh[k][:, :, :], miss[k][:, :, :], ACT.Relu, scale=-1.0, bias=one[:, :]).then_inc(oh_ready, 1)
                act.wait_ge(gathered[k], nth * (16 * BT))
                act.wait_ge(best_ready, j + 1)
                for t in range(XT):
                    for h in range(HEADS):
                        last = nc.scalar.activation(far[k % 2][:, t, h, :], miss[k][:, BT - XT + t, :], ACT.Identity,
                                                    bias=G[k][:, BT - XT + t, DCOL + h:DCOL + h + 1])
                last.then_inc(far_ready, 1)

            def finish(j, k):
                act.wait_ge(oh_ps, j + 1)
                nc.scalar.copy(ohT[k % 2][:, :, :], pst[k % 2][:, :, :]).then_inc(ohT_ready, 1)
                act.wait_ge(cdiff_ready, j + 1)
                nc.scalar.activation(cc[k][:, :], cdiff[:, :], ACT.Exp).then_inc(c_ready, 1)
                act.wait_ge(z_ready, j + 1)
                nc.scalar.activation(w[:, :, :], z[:, :, :], ACT.Exp).then_inc(w_ready, 1)

            act.wait_ge(lo_ready, 2)
            targets(0, 0)
            targets(1, 1)
            match(0, 0, 1)
            with act.Fori(0, NB // TURN - 1) as i:
                for k in range(TURN):
                    j = i * TURN + k
                    targets(j + 2, (k + 2) % RING)
                    match(j + 1, (k + 1) % RING, i * (TURN // RING) + ((k + 1) // RING + 1))
                    finish(j, k % RING)
            for k in range(TURN):
                j = NB - TURN + k
                if k + 2 < TURN:
                    targets(j + 2, (k + 2) % RING)
                if k + 1 < TURN:
                    match(j + 1, (k + 1) % RING, (j + 1) // RING + 1)
                finish(j, k % RING)

        @block.vector
        def _(dve):
            V = nc.vector
            link = Link(dve, chain2, pause["dve"])
            dve.sem_inc(rows_used, RING)
            dve.sem_inc(summed, RING)
            dve.sem_inc(best_ready, 2)
            dve.wait_ge(slots_in, 16)
            link(V.memset(one[:, :], 1.0))
            link(V.tensor_scalar(colx[:, :], rec2[:, :], NONE, None, ALU.bitwise_and))
            link(V.tensor_copy(lo[:, :], colx[:, :]))
            link(V.tensor_scalar(colx[:, :], rec2[:, :], 8, None, ALU.logical_shift_right))
            dve.sem_inc(lo_ready, 2)
            link(V.memset(mx[:, :, :], FAR_ROOT ** 2 * 2))
            link(V.memset(acc[:, :, :], 0.0))

            def weighted(j, k):
                dve.wait_ge(w_ready, j + 1)
                link.put(V.tensor_tensor(wv[k % 2][:, :, :, :],
                                     G[k][:, :, 0:DOUT + 1].unsqueeze(2).to_broadcast([P, BT, HEADS, DOUT + 1]),
                                     w[:, :, :].unsqueeze(3).to_broadcast([P, BT, HEADS, DOUT + 1]), ALU.mult),
                         rows_used, j + 1 + RING)

            def buckets(i):
                return nc.values_load_multi_w_load_instructions(
                    bid_i[0:1, bass.ds(i * TURN, TURN + 2)], engines=[mybir.EngineType.DVE], min_val=0, max_val=TOK - 1)[1]

            def add_up(j, k, bid):
                dve.wait_ge(sums_ready, j + 1)
                dve.wait_ge(c_ready, j + 1)
                a_ = acc[:, bass.ds(bid, 1), :].rearrange("p a (h c) -> p (a h) c", h=HEADS)
                link(V.tensor_tensor(a_, a_, cc[k][:, :].unsqueeze(2).to_broadcast([P, HEADS, DOUT + 1]), ALU.mult))
                link(V.tensor_tensor(a_, a_, psa[k % 2][:, 0:AGG].rearrange("p (h c) -> p h c", h=HEADS), ALU.add), summed, j + 1 + RING)

            def step(i, u, bids, first):
                j, k = i * TURN + u, u % RING
                dve.wait_ge(gathered[k], (i * (TURN // RING) + (u // RING + 1)) * (16 * BT))
                dve.wait_ge(miss_ready, j + 1)
                for t in range(BT - XT):
                    for h in range(HEADS):
                        d = G[k][:, t, DCOL + h:DCOL + h + 1]
                        if t == 0:
                            link.put(V.tensor_scalar(best[:, h, :], miss[k][:, t, :], d, None, ALU.add))
                        else:
                            link.need(HEADS)
                            link.put(V.scalar_tensor_tensor(best[:, h, :], miss[k][:, t, :], d, best[:, h, :],
                                                            ALU.add, ALU.min))
                dve.wait_ge(far_ready, j + 1)
                for t in range(XT):
                    link.need()
                    link.put(V.tensor_tensor(best[:, :, :], best[:, :, :], far[k % 2][:, t, :, :], ALU.min),
                             *((best_ready, j + 3) if t == XT - 1 else ()))
                if not (first and u < 2):
                    add_up(j - 2, (k - 2) % RING, bids[u])
                bid = bids[u + 2]
                m_ = mx[:, bass.ds(bid, 1), :].rearrange("p a h -> p (a h)")
                s_ = s_res[:, bass.ds(bid, 1), :].rearrange("p a h -> p (a h)")
                link.put(V.tensor_tensor(sd[:, HEADS:], s_, m_, ALU.subtract))
                link.put(V.tensor_copy(smb[:, 0:HEADS], s_))
                dve.wait_ge(bestT_ready, j + 1)
                link(V.tensor_reduce(bm[:, :], psb[:, :, :], AX.X, ALU.min))
                link(V.tensor_tensor(m_, m_, bm[:, :], ALU.min))
                link(V.tensor_tensor(sd[:, 0:HEADS], s_, m_, ALU.subtract))
                link(V.scalar_tensor_tensor(smb[:, HEADS:], sd[:, :], SLOPE, sd[:, :], ALU.mult, ALU.max), smb_ready, j + 1)
                if not (first and u < 1):
                    weighted(j - 1, (k - 1) % RING)
                link(V.tensor_tensor(cdiff[:, :], smb[:, 2 * HEADS:], smb[:, HEADS:2 * HEADS], ALU.subtract), cdiff_ready, j + 1)
                dve.wait_ge(se_ready, j + 1)
                se = pss[:, 0:BT * 2 * HEADS].rearrange("p (t c) -> p t c", t=BT)
                link(V.tensor_tensor(z[:, :, :], se[:, :, 0:HEADS], G[k][:, :, DCOL:DCOL + HEADS], ALU.subtract))
                link(V.scalar_tensor_tensor(z[:, :, :], z[:, :, :], SLOPE, z[:, :, :], ALU.mult, ALU.max))
                link(V.tensor_tensor(z[:, :, :], z[:, :, :], se[:, :, HEADS:], ALU.subtract), z_ready, j + 1)

            bids = buckets(0)
            for u in range(TURN):
                step(0, u, bids, True)
            link.settle()
            per = TURN * ((BT - XT) * HEADS + XT - 1 + 5 + 2 + 1)
            link.enter()
            with dve.Fori(1, NB // TURN) as i:
                link.loop(i - 1, per)
                bids = buckets(i)
                for u in range(TURN):
                    step(i, u, bids, False)
                link.settle()
                assert link.n == per, (link.n, per)
            link.leave(per * (NB // TURN - 1))
            weighted(NB - 1, RING - 1)
            bids = buckets(NB // TURN - 1)
            add_up(NB - 2, RING - 2, bids[TURN])
            add_up(NB - 1, RING - 1, bids[TURN + 1])
            den = acc[:, :, :].rearrange("p b (h c) -> p b h c", h=HEADS)
            link(V.tensor_scalar(rden[:, :, :], den[:, :, :, DOUT], 1e-30, None, ALU.max))
            link(V.reciprocal(rden[:, :, :], rden[:, :, :]))
            for h in range(HEADS):
                link(V.tensor_tensor(den[:, :, h, 0:DOUT], den[:, :, h, 0:DOUT],
                                     rden[:, :, h].unsqueeze(2).to_broadcast([P, TOK, DOUT]), ALU.mult))
                xs = x2[:, :, h * DOUT:(h + 1) * DOUT]
                link(V.tensor_tensor(xs, xs, den[:, :, h, 0:DOUT], ALU.add))
            link.settle()

        @block.tensor
        def _(pe):
            T = nc.tensor

            def head(j, k):
                pe.wait_ge(oh_ready, j + 1)
                for t in range(BT):
                    last = T.transpose(pst[k % 2][:, t, :], oh[k][:, t, :], ident[:, :])
                last.then_inc(oh_ps, 1)
                pe.wait_ge(best_ready, j + 3)
                for h in range(HEADS):
                    last = T.transpose(psb[:, h, :], best[:, h, :], ident[:, :])
                last.then_inc(bestT_ready, 1)
                pe.wait_ge(smb_ready, j + 1)
                pe.wait_ge(ohT_ready, j + 1)
                for t in range(BT):
                    last = T.matmul(pss[:, t * 2 * HEADS:(t + 1) * 2 * HEADS], ohT[k % 2][:, t, :], smb[:, 0:2 * HEADS],
                                    start=True, stop=True)
                last.then_inc(se_ready, 1)

            def product(j, k):
                pe.wait_ge(rows_used, j + 1 + RING)
                for t in range(BT):
                    last = T.matmul(psa[k % 2][:, 0:AGG], oh[k][:, t, :], wv[k % 2][:, t, :, :].rearrange("p h c -> p (h c)"),
                                    start=(t == 0), stop=(t == BT - 1))
                last.then_inc(sums_ready, 1)

            for k in range(RING):
                head(k, k)
                if k:
                    product(k - 1, k - 1)
            with pe.Fori(1, NB // RING) as i:
                for k in range(RING):
                    j = i * RING + k
                    head(j, k)
                    product(j - 1, (k - 1) % RING)
            product(NB - 1, RING - 1)


def phase3(nc, v):
    x2, ident, iota_f, pcol, ones = (v[k] for k in ("x2", "ident", "iota_f", "pcol", "ones"))
    rwT, rb, E1, b1, E2, b2, out = (v[k] for k in ("rwT", "rb", "E1", "b1", "E2", "b2", "out"))
    pause, sem = v["pause"], v["sem"]
    HT = EXP * EH // P
    ctx = ExitStack()
    with ctx:
        def sb(name, shape, dt):
            return ctx.enter_context(nc.sbuf_tensor(name, shape, dt))

        def ps(name, shape):
            return ctx.enter_context(nc.psum_tensor(name, shape, fp32))

        e1 = sb("e1", [P, 2, EXP, EH], fp32)
        e2 = sb("e2", [P, HT, C], fp32)
        eb1 = sb("eb1", [P, HT], fp32)
        eb2 = sb("eb2", [EXP, C], fp32)
        rw = sb("rw", [P, 2, EXP], fp32)
        rbr = sb("rbr", [1, EXP], fp32)
        eid = sb("eid", [P, HT], fp32)
        st = sb("st3", [P, 6], fp32)
        mv = sb("mv3", [P, 2], fp32)
        rstd = sb("rstd3", [P, 1], fp32)
        rt = sb("rt3", [P, 1], fp32)
        yn = sb("yn", [P, C], fp32)
        ynT = sb("ynT", [P, 2, P], fp32)
        lg = sb("lg", [P, EXP], fp32)
        top = sb("top", [P, 8], fp32)
        topi = sb("topi", [P, 8], u32)
        idx = sb("idx", [P, 1], fp32)
        idxw = sb("idxw", [P, P], fp32)
        idxb = sb("idxb", [P, P], fp32)
        pick = sb("pick", [EXP, P], fp32)
        hs = sb("hs", [P, HT, P], fp32)
        ot = sb("ot", [P, 1, C], fp32)
        psT = ps("psT3", [P, 2, P])
        psl = ps("psl", [P, 512])
        psh = [ps(f"psh{n}", [P, 4, P]) for n in range(4)]
        psy = ps("psy", [P, 512])

        w3_in, eid_ready = sem("w3_in"), sem("eid_ready")
        yn_ready, yT_ready, ynT_ready, l_ready, idxw_ready, idx_ps, pick_ready, h_ready, relu_ready, masked, y_ready, \
            out_ready, out_sent, out_free = (sem(k + "3") for k in (
                "yn_ready", "yT_ready", "ynT_ready", "l_ready", "idxw_ready", "idx_ps", "pick_ready", "h_ready",
                "relu_ready", "masked", "y_ready", "out_ready", "out_sent", "out_free"))
        chain = sem("chain4")
        with nc.Block() as block:
            @block.sync
            def _(sp):
                for k in range(2):
                    sp.dma_start(e1[:, k, :, :], E1[:, k * P:(k + 1) * P, :].rearrange("e p h -> p e h")).then_inc(w3_in, 16)
                for dst, src in ((e2[:, :, :], E2.rearrange("(m p) c -> p m c", p=P)),
                                 (eb1[:, :], b1), (eb2[:, :], b2),
                                 (rw[:, :, :], rwT.rearrange("(k p) e -> p k e", p=P)), (rbr[:, :], rb)):
                    sp.dma_start(dst, src).then_inc(w3_in, 16)
                with sp.Fori(0, TOK) as i:
                    sp.wait_ge(out_ready, i + 1)
                    sp.dma_start(out[bass.ds(i * P, P), :], ot[:, 0, :]).then_inc(out_sent, 16)
                    sp.wait_ge(out_sent, i * 16 + 16)
                    sp.sem_inc(out_free, 1)
                sp.wait_ge(out_sent, 16 * TOK)

            @block.scalar
            def _(act):
                act.wait_ge(w3_in, 16 * 7)
                with act.Fori(0, TOK) as i:
                    act.wait_ge(yT_ready, i + 1)
                    nc.scalar.copy(ynT[:, :, :], psT[:, :, :]).then_inc(ynT_ready, 1)
                    for q in range(4):
                        act.wait_ge(h_ready, i * 4 + q + 1)
                        for m in range(4):
                            last = nc.scalar.activation(hs[:, 4 * q + m, :], psh[q][:, m, :], ACT.Relu,
                                                        bias=eb1[:, 4 * q + m:4 * q + m + 1])
                        last.then_inc(relu_ready, 1)

            @block.vector
            def _(dve):
                V = nc.vector
                link = Link(dve, chain, pause["dve"])
                dve.sem_inc(out_free, 1)
                link(V.tensor_scalar(eid[:, :], iota_f[:, 0:HT], 2.0, None, ALU.mult))
                link(V.tensor_scalar(idx[:, :], pcol[:, :], float(EH), None, ALU.is_ge))
                link(V.tensor_scalar(eid[:, :], eid[:, :], idx[:, :], None, ALU.add))
                link.enter()
                per = 2 + RSQRT_STEPS + 5 + HT
                with dve.Fori(0, TOK) as i:
                    link.loop(i, per)
                    xi = x2[:, bass.ds(i, 1), :].rearrange("p a c -> p (a c)")
                    link(V.bn_stats(st[:, :], xi))
                    link.settle()
                    link(V.bn_aggr(mv[:, :], st[:, :]))
                    rsqrt(V, link, rstd[:, :], mv[:, 1:2], rt[:, :])
                    link(V.tensor_scalar(yn[:, :], xi, mv[:, 0:1], rstd[:, :], ALU.subtract, ALU.mult), yn_ready, i + 1)
                    dve.wait_ge(l_ready, i + 1)
                    link(V.tensor_copy(lg[:, :], psl[:, 0:EXP]))
                    link.settle()
                    link(V.max(top[:, :], lg[:, :]))
                    link.settle()
                    link(V.max_index(topi[:, :], top[:, :], lg[:, :]))
                    link(V.tensor_copy(idx[:, :], topi[:, 0:1]))
                    link(V.tensor_scalar(idxw[:, :], ones[:, :], idx[:, :], None, ALU.mult), idxw_ready, i + 1)
                    dve.wait_ge(idx_ps, i + 1)
                    link(V.tensor_copy(idxb[:, :], psl[:, P:2 * P]))
                    link(V.tensor_scalar(pick[:, :], idxb[0:EXP, :], pcol[0:EXP, :], None, ALU.is_equal), pick_ready, i + 1)
                    for q in range(4):
                        dve.wait_ge(relu_ready, i * 4 + q + 1)
                        for m in range(4 * q, 4 * q + 4):
                            link(V.scalar_tensor_tensor(hs[:, m, :], idxb[:, :], eid[:, m:m + 1], hs[:, m, :],
                                                        ALU.is_equal, ALU.mult))
                    dve.sem_inc(masked, 1)
                    dve.wait_ge(y_ready, i + 1)
                    dve.wait_ge(out_free, i + 1)
                    link(V.scalar_tensor_tensor(ot[:, :, :], psy[:, 0:C].unsqueeze(1), 0.0, x2[:, bass.ds(i, 1), :],
                                                ALU.max, ALU.add), out_ready, i + 1)
                    assert link.n == per, link.n
                link.leave(per * TOK)

            @block.tensor
            def _(pe):
                T = nc.tensor
                pe.wait_ge(w3_in, 16 * 7)
                with pe.Fori(0, TOK) as i:
                    pe.wait_ge(yn_ready, i + 1)
                    for k in range(2):
                        last = T.transpose(psT[:, k, :], yn[:, k * P:(k + 1) * P], ident[:, :])
                    last.then_inc(yT_ready, 1)
                    pe.wait_ge(ynT_ready, i + 1)
                    for k in range(2):
                        T.matmul(psl[:, 0:EXP], ynT[:, k, :], rw[:, k, :], start=(k == 0), stop=False)
                    T.matmul(psl[:, 0:EXP], ones[0:1, :], rbr[:, :], start=False, stop=True).then_inc(l_ready, 1)
                    for q in range(4):
                        for m in range(4):
                            e = 2 * (4 * q + m)
                            for k in range(2):
                                last = T.matmul(psh[q][:, m, :], e1[:, k, e:e + 2, :].rearrange("p e h -> p (e h)"),
                                                ynT[:, k, :], start=(k == 0), stop=(k == 1))
                        last.then_inc(h_ready, 1)
                    pe.wait_ge(idxw_ready, i + 1)
                    T.matmul(psl[:, P:2 * P], idxw[:, :], ident[:, :], start=True, stop=True).then_inc(idx_ps, 1)
                    pe.wait_ge(masked, i + 1)
                    T.matmul(psy[:, 0:C], pick[:, :], eb2[:, :], start=True, stop=False)
                    for m in range(HT):
                        last = T.matmul(psy[:, 0:C], hs[:, m, :], e2[:, m, :], start=False, stop=(m == HT - 1))
                    last.then_inc(y_ready, 1)


_INS = ["x", "row", "col", "W", "WT", "b", "a", "Wqkv", "Wm", "W1", "W2", "lnp", "rwT", "rb", "E1", "b1", "E2", "b2"]


def kernel(**inputs):
    import numpy as _np
    import concourse.bacc as _bacc
    from concourse import mybir as _mybir
    from concourse.bass_utils import run_bass_kernel_spmd as _run

    g = {k: _np.asarray(v) for k, v in inputs.items()}

    def edges(v, fill):
        return _np.concatenate([v, _np.full(P * EC - E, fill, v.dtype)]).reshape(P, EC)

    host = {
        "x": _np.concatenate([g["x"], _np.zeros((NP - N, C), g["x"].dtype)]),
        "row": edges(g["src"], NP - 1), "col": edges(g["dst"], 0),
        "W": g["L0_gnn_W"], "WT": g["L0_gnn_W"].T, "b": g["L0_gnn_b"].reshape(DOUT, 1),
        "a": _np.concatenate([g["L0_gnn_a_dst"], g["L0_gnn_a_src"]]).T,
        "Wqkv": _np.concatenate([g["L0_mix_Wq"], g["L0_mix_Wk"], g["L0_mix_Wv"]], axis=1),
        "Wm": g["L0_mix_Wm"], "W1": g["L0_mix_W1"], "W2": g["L0_mix_W2"],
        "lnp": _np.stack([g["L0_mix_g1"], g["L0_mix_b1"], g["L0_mix_g2"], g["L0_mix_b2"]]),
        "rwT": g["L0_ffn_router_w"].T, "rb": g["L0_ffn_router_b"].reshape(1, EXP),
        "E1": g["L0_ffn_W1"], "b1": g["L0_ffn_b1"].reshape(EXP * EH // P, P).T,
        "E2": g["L0_ffn_W2"].reshape(EXP * EH, C), "b2": g["L0_ffn_b2"],
    }
    nc = _bacc.Bacc("TRN2", target_bir_lowering=False, num_devices=1)
    arrays, args = {}, []
    for name in _INS:
        arr = _np.ascontiguousarray(host[name])
        arrays[f"in_{name}_dram"] = arr
        args.append(nc.dram_tensor(f"in_{name}_dram", arr.shape, _mybir.dt.from_np(arr.dtype), kind="ExternalInput").ap())
    args.append(nc.dram_tensor("out_0_dram", (NP, C), fp32, kind="ExternalOutput").ap())
    build(nc, *args)
    r = _run(nc, [arrays], core_ids=[0])
    return r.results[0]["out_0_dram"][:N]
```

```python
import concourse.bass as bass
from concourse import mybir
from contextlib import ExitStack

N, C, E = 6250, 256, 200000
P = 128
TOK = -(-N // P)
GROUP = 7
NP = TOK * P
HEADS, DOUT = 4, 64
SLOPE = 0.2
TABW = 72
DCOL = DOUT + 1
AGG = HEADS * (DOUT + 1)
STAGE = 28
PARTS = 2
EC = -(-E // (2 * PARTS * P * STAGE)) * 2 * PARTS * STAGE
EP = EC // PARTS
TURNS = EC // STAGE
BT = 8
BE = BT * P
NB = (P * EC - TOK) // BE + TOK
RING = 4
NB = -(-NB // RING) * RING
ET = NB * BT
XT = 6
NONE = 255
FAR_ROOT = 1e15
MD = 32
HID = 512
EXP, EH = 32, 64
PLACES = 8
ST = -(-((NP - EXP) // P + EXP) // PLACES) * PLACES
LAG = 3
ATT_EPS, LN_EPS = 1e-6, 1e-5

fp32 = mybir.dt.float32
i32 = mybir.dt.int32
u32 = mybir.dt.uint32
ALU = mybir.AluOpType
ACT = mybir.ActivationFunctionType
AX = mybir.AxisListType


class Link:

    def __init__(self, eng, sem, pause):
        self.eng, self.sem, self.pause, self.base, self.n = eng, sem, pause, 0, 0

    def loop(self, i, per):
        self.base, self.n = self.base0 + i * per, 0

    def enter(self):
        self.base0 = self.base + self.n

    def leave(self, total):
        self.base, self.n = self.base0 + total, 0

    def put(self, ins, sem=None, value=None):
        if sem is None:
            self.n += 1
            sem, value = self.sem, self.base + self.n
        ins.then_inc(sem, 1)
        self.last = sem, value

    def need(self, back=1):
        if back == 1:
            self.eng.wait_ge(*self.last)
        else:
            self.eng.wait_ge(self.sem, self.base + self.n + 1 - back)

    def chained(self):
        self.eng.wait_ge(self.sem, self.base + self.n)

    def settle(self):
        self.eng.sem_inc(self.pause, 1)

    def __call__(self, ins, sem=None, value=None):
        self.put(ins, sem, value)
        self.need()


def build(nc, x, row, col, W, WT, b, a, Wqkv, Wm, W1, W2, lnp, rwT, rb, E1, b1, E2, b2, out):
    table = nc.dram_tensor("table", (NP, TABW), fp32).ap()
    slots = nc.dram_tensor("slots", (P * ET, 1), i32).ap()
    ctx = ExitStack()
    with ctx:
        def sb(name, shape, dt, c=ctx):
            return c.enter_context(nc.sbuf_tensor(name, shape, dt))

        def ps(name, shape, c=ctx, dt=fp32):
            return c.enter_context(nc.psum_tensor(name, shape, dt))

        def sem(name):
            return ctx.enter_context(nc.semaphore(name))

        pause = {e: sem("pause_" + e) for e in ("dve", "act", "pool", "pe")}

        x2 = sb("x2", [P, TOK + 2, C], fp32)
        s_res = sb("s_res", [P, TOK, HEADS], fp32)
        ident = sb("ident", [P, P], fp32)
        iota_f = sb("iota_f", [P, P], fp32)
        ones = sb("ones", [P, P], fp32)
        bid_i = sb("bid_i", [1, NB + 2], i32)

        phase1(nc, locals())
        phase2(nc, locals())
        phase3(nc, locals())


NEWTON = 3


def rsqrt(V, link, y, var, t):
    link(V.tensor_scalar(var, var, LN_EPS, None, ALU.add))
    link(V.tensor_scalar(y.bitcast(i32), var.bitcast(i32), -0.5, float(0x5F3759DF), ALU.mult, ALU.add))
    for _ in range(NEWTON):
        link(V.tensor_tensor(t, y, y, ALU.mult))
        link(V.tensor_tensor(t, t, var, ALU.mult))
        link(V.tensor_scalar(t, t, -0.5, 1.5, ALU.mult, ALU.add))
        link(V.tensor_tensor(y, y, t, ALU.mult))


def spreads(V, dve, link, x2, st, mv, mvs, rstd, rt):
    link.enter()
    with dve.Fori(0, TOK // GROUP) as i:
        link.loop(i, 2 * GROUP + 1)
        for n in range(GROUP):
            link.put(V.bn_stats(st[:, n, :], x2[:, bass.ds(i * GROUP + n, 1), :].rearrange("p a c -> p (a c)")))
        link.need()
        link.settle()
        for n in range(GROUP):
            link.put(V.bn_aggr(mv[:, n, :], st[:, n, :]))
        link.need()
        link(V.tensor_copy(mvs[:, bass.ds(i * GROUP, GROUP), :], mv[:, :, :]))
        link.settle()
    link.leave((2 * GROUP + 1) * (TOK // GROUP))
    rsqrt(V, link, rstd[:, :], mvs[:, :, 1], rt[:, :])


def phase1(nc, v):
    x, row, col, W, WT, b, a = (v[k] for k in ("x", "row", "col", "W", "WT", "b", "a"))
    Wqkv, Wm, W1, W2, lnp = (v[k] for k in ("Wqkv", "Wm", "W1", "W2", "lnp"))
    table, slots = v["table"], v["slots"]
    x2, s_res, ident, iota_f, ones, bid_i = (v[k] for k in ("x2", "s_res", "ident", "iota_f", "ones", "bid_i"))
    pause, sem = v["pause"], v["sem"]
    ctx = ExitStack()
    with ctx:
        def sb(name, shape, dt):
            return ctx.enter_context(nc.sbuf_tensor(name, shape, dt))

        def ps(name, shape):
            return ctx.enter_context(nc.psum_tensor(name, shape, fp32))

        rec = sb("rec", [P, EC], i32)
        addr = sb("addr", [P, EC], i32)
        blk = sb("blk", [P, EC], fp32)
        pos = sb("pos", [P, EC], fp32)
        eq = sb("eq", [P, EC], fp32)
        cum = sb("cum", [P, EC], fp32)
        cnt = sb("cnt", [P, TOK], fp32)
        base = sb("base", [P, TOK], fp32)
        tot = sb("tot", [P, TOK], fp32)
        tot_i = sb("tot_i", [P, TOK], i32)
        ends = sb("ends", [P, TOK], fp32)
        before = sb("before", [P, P], fp32)
        rec_s = [sb(f"rec_s{n}", [P, STAGE], i32) for n in range(2)]
        addr_s = [sb(f"addr_s{n}", [P, STAGE], i32) for n in range(2)]
        biota = sb("biota", [1, NB], fp32)
        bidf = sb("bidf", [1, NB], fp32)
        wcat = sb("wcat", [P, 2, TABW + 1], fp32)
        brow = sb("brow", [1, TABW + 1], fp32)
        wT = sb("wT", [DOUT, C], fp32)
        aT = sb("aT", [DOUT, 2 * HEADS], fp32)
        bcol = sb("bcol", [DOUT, 1], fp32)
        wqkv = sb("wqkv", [P, 2, 3 * C], fp32)
        wm = sb("wm", [P, 2, C], fp32)
        w1 = sb("w1", [P, 4, HID], fp32)
        w2 = sb("w2", [P, 4, C], fp32)
        blockm = sb("blockm", [P, P], fp32)
        valid = sb("valid", [P, TOK], fp32)
        kvb = sb("kvb", [P, 2, P], fp32)
        ksb = sb("ksb", [P, 2, P], fp32)
        kvacc = sb("kvacc", [P, 2, P + 1], fp32)
        xnT = sb("xnT", [P, 2, NP], fp32)
        of_b = [xnT[:, 1, (n + 1) * EP:(n + 2) * EP] for n in range(2)]
        mvs = sb("mvs", [P, TOK, 2], fp32)
        rstd = sb("rstd", [P, TOK], fp32)
        rt = sb("rt", [P, TOK], fp32)
        sts = sb("sts", [P, GROUP, 6], fp32)
        mvg = sb("mvg", [P, GROUP, 2], fp32)
        st = sb("st", [P, 6], fp32)
        mv2 = sb("mv2", [P, 2, 2], fp32)
        rs2 = sb("rs2", [P, 2], fp32)
        rt2 = sb("rt2", [P, 2], fp32)
        xn = sb("xn", [P, 2, C], fp32)
        xTs = sb("xTs", [P, 2, 2 * P], fp32)
        tab = sb("tab", [P, 2, TABW], fp32)
        kmin = sb("kmin", [P, 2, C], fp32)
        kexp = sb("kexp", [P, 2, C], fp32)
        kk = sb("kk", [P, 2, C], fp32)
        va = sb("va", [P, 2, 2, P + 1], fp32)
        rec_d = sb("rec_d", [P, 2, 2 * P], fp32)
        msgT = sb("msgT", [P, 2, 2 * P], fp32)
        m1 = sb("m1", [P, 2, C], fp32)
        m1T = sb("m1T", [P, 2, 2 * P], fp32)
        hT = sb("hT", [P, 4, 2 * P], fp32)
        lnb = sb("lnb", [P, 4, C], fp32)

        ps_cnt = ps("ps_cnt", [P, 2, P])
        psT = ps("psT", [P, 2, 2 * P])
        ps_all = ps("ps_all", [P, 4 * 512])
        ps_pos = ps_all[:, 0:EP]
        ps_kv = ps_all[:, 0:1024].rearrange("p (t n) -> p t n", t=2)
        ps_h = ps_all[:, 1024:2048].rearrange("p (m n) -> p m n", m=4)
        ps_o = ps("ps_o", [P, 2, C])
        ps_q = ps("ps_q", [P, 2, 2 * P])

        rows_in, w_in, ln_in, filled, consts = (sem(k) for k in ("rows_in", "w_in", "ln_in", "filled", "consts"))
        fill_ready, counted, ranked = sem("fill_ready"), sem("counted"), sem("ranked")
        wa_ready, wa_done, blk_ready = sem("wa_ready"), sem("wa_done"), sem("blk_ready")
        placed, staged, scattered = sem("placed"), sem("staged"), [sem(f"scattered{n}") for n in range(2)]
        xn_ready, xT_ready, xTs_ready, kv_ready, kmin_ready, kexp_ready, k_ready, KV_ready = (
            sem(k) for k in ("xn_ready", "xT_ready", "xTs_ready", "kv_ready", "kmin_ready",
                             "kexp_ready", "k_ready", "KV_ready"))
        tab_ready, tab_out = sem("tab_ready"), sem("tab_out")
        kvb_ready, q_ready, qmin_ready, qexp_ready, q_done, dm_ready, msg_ready, m_ready, m1_ready, m1T_ps, m1T_ready, \
            h_ready, hT_ready, o_ready = (sem(k) for k in (
                "kvb_ready", "q_ready", "qmin_ready", "qexp_ready", "q_done", "dm_ready", "msg_ready", "m_ready",
                "m1_ready", "m1T_ps", "m1T_ready", "h_ready", "hT_ready", "o_ready"))
        KV_used, o_used = sem("KV_used"), sem("o_used")
        x_all, tab_free = sem("x_all"), sem("tab_free")
        dve_chain = sem("dve_chain")
        edges_near, of_ready, of_used = sem("edges_near"), sem("of_ready"), sem("of_used")
        pool_const = sem("pool_const")

        block = ctx.enter_context(nc.Block())

        @block.sync
        def _(sp):
            sp.dma_start(rec[:, :], row).then_inc(rows_in, 16)
            sp.dma_start(x2[:, 0:TOK, :], x.rearrange("(t p) c -> p t c", p=P)).then_inc(x_all, 16)
            sp.dma_start(addr[:, :], col).then_inc(rows_in, 16)
            for dst, src in ((wcat[:, :, 0:DOUT], W.rearrange("(k p) n -> p k n", p=P)), (wT[:, :], WT), (aT[:, :], a),
                             (bcol[:, :], b), (brow[:, 0:DOUT], b.rearrange("n o -> o n")),
                             (wqkv[:, :, :], Wqkv.rearrange("(k p) n -> p k n", p=P)),
                             (wm[:, :, :], Wm.rearrange("(k p) n -> p k n", p=P)),
                             (w1[:, :, :], W1.rearrange("(k p) n -> p k n", p=P)),
                             (w2[:, :, :], W2.rearrange("(k p) n -> p k n", p=P))):
                sp.dma_start(dst, src).then_inc(w_in, 16)
            sp.wait_ge(fill_ready, 1)
            sp.dma_start(slots.rearrange("(p e) o -> p (e o)", p=P), xnT[:, 0, 0:ET].bitcast(i32)).then_inc(filled, 16)

            def rows_out(i, w):
                sp.wait_ge(tab_ready, i + 1)
                sp.dma_start(table[bass.ds(i * (2 * P), w * P), :].rearrange("(t p) c -> p t c", p=P),
                             tab[:, 0:w, :]).then_inc(tab_out, 16)
                sp.wait_ge(tab_out, i * 16 + 16)
                sp.sem_inc(tab_free, 1)

            with sp.Fori(0, TOK // 2) as i:
                rows_out(i, 2)
            rows_out(TOK // 2, TOK % 2)

        @block.gpsimd
        def _(pool):
            pool.memset(ones[:, :], 1.0).then_inc(consts, 1)
            pool.memset(ident[:, :], 1.0).then_inc(pool_const, 1)
            pool.memset(before[:, :], 1.0).then_inc(pool_const, 1)
            pool.memset(blockm[:, :], 1.0).then_inc(pool_const, 1)
            pool.wait_ge(pool_const, 3)
            pool.affine_select(out=ident[:, :], in_=ident[:, :], compare_op=ALU.is_equal, fill=0.0, base=0,
                               pattern=[[-1, P]], channel_multiplier=1).then_inc(consts, 1)
            pool.affine_select(out=before[:, :], in_=before[:, :], compare_op=ALU.is_gt, fill=0.0, base=0,
                               pattern=[[1, P]], channel_multiplier=-1).then_inc(consts, 1)
            bm = blockm[:, :].rearrange("p (a c) -> p a c", c=MD)
            pool.affine_select(out=bm, in_=bm, compare_op=ALU.is_ge, fill=0.0, base=0,
                               pattern=[[-MD, P // MD], [0, MD]], channel_multiplier=1).then_inc(pool_const, 1)
            pool.wait_ge(pool_const, 4)
            pool.affine_select(out=bm, in_=bm, compare_op=ALU.is_ge, fill=0.0, base=MD - 1,
                               pattern=[[MD, P // MD], [0, MD]], channel_multiplier=-1).then_inc(consts, 1)
            for t, pattern, up in ((iota_f, [[1, P]], 0), (valid, [[P, TOK]], 1),
                                   (biota, [[1, NB]], 0)):
                pool.iota(t[:, :], pattern, base=0, channel_multiplier=up,
                          allow_small_or_imprecise_dtypes=True).then_inc(consts, 1)
            for c in range(4):
                pool.dma_start(lnb[:, c, :], lnp[c:c + 1, :].to_broadcast([P, C])).then_inc(ln_in, 16)
            pool.wait_ge(ln_in, 64)
            pool.wait_ge(filled, 16)

            def turn(i, n, wait):
                if wait:
                    pool.wait_ge(scattered[n], i * (16 * STAGE))
                    pool.sem_inc(pause["pool"], 1)
                cols = bass.ds(i * (2 * STAGE) + n * STAGE, STAGE)
                pool.tensor_copy(rec_s[n][:, :], rec[:, cols]).then_inc(staged, 1)
                pool.tensor_copy(addr_s[n][:, :], addr[:, cols]).then_inc(staged, 1)
                pool.wait_ge(staged, i * 4 + 2 * n + 2)
                pool.sem_inc(pause["pool"], 1)
                for k in range(STAGE):
                    pool.indirect_dma_start(slots, bass.IndirectOffsetOnAxis(ap=addr_s[n][:, k:k + 1].bitcast(u32), axis=0),
                                            rec_s[n][:, k:k + 1], None).then_inc(scattered[n], 16)

            per = TURNS // (2 * PARTS)
            for q in range(PARTS):
                pool.wait_ge(placed, q + 1)
                pool.sem_inc(pause["pool"], 1)
                if q == 0:
                    for n in range(2):
                        turn(0, n, False)
                with pool.Fori(max(q * per, 1), (q + 1) * per) as i:
                    for n in range(2):
                        turn(i, n, True)
            for n in range(2):
                pool.wait_ge(scattered[n], 16 * STAGE * TURNS // 2)

        @block.scalar
        def _(act):
            act.wait_ge(wa_ready, 1)
            wa = ps_h[:, 0, 0:16].rearrange("p (k n) -> p k n", k=2)
            nc.scalar.mul(wcat[:, :, DCOL:DCOL + HEADS], wa[:, :, 0:HEADS], -1.0)
            nc.scalar.copy(wcat[:, :, DCOL + HEADS:], wa[:, :, HEADS:]).then_inc(wa_done, 1)
            nc.scalar.mul(brow[:, DCOL:DCOL + HEADS], ps_h[0:1, 0, 16:16 + HEADS], -1.0)
            nc.scalar.copy(brow[:, DCOL + HEADS:], ps_h[0:1, 0, 16 + HEADS:16 + 2 * HEADS]).then_inc(wa_done, 1)

            def edges_of(q, b_, n):
                act.wait_ge(of_used, b_ + (q * TOK + 1))
                act.sem_inc(pause["act"], 1)
                nc.scalar.activation(of_b[n], blk[:, q * EP:(q + 1) * EP], ACT.Square, scale=-1.0,
                                     bias=iota_f[:, bass.ds(b_, 1)]).then_inc(edges_near, 1)
                act.wait_ge(edges_near, b_ + (q * TOK + 1))
                nc.scalar.activation(of_b[n], of_b[n], ACT.Relu, scale=-1.0, bias=ones[:, 0:1]).then_inc(of_ready, 1)

            act.wait_ge(blk_ready, 1)
            act.wait_ge(consts, 7)
            for q in range(PARTS):
                with act.Fori(0, TOK // 8) as i:
                    for n in range(8):
                        edges_of(q, i * 8 + n, (q * TOK + n) % 2)
                edges_of(q, TOK - 1, (q * TOK + TOK - 1) % 2)

            def first(i, w):
                act.wait_ge(xT_ready, i + 1)
                nc.scalar.copy(xTs[:, :, 0:w * P], psT[:, :, 0:w * P]).then_inc(xTs_ready, 1)
                act.wait_ge(kv_ready, i + 1)
                act.wait_ge(tab_free, i + 1)
                nc.scalar.copy(tab[:, 0:w, :], ps_o[:, 0:w, 0:TABW]).then_inc(tab_ready, 1)
                act.wait_ge(kmin_ready, i + 1)
                nc.scalar.activation(kexp[:, 0:w, :], kmin[:, 0:w, :], ACT.Exp).then_inc(kexp_ready, 1)

            def second(i, w):
                act.wait_ge(qmin_ready, i + 1)
                nc.scalar.activation(kexp[:, :, 0:w * P], kmin[:, :, 0:w * P], ACT.Exp).then_inc(qexp_ready, 1)
                act.wait_ge(m1T_ps, i + 1)
                nc.scalar.copy(m1T[:, :, 0:w * P], psT[:, :, 0:w * P]).then_inc(m1T_ready, 1)
                for m in range(0, 4, 2):
                    act.wait_ge(h_ready, i * 2 + m // 2 + 1)
                    nc.scalar.activation(hT[:, m:m + 2, 0:w * P], ps_h[:, m:m + 2, 0:w * P], ACT.Relu).then_inc(hT_ready, 1)

            for part in (first, second):
                with act.Fori(0, TOK // 2) as i:
                    part(i, 2)
                part(TOK // 2, TOK % 2)

        @block.vector
        def _(dve):
            link = Link(dve, dve_chain, pause["dve"])
            V = nc.vector
            dve.sem_inc(tab_free, 1)
            V.memset(xnT[:, 0, 0:ET].bitcast(i32), NONE).then_inc(fill_ready, 1)
            V.memset(wcat[:, :, DOUT:DCOL], 0.0)
            V.memset(brow[:, DOUT:DCOL], 1.0).then_inc(wa_done, 1)
            dve.sem_inc(of_used, 2)
            dve.wait_ge(rows_in, 32)
            link(V.tensor_scalar(cum[:, :].bitcast(i32), rec[:, :], 7, None, ALU.arith_shift_right))
            link(V.tensor_copy(blk[:, :], cum[:, :].bitcast(i32)))
            dve.sem_inc(blk_ready, 1)
            link(V.tensor_scalar(eq[:, :].bitcast(i32), rec[:, :], P - 1, None, ALU.bitwise_and))
            link(V.tensor_scalar(cum[:, :].bitcast(i32), addr[:, :], 8, None, ALU.logical_shift_left))
            link(V.tensor_tensor(rec[:, :], cum[:, :].bitcast(i32), eq[:, :].bitcast(i32), ALU.bitwise_or))
            link(V.memset(pos[:, :], 0.0))
            dve.wait_ge(consts, 7)
            link(V.tensor_scalar(valid[:, :], valid[:, :], float(N), None, ALU.is_lt))
            link.enter()
            with dve.Fori(0, TOK // GROUP) as i:
                link.loop(i, GROUP)
                for n in range(GROUP):
                    b_ = bass.ds(i * GROUP + n, 1)
                    link(V.tensor_scalar(eq[:, :], blk[:, :], iota_f[:, b_], 0.0, ALU.is_equal, ALU.add,
                                         accum_out=cnt[:, b_]))
                link.settle()
            link.leave(TOK)
            dve.sem_inc(counted, 1)
            dve.wait_ge(ranked, 1)
            link(V.tensor_scalar(tot_i[:, :], ps_cnt[:, 1, 0:TOK], float(BE - 1), None, ALU.add))
            link(V.tensor_scalar(tot_i[:, :], tot_i[:, :], BE.bit_length() - 1, None, ALU.arith_shift_right))
            link(V.tensor_copy(tot[:, :], tot_i[:, :]))
            link(V.tensor_tensor_scan(ends[:, :], ones[:, 0:TOK], tot[:, :], 0.0, ALU.mult, ALU.add))
            link(V.tensor_tensor(base[:, :], ends[:, :], tot[:, :], ALU.subtract))
            link(V.scalar_tensor_tensor(base[:, :], base[:, :], float(BE), ps_cnt[:, 0, 0:TOK], ALU.mult, ALU.add))
            link(V.tensor_scalar(base[:, :], base[:, :], -1.0, None, ALU.add))
            def ranks(q, b_, n):
                at = base[:, bass.ds(b_, 1)]
                dve.wait_ge(of_ready, b_ + (q * TOK + 1))
                link(V.tensor_tensor_scan(ps_pos, ones[:, 0:1].to_broadcast([P, EP]), of_b[n], at, ALU.mult, ALU.add))
                link.settle()
                link.put(V.tensor_copy(at, ps_pos[:, EP - 1:EP]))
                link(V.copy_predicated(pos[:, q * EP:(q + 1) * EP], of_b[n].bitcast(u32), ps_pos),
                     of_used, b_ + (q * TOK + 3))

            dve.wait_ge(wa_done, 3)
            for q in range(PARTS):
                link.enter()
                with dve.Fori(0, TOK // 8) as i:
                    link.loop(i, 16)
                    for n in range(8):
                        ranks(q, i * 8 + n, (q * TOK + n) % 2)
                    link.settle()
                link.leave(TOK // 8 * 16)
                ranks(q, TOK - 1, (q * TOK + TOK - 1) % 2)
                addr_q, eq_q, cum_q = (t[:, q * EP:(q + 1) * EP] for t in (addr, eq, cum))
                link(V.tensor_copy(addr_q, pos[:, q * EP:(q + 1) * EP]))
                link(V.tensor_scalar(eq_q.bitcast(i32), addr_q, P - 1, None, ALU.bitwise_and))
                link(V.tensor_scalar(cum_q.bitcast(i32), addr_q, 7, None, ALU.arith_shift_right))
                link(V.scalar_tensor_tensor(addr_q, eq_q.bitcast(i32), float(ET), cum_q.bitcast(i32), ALU.mult, ALU.add),
                     placed, q + 1)
            dve.wait_ge(x_all, 16)
            link(V.memset(x2[:, TOK:, :], 0.0))
            spreads(V, dve, link, x2, sts, mvg, mvs, rstd, rt)
            dve.wait_ge(filled, 16)

            def first(i, w):
                for t in range(w):
                    link.put(V.tensor_scalar(xn[:, t:t + 1, :], x2[:, bass.ds(i * 2 + t, 1), :], mvs[:, bass.ds(i * 2 + t, 1), 0],
                                             rstd[:, bass.ds(i * 2 + t, 1)], ALU.subtract, ALU.mult),
                             *((xn_ready, i + 1) if t == w - 1 else ()))
                link.need()
                xs = x2[:, bass.ds(i * 2, w), :]
                link.put(V.tensor_tensor(xs, xs, xn[:, 0:w, :], ALU.add))
                dve.wait_ge(kv_ready, i + 1)
                link(V.tensor_scalar(kmin[:, 0:w, :], ps_kv[:, 0:w, 0:C], 0.0, None, ALU.min), kmin_ready, i + 1)
                link.put(V.tensor_copy(va[:, 0:w, :, 0:P], ps_kv[:, 0:w, C:2 * C].rearrange("p t (g n) -> p t g n", g=2)))
                link.put(V.tensor_copy(va[:, 0:w, :, P], valid[:, bass.ds(i * 2, w)].unsqueeze(2).to_broadcast([P, w, 2])))
                dve.wait_ge(tab_ready, i + 1)
                link.put(V.tensor_copy(s_res[:, bass.ds(i * 2, w), :], ps_o[:, 0:w, DCOL + HEADS:TABW + 1]))
                dve.wait_ge(kexp_ready, i + 1)
                link(V.scalar_tensor_tensor(kk[:, 0:w, :], ps_kv[:, 0:w, 0:C], 0.0, kexp[:, 0:w, :], ALU.max, ALU.add),
                     k_ready, i + 1)
                link.put(V.tensor_copy(xnT[:, :, bass.ds(i * (2 * P), w * P)], xTs[:, :, 0:w * P]))
                dve.wait_ge(KV_ready, i + 1)
                link(V.tensor_tensor(kvacc[:, :, :], kvacc[:, :, :], ps_q[:, :, 0:P + 1], ALU.add), KV_used, i + 1)

            def norm(w, dst, sem=None, value=None):
                for t in range(w):
                    link(V.bn_stats(st[:, :], ps_o[:, t, :]))
                    link.settle()
                    link(V.bn_aggr(mv2[:, t, :], st[:, :]))
                rsqrt(V, link, rs2[:, 0:w], mv2[:, 0:w, 1], rt2[:, 0:w])
                for t in range(w):
                    link.put(V.tensor_scalar(dst[:, t, :], ps_o[:, t, :], mv2[:, t, 0:1], rs2[:, t:t + 1], ALU.subtract, ALU.mult),
                             *((sem, value) if t == w - 1 else ()))
                link.need()

            def scaled(w, n, sem=None, value=None):
                g_, b_ = (lnb[:, 2 * n + c:2 * n + c + 1, :].to_broadcast([P, w, C]) for c in range(2))
                link(V.tensor_tensor(m1[:, 0:w, :], m1[:, 0:w, :], g_, ALU.mult))
                link(V.tensor_tensor(m1[:, 0:w, :], m1[:, 0:w, :], b_, ALU.add), sem, value)

            def second(i, w):
                f = w * P
                dve.wait_ge(q_ready, i + 1)
                link(V.tensor_scalar(kmin[:, :, 0:f], ps_q[:, :, 0:f], 0.0, None, ALU.min), qmin_ready, i + 1)
                dve.wait_ge(qexp_ready, i + 1)
                link(V.scalar_tensor_tensor(kk[:, :, 0:f], ps_q[:, :, 0:f], 0.0, kexp[:, :, 0:f], ALU.max, ALU.add), q_done, i + 1)
                dve.wait_ge(dm_ready, i + 1)
                link(V.tensor_scalar(rec_d[:, :, 0:f], ps_kv[:, :, 0:f], ATT_EPS, None, ALU.add))
                link(V.reciprocal(rec_d[:, :, 0:f], rec_d[:, :, 0:f]))
                link(V.tensor_tensor(msgT[:, :, 0:f], ps_kv[:, :, 2 * P:2 * P + f], rec_d[:, :, 0:f], ALU.mult), msg_ready, i + 1)
                dve.wait_ge(m_ready, i + 1)
                norm(w, m1)
                scaled(w, 0, m1_ready, i + 1)
                dve.wait_ge(o_ready, i + 1)
                norm(w, m1, o_used, i + 1)
                scaled(w, 1)
                xs = x2[:, bass.ds(i * 2, w), :]
                link(V.tensor_tensor(xs, xs, m1[:, 0:w, :], ALU.add))
                link.settle()

            def passed(part, per):
                link.enter()
                with dve.Fori(0, TOK // 2) as i:
                    link.loop(i, per)
                    part(i, 2)
                    assert link.n == per, (link.n, per)
                link.leave(per * (TOK // 2))
                part(TOK // 2, TOK % 2)

            link(V.memset(kvacc[:, :, :], 0.0))
            passed(first, 6)
            for g in range(2):
                link(V.tensor_tensor(kvb[:, g, :], kvacc[:, g, 0:P], blockm[:, :], ALU.mult))
                link(V.tensor_scalar(ksb[:, g, :], blockm[:, :], kvacc[:, g, P:P + 1], None, ALU.mult))
            dve.sem_inc(kvb_ready, 1)
            dve.wait_ge(ln_in, 64)
            passed(second, 1 + 2 * (4 + 2 + 4 * NEWTON) + 1 + 1 + 3 + 3)
            link(V.memset(bidf[:, :], 0.0))
            link.enter()
            with dve.Fori(0, TOK // GROUP) as i:
                link.loop(i, GROUP)
                for n in range(GROUP):
                    link(V.scalar_tensor_tensor(bidf[:, :], biota[:, :], ends[0:1, bass.ds(i * GROUP + n, 1)], bidf[:, :],
                                                ALU.is_ge, ALU.add))
                link.settle()
            link.leave(TOK)
            link(V.tensor_scalar(bidf[:, :], bidf[:, :], float(TOK - 1), None, ALU.min))
            link(V.memset(bid_i[:, 0:2], 0))
            link(V.tensor_copy(bid_i[:, 2:], bidf[:, :]))

        @block.tensor
        def _(pe):
            T = nc.tensor
            pe.sem_inc(pause["pe"], 1)
            pe.wait_ge(w_in, 16 * 9)
            for k in range(2):
                T.matmul(ps_h[:, 0, 8 * k:8 * k + 8], wT[:, k * P:(k + 1) * P], aT[:, :], start=True, stop=True)
            T.matmul(ps_h[0:1, 0, 16:24], bcol[:, :], aT[:, :], start=True, stop=True).then_inc(wa_ready, 1)
            pe.wait_ge(counted, 1)
            T.matmul(ps_cnt[:, 0, 0:TOK], before[:, :], cnt[:, :], start=True, stop=True)
            T.matmul(ps_cnt[:, 1, 0:TOK], ones[:, :], cnt[:, :], start=True, stop=True).then_inc(ranked, 1)
            pe.wait_ge(wa_done, 3)

            def first(i, w):
                pe.wait_ge(xn_ready, i + 1)
                for t in range(w):
                    for k in range(2):
                        last = T.transpose(psT[:, k, t * P:(t + 1) * P], xn[:, t, k * P:(k + 1) * P], ident[:, :])
                last.then_inc(xT_ready, 1)
                pe.wait_ge(xTs_ready, i + 1)
                for t in range(w):
                    xk = [xTs[:, k, t * P:(t + 1) * P] for k in range(2)]
                    for k in range(2):
                        T.matmul(ps_kv[:, t, :], xk[k], wqkv[:, k, C:3 * C], start=(k == 0), stop=(k == 1))
                    for k in range(2):
                        T.matmul(ps_o[:, t, 0:TABW + 1], xk[k], wcat[:, k, :], start=(k == 0), stop=False)
                    last = T.matmul(ps_o[:, t, 0:TABW + 1], ones[0:1, :], brow[:, :], start=False, stop=True)
                last.then_inc(kv_ready, 1)
                pe.wait_ge(k_ready, i + 1)
                for g in range(2):
                    for t in range(w):
                        last = T.matmul(ps_q[:, g, 0:P + 1], kk[:, t, g * P:(g + 1) * P], va[:, t, g, :],
                                        start=(t == 0), stop=(t == w - 1))
                last.then_inc(KV_ready, 1)
                pe.wait_ge(KV_used, i + 1)
                pe.sem_inc(pause["pe"], 1)

            def queries(i, w):
                f = w * P
                tok = bass.ds(i * (2 * P), f)
                for m in range(2):
                    for k in range(2):
                        last = T.matmul(ps_q[:, m, 0:f], wqkv[:, k, m * P:(m + 1) * P], xnT[:, k, tok],
                                        start=(k == 0), stop=(k == 1))
                last.then_inc(q_ready, 1)

            def second(i, w, after):
                f = w * P
                tok = bass.ds(i * (2 * P), f)
                pe.wait_ge(q_done, i + 1)
                for g in range(2):
                    T.matmul(ps_kv[:, g, 0:f], ksb[:, g, :], kk[:, g, 0:f], start=True, stop=True)
                    last = T.matmul(ps_kv[:, g, 2 * P:2 * P + f], kvb[:, g, :], kk[:, g, 0:f], start=True, stop=True)
                last.then_inc(dm_ready, 1)
                pe.wait_ge(msg_ready, i + 1)
                for t in range(w):
                    for g in range(2):
                        last = T.matmul(ps_o[:, t, :], msgT[:, g, t * P:(t + 1) * P], wm[:, g, :], start=(g == 0), stop=(g == 1))
                last.then_inc(m_ready, 1)

                def hidden(m, ks):
                    for k in ks:
                        src = xnT[:, k, tok] if k < 2 else m1T[:, k - 2, 0:f]
                        last = T.matmul(ps_h[:, m, 0:f], w1[:, k, m * P:(m + 1) * P], src, start=(k == 0), stop=(k == 3))
                    return last

                for m in range(0, 4, 2):
                    hidden(m, range(2))
                pe.wait_ge(m1_ready, i + 1)
                for t in range(w):
                    for k in range(2):
                        last = T.transpose(psT[:, k, t * P:(t + 1) * P], m1[:, t, k * P:(k + 1) * P], ident[:, :])
                last.then_inc(m1T_ps, 1)
                pe.wait_ge(m1T_ready, i + 1)
                for m in range(0, 4, 2):
                    hidden(m, range(2, 4))
                    hidden(m + 1, range(4)).then_inc(h_ready, 1)
                if after:
                    queries(i + 1, after)
                pe.wait_ge(hT_ready, i * 2 + 2)
                for t in range(w):
                    for k in range(4):
                        last = T.matmul(ps_o[:, t, :], hT[:, k, t * P:(t + 1) * P], w2[:, k, :], start=(k == 0), stop=(k == 3))
                last.then_inc(o_ready, 1)

            with pe.Fori(0, TOK // 2) as i:
                first(i, 2)
            first(TOK // 2, TOK % 2)
            pe.wait_ge(kvb_ready, 1)
            queries(0, 2)
            with pe.Fori(0, TOK // 2 - 1) as i:
                second(i, 2, 2)
            second(TOK // 2 - 1, 2, TOK % 2)
            second(TOK // 2, TOK % 2, 0)


def phase2(nc, v):
    table, slots = v["table"], v["slots"]
    x2, s_res, ident, iota_f, bid_i = (v[k] for k in ("x2", "s_res", "ident", "iota_f", "bid_i"))
    pause, sem = v["pause"], v["sem"]
    ctx = ExitStack()
    with ctx:
        def sb(name, shape, dt):
            return ctx.enter_context(nc.sbuf_tensor(name, shape, dt))

        def ps(name, shape):
            return ctx.enter_context(nc.psum_tensor(name, shape, fp32))

        colx = sb("colx", [P, ET], i32)
        lo = sb("lo", [P, ET], fp32)
        mx = sb("mx", [P, TOK, HEADS], fp32)
        acc = sb("acc", [P, TOK, AGG], fp32)
        ix = [sb(f"ix{n}", [P, BT], i32) for n in range(RING)]
        G = [sb(f"G{n}", [P, BT, TABW], fp32) for n in range(RING)]
        oh = [sb(f"oh{n}", [P, BT, P], fp32) for n in range(RING)]
        cc = [sb(f"cc{n}", [P, HEADS], fp32) for n in range(RING)]
        miss = [sb(f"miss{n}", [P, BT, P], fp32) for n in range(2)]
        far = [sb(f"far{n}", [P, XT, HEADS, P], fp32) for n in range(2)]
        ohT = sb("ohT", [P, BT, P], fp32)
        wv = sb("wv", [P, BT, HEADS, DOUT + 1], fp32)
        best = sb("best", [P, HEADS, P], fp32)
        one = sb("one", [P, 1], fp32)
        bm = sb("bm", [P, HEADS], fp32)
        sd = sb("sd", [P, 2 * HEADS], fp32)
        smb = sb("smb", [P, 3 * HEADS], fp32)
        cdiff = sb("cdiff", [P, HEADS], fp32)
        z = sb("z", [P, BT, HEADS], fp32)
        w = sb("w", [P, BT, HEADS], fp32)
        rden = sb("rden", [P, TOK, HEADS], fp32)

        psb = ps("psb", [P, HEADS, P])
        pst = [ps(f"pst{n}", [P, BT, P]) for n in range(2)]
        pss = ps("pss", [P, 512])
        psa = [ps(f"psa{n}", [P, 512]) for n in range(2)]

        slots_in, lo_ready = sem("slots_in"), sem("lo_ready")
        gathered = [sem(f"gathered{n}") for n in range(RING)]
        ix_ready, miss_ready, oh_ready, oh_ps, ohT_ready = (sem(k) for k in (
            "ix_ready", "miss_ready", "oh_ready", "oh_ps", "ohT_ready"))
        best_ready, bestT_ready, smb_ready, cdiff_ready, c_ready, se_ready, z_ready, w_ready, sums_ready = (
            sem(k) for k in ("best_ready", "bestT_ready", "smb_ready", "cdiff_ready", "c_ready", "se_ready", "z_ready",
                             "w_ready", "sums_ready"))
        off_ready = sem("off_ready")
        far_ready = sem("far_ready")
        rows_used, summed = sem("rows_used"), sem("summed")
        chain2 = sem("chain2")

        block = ctx.enter_context(nc.Block())

        @block.sync
        def _(sp):
            sp.dma_start(colx[:, :], slots.rearrange("(p e) o -> p (e o)", p=P)).then_inc(slots_in, 16)

        @block.gpsimd
        def _(pool):
            pool.wait_ge(lo_ready, 1)
            with pool.Fori(0, NB // RING) as i:
                for k in range(RING):
                    j = i * RING + k
                    pool.wait_ge(rows_used, j + 1)
                    pool.sem_inc(pause["pool"], 1)
                    pool.wait_ge(ix_ready, j + 1)
                    pool.sem_inc(pause["pool"], 1)
                    for t in range(BT):
                        pool.indirect_dma_start(G[k][:, t, :], None, table, bass.IndirectOffsetOnAxis(
                            ap=ix[k][:, t:t + 1].bitcast(u32), axis=0)).then_inc(gathered[k], 16)
                    pool.wait_ge(best_ready, j + 1)
                    pool.sem_inc(pause["pool"], 1)
                    pool.tensor_tensor(miss[k % 2][:, :, :], iota_f[:, :].unsqueeze(1).to_broadcast([P, BT, P]),
                                       lo[:, bass.ds(j * BT, BT)].unsqueeze(2).to_broadcast([P, BT, P]),
                                       ALU.subtract).then_inc(off_ready, 1)

        @block.scalar
        def _(act):
            def targets(j, k):
                act.wait_ge(rows_used, j + 1)
                act.sem_inc(pause["act"], 1)
                nc.scalar.copy(ix[k][:, :], colx[:, bass.ds(j * BT, BT)]).then_inc(ix_ready, 1)

            def match(j, k):
                m_ = miss[k % 2]
                act.wait_ge(off_ready, j + 1)
                nc.scalar.activation(m_[:, :, :], m_[:, :, :], ACT.Square, scale=FAR_ROOT).then_inc(miss_ready, 1)
                act.wait_ge(miss_ready, j + 1)
                act.wait_ge(summed, j + 1)
                nc.scalar.activation(oh[k][:, :, :], m_[:, :, :], ACT.Relu, scale=-1.0, bias=one[:, :]).then_inc(oh_ready, 1)

            def turned(j, k):
                act.wait_ge(oh_ps, j + 1)
                nc.scalar.copy(ohT[:, :, :], pst[k % 2][:, :, :]).then_inc(ohT_ready, 1)

            def put_d(j, k, nth):
                act.wait_ge(gathered[k], nth * (16 * BT))
                act.wait_ge(best_ready, j + 1)
                for t in range(XT):
                    for h in range(HEADS):
                        last = nc.scalar.activation(far[k % 2][:, t, h, :], miss[k % 2][:, BT - XT + t, :], ACT.Identity,
                                                    bias=G[k][:, BT - XT + t, DCOL + h:DCOL + h + 1])
                last.then_inc(far_ready, 1)

            def weights(j, k):
                act.wait_ge(cdiff_ready, j + 1)
                nc.scalar.activation(cc[k][:, :], cdiff[:, :], ACT.Exp).then_inc(c_ready, 1)
                act.wait_ge(z_ready, j + 1)
                nc.scalar.activation(w[:, :, :], z[:, :, :], ACT.Exp).then_inc(w_ready, 1)

            act.wait_ge(lo_ready, 1)
            targets(0, 0)
            targets(1, 1)
            match(0, 0)
            put_d(0, 0, 1)
            with act.Fori(0, NB // RING - 1) as i:
                for k in range(RING):
                    j, l = i * RING + k, (k + 1) % RING
                    targets(j + 2, (k + 2) % RING)
                    match(j + 1, l)
                    turned(j, k)
                    put_d(j + 1, l, i + ((k + 1) // RING + 1))
                    weights(j, k)
            for k in range(RING):
                j = NB - RING + k
                if k + 2 < RING:
                    targets(j + 2, k + 2)
                if k + 1 < RING:
                    match(j + 1, k + 1)
                turned(j, k)
                if k + 1 < RING:
                    put_d(j + 1, k + 1, NB // RING)
                weights(j, k)

        @block.vector
        def _(dve):
            V = nc.vector
            link = Link(dve, chain2, pause["dve"])
            dve.sem_inc(rows_used, RING)
            dve.sem_inc(summed, RING)
            dve.sem_inc(best_ready, 2)
            dve.sem_inc(sums_ready, 1)
            dve.wait_ge(slots_in, 16)
            link(V.memset(one[:, :], 1.0))
            link(V.tensor_scalar(lo[:, :].bitcast(i32), colx[:, :], NONE, None, ALU.bitwise_and))
            link(V.tensor_copy(lo[:, :], lo[:, :].bitcast(i32)))
            link(V.tensor_scalar(colx[:, :], colx[:, :], 8, None, ALU.logical_shift_right))
            dve.sem_inc(lo_ready, 1)
            link(V.memset(mx[:, :, :], FAR_ROOT ** 2 * 2))
            link(V.memset(acc[:, :, :], 0.0))

            def weighted(j, k):
                dve.wait_ge(w_ready, j + 1)
                dve.wait_ge(sums_ready, j + 1)
                link.put(V.tensor_tensor(wv[:, :, :, :],
                                     G[k][:, :, 0:DOUT + 1].unsqueeze(2).to_broadcast([P, BT, HEADS, DOUT + 1]),
                                     w[:, :, :].unsqueeze(3).to_broadcast([P, BT, HEADS, DOUT + 1]), ALU.mult),
                         rows_used, j + 1 + RING)

            def bucket(j):
                return nc.values_load_multi_w_load_instructions(
                    bid_i[0:1, bass.ds(j, 1)], engines=[mybir.EngineType.DVE], min_val=0, max_val=TOK - 1,
                    skip_runtime_bounds_check_because="phase 1 clamps the buckets to 0..TOK - 1")[1][0]

            def total(bid):
                return acc[:, bass.ds(bid, 1), :].rearrange("p a (h c) -> p (a h) c", h=HEADS)

            def scaled(j, k, bid):
                dve.wait_ge(c_ready, j + 1)
                link.put(V.tensor_tensor(total(bid), total(bid),
                                         cc[k][:, :].unsqueeze(2).to_broadcast([P, HEADS, DOUT + 1]), ALU.mult))

            def add_up(j, k, bid):
                dve.wait_ge(sums_ready, j + 2)
                link.put(V.tensor_tensor(total(bid), total(bid), psa[k % 2][:, 0:AGG].rearrange("p (h c) -> p h c", h=HEADS),
                                         ALU.add), summed, j + 1 + RING)

            def old(bid):
                m_ = mx[:, bass.ds(bid, 1), :].rearrange("p a h -> p (a h)")
                s_ = s_res[:, bass.ds(bid, 1), :].rearrange("p a h -> p (a h)")
                link.put(V.tensor_tensor(sd[:, HEADS:], s_, m_, ALU.subtract))
                link.put(V.tensor_copy(smb[:, 0:HEADS], s_))
                return m_, s_

            def leaves(i, k):
                j, m_in = i * RING + k, miss[k % 2]
                dve.wait_ge(gathered[k], (i + 1) * (16 * BT))
                dve.wait_ge(miss_ready, j + 1)
                for t in range(BT - XT):
                    for h in range(HEADS):
                        d = G[k][:, t, DCOL + h:DCOL + h + 1]
                        if t == 0:
                            link.put(V.tensor_scalar(best[:, h, :], m_in[:, t, :], d, None, ALU.add))
                        else:
                            link.need(HEADS)
                            link.put(V.scalar_tensor_tensor(best[:, h, :], m_in[:, t, :], d, best[:, h, :],
                                                            ALU.add, ALU.min))
                        yield

            def step(i, k, bids, first):
                j = i * RING + k
                if k == 0:
                    for _ in leaves(i, k):
                        pass
                sums = not (first and k < 2)
                dve.wait_ge(far_ready, j + 1)
                f_ = far[k % 2]
                link.put(V.tensor_tensor(f_[:, 0:XT // 2, :, :], f_[:, 0:XT // 2, :, :], f_[:, XT // 2:, :, :], ALU.min))
                if k == 0 and not first:
                    bids[:] = [bucket(i * RING + n) for n in range(3)]
                link.need()
                link.put(V.tensor_tensor(best[:, :, :], best[:, :, :], f_[:, 0, :, :], ALU.min))
                link.put(V.tensor_tensor(f_[:, 1, :, :], f_[:, 1, :, :], f_[:, 2, :, :], ALU.min))
                if sums:
                    scaled(j - 2, (k - 2) % RING, bids[k])
                if k == 0 and not first:
                    bids.extend(bucket(i * RING + n) for n in range(3, RING + 2))
                if sums:
                    link.need(2)
                else:
                    link.need()
                link.put(V.tensor_tensor(best[:, :, :], best[:, :, :], f_[:, 1, :, :], ALU.min), best_ready, j + 3)
                if sums:
                    link.chained()
                    add_up(j - 2, (k - 2) % RING, bids[k])
                m_, s_ = old(bids[k + 2])
                dve.wait_ge(bestT_ready, j + 1)
                link(V.tensor_reduce(bm[:, :], psb[:, :, :], AX.X, ALU.min))
                link(V.tensor_tensor(m_, m_, bm[:, :], ALU.min))
                link(V.tensor_tensor(sd[:, 0:HEADS], s_, m_, ALU.subtract))
                link(V.scalar_tensor_tensor(smb[:, HEADS:], sd[:, :], SLOPE, sd[:, :], ALU.mult, ALU.max), smb_ready, j + 1)
                if k or not first:
                    weighted(j - 1, (k - 1) % RING)
                link.put(V.tensor_tensor(cdiff[:, :], smb[:, 2 * HEADS:], smb[:, HEADS:2 * HEADS], ALU.subtract), cdiff_ready, j + 1)
                leaf = leaves(i, k + 1) if k + 1 < RING else iter(())
                se = pss[:, 0:BT * 2 * HEADS].rearrange("p (t c) -> p t c", t=BT)
                dve.wait_ge(se_ready, j + 1)
                link.put(V.tensor_tensor(z[:, :, :], se[:, :, 0:HEADS], G[k][:, :, DCOL:DCOL + HEADS], ALU.subtract))
                between = 2 if next(leaf, None) is None and k + 1 < RING else 1
                link.need(between)
                link.put(V.scalar_tensor_tensor(z[:, :, :], z[:, :, :], SLOPE, z[:, :, :], ALU.mult, ALU.max))
                next(leaf, None)
                link.need(between)
                link.put(V.tensor_tensor(z[:, :, :], z[:, :, :], se[:, :, HEADS:], ALU.subtract), z_ready, j + 1)
                for _ in leaf:
                    pass

            bids = [bucket(j) for j in range(RING + 2)]
            for k in range(RING):
                step(0, k, bids, True)
            link.settle()
            per = RING * ((BT - XT) * HEADS + 3 + 5 + 2 + 1)
            link.enter()
            with dve.Fori(1, NB // RING) as i:
                link.loop(i - 1, per)
                bids = []
                for k in range(RING):
                    step(i, k, bids, False)
                link.settle()
                assert link.n == per, (link.n, per)
            link.leave(per * (NB // RING - 1))
            weighted(NB - 1, RING - 1)
            bids = [bucket(NB - RING + k) for k in range(RING + 2)]
            for k in (2, 1):
                scaled(NB - k, RING - k, bids[RING + 2 - k])
                link.need()
                add_up(NB - k, RING - k, bids[RING + 2 - k])
                link.need()
            den = acc[:, :, :].rearrange("p b (h c) -> p b h c", h=HEADS)
            link(V.tensor_scalar(rden[:, :, :], den[:, :, :, DOUT], 1e-30, None, ALU.max))
            link(V.reciprocal(rden[:, :, :], rden[:, :, :]))
            for h in range(HEADS):
                link(V.tensor_tensor(den[:, :, h, 0:DOUT], den[:, :, h, 0:DOUT],
                                     rden[:, :, h].unsqueeze(2).to_broadcast([P, TOK, DOUT]), ALU.mult))
                xs = x2[:, 0:TOK, h * DOUT:(h + 1) * DOUT]
                link(V.tensor_tensor(xs, xs, den[:, :, h, 0:DOUT], ALU.add))
            link.settle()

        @block.tensor
        def _(pe):
            T = nc.tensor

            def turn(j, k):
                pe.wait_ge(oh_ready, j + 1)
                for t in range(BT):
                    last = T.transpose(pst[k % 2][:, t, :], oh[k][:, t, :], ident[:, :])
                last.then_inc(oh_ps, 1)

            def maxima(j):
                pe.wait_ge(best_ready, j + 3)
                for h in range(HEADS):
                    last = T.transpose(psb[:, h, :], best[:, h, :], ident[:, :])
                last.then_inc(bestT_ready, 1)

            def picked(j):
                pe.wait_ge(smb_ready, j + 1)
                pe.wait_ge(ohT_ready, j + 1)
                for t in range(BT):
                    last = T.matmul(pss[:, t * 2 * HEADS:(t + 1) * 2 * HEADS], ohT[:, t, :], smb[:, 0:2 * HEADS],
                                    start=True, stop=True)
                last.then_inc(se_ready, 1)

            def product(j, k):
                pe.wait_ge(rows_used, j + 1 + RING)
                for t in range(BT):
                    last = T.matmul(psa[k % 2][:, 0:AGG], oh[k][:, t, :], wv[:, t, :, :].rearrange("p h c -> p (h c)"),
                                    start=(t == 0), stop=(t == BT - 1))
                last.then_inc(sums_ready, 1)

            def step(j, k, first=False, last=False):
                if not last:
                    turn(j + 1, (k + 1) % RING)
                maxima(j)
                picked(j)
                if not first:
                    product(j - 1, (k - 1) % RING)

            turn(0, 0)
            for k in range(RING):
                step(k, k, first=(k == 0))
            with pe.Fori(1, NB // RING - 1) as i:
                for k in range(RING):
                    step(i * RING + k, k)
            for k in range(RING):
                step(NB - RING + k, k, last=(k == RING - 1))
            product(NB - 1, RING - 1)


def phase3(nc, v):
    x2, ident, iota_f, ones = (v[k] for k in ("x2", "ident", "iota_f", "ones"))
    rwT, rb, E1, b1, E2, b2, out = (v[k] for k in ("rwT", "rb", "E1", "b1", "E2", "b2", "out"))
    pause, sem = v["pause"], v["sem"]
    normal = nc.dram_tensor("normal", ((TOK + 1) * P, C), fp32).ap()
    added = nc.dram_tensor("added", (NP + ST * P, C), fp32).ap()
    eslots = nc.dram_tensor("eslots", (P * ST, 1), i32).ap()
    ctx = ExitStack()
    with ctx:
        def sb(name, shape, dt, c=ctx):
            return c.enter_context(nc.sbuf_tensor(name, shape, dt))

        def ps(name, shape, c=ctx):
            return c.enter_context(nc.psum_tensor(name, shape, fp32))

        e1 = sb("e1", [P, 2, EXP, EH], fp32)
        e1b = sb("e1b", [1, EXP, EH], fp32)
        e2 = sb("e2", [EH + 1, EXP, C], fp32)
        eid_i = sb("eid_i", [1, ST + PLACES + LAG], i32)
        route(nc, v, sb, ps, e1, e1b, e2, eid_i, normal, eslots)
        experts(nc, v, sb, ps, e1, e1b, e2, eid_i, normal, added, eslots)

        parts = TOK // GROUP
        yall = sb("yall", [P, TOK, C], fp32)
        y_in = [sem(f"y_in{n}") for n in range(parts)]
        summed3, all_out = sem("summed3"), sem("all_out")
        with nc.Block() as block:
            @block.sync
            def _(sp):
                for n in range(parts):
                    rows = slice(n * GROUP * P, (n + 1) * GROUP * P)
                    sp.dma_start(yall[:, n * GROUP:(n + 1) * GROUP, :],
                                 added[rows, :].rearrange("(t p) c -> p t c", p=P)).then_inc(y_in[n], 16)
                for n in range(parts):
                    rows = slice(n * GROUP * P, (n + 1) * GROUP * P)
                    sp.wait_ge(summed3, n + 1)
                    sp.dma_start(out[rows, :].rearrange("(t p) c -> p t c", p=P),
                                 yall[:, n * GROUP:(n + 1) * GROUP, :]).then_inc(all_out, 16)
                sp.wait_ge(all_out, 16 * parts)

            @block.vector
            def _(dve):
                for n in range(parts):
                    dve.wait_ge(y_in[n], 16)
                    y_ = yall[:, n * GROUP:(n + 1) * GROUP, :]
                    nc.vector.tensor_tensor(y_, y_, x2[:, n * GROUP:(n + 1) * GROUP, :], ALU.add).then_inc(summed3, 1)


def route(nc, v, sb_, ps_, e1, e1b, e2, eid_i, normal, eslots):
    x2, ident, iota_f, ones = (v[k] for k in ("x2", "ident", "iota_f", "ones"))
    rwT, rb, E1, b1, E2, b2 = (v[k] for k in ("rwT", "rb", "E1", "b1", "E2", "b2"))
    pause, sem = v["pause"], v["sem"]
    EQ = EXP // 4
    SG = 7
    ctx = ExitStack()
    with ctx:
        def sb(name, shape, dt):
            return sb_(name, shape, dt, ctx)

        def ps(name, shape):
            return ps_(name, shape, ctx)

        rw = sb("rw", [P, 2, EXP], fp32)
        rbr = sb("rbr", [P, EXP], fp32)
        st = sb("st3", [P, GROUP, 6], fp32)
        mv = sb("mv3", [P, GROUP, 2], fp32)
        mvs = sb("mvs3", [P, TOK + 2, 2], fp32)
        rstd = sb("rstd3", [P, TOK + 2], fp32)
        rt = sb("rt3", [P, TOK + 2], fp32)
        yn = [sb(f"yn{n}", [P, 1, C], fp32) for n in range(2)]
        ynT = [sb(f"ynT{n}", [P, 2, P], fp32) for n in range(2)]
        before = sb("before3", [P, P], fp32)
        lg = sb("lg", [P, TOK + 1, EXP], fp32)
        most = sb("most", [P, TOK], fp32)
        late = sb("late", [P, EXP], fp32)
        score = sb("score", [P, TOK, EXP], fp32)
        isx = sb("isx", [P, EXP, TOK], fp32)
        cnt = sb("cnt3", [P, EXP, TOK], fp32)
        cum = sb("cum3", [P, EXP, TOK], fp32)
        tot = sb("tot3", [P, EXP], fp32)
        start = sb("start3", [P, EXP], fp32)
        tiles_i = sb("tiles_i", [P, EXP], i32)
        tiles = sb("tiles3", [P, EXP], fp32)
        ends = sb("ends3", [P, EXP], fp32)
        siota = sb("siota", [1, ST], fp32)
        past = sb("past", [1, ST, EXP], fp32)
        eidf = sb("eidf", [1, ST], fp32)
        place = sb("place", [P, TOK], fp32)
        pl_i = sb("pl_i", [P, TOK], i32)
        hi_i = sb("hi_i", [P, TOK], i32)
        node = sb("node", [P, TOK], i32)
        empty = sb("empty", [P, ST], i32)
        node_s = [sb(f"node_s{n}", [P, SG], i32) for n in range(2)]
        pl_s = [sb(f"pl_s{n}", [P, SG], i32) for n in range(2)]
        psT = [ps(f"psT3{n}", [P, 2, P]) for n in range(2)]
        psl = [ps(f"psl{n}", [P, 512]) for n in range(2)]
        psc = ps("psc", [P, 4, 512])

        w3_in, const3, empty_out, yn_sent = sem("w3_in"), sem("const3"), sem("empty_out"), [sem(f"yn_sent{n}") for n in range(2)]
        yn_ready = sem("yn_ready3")
        yT_ready, ynT_ready, l_ready, l_taken = (sem(k) for k in ("yT_ready3", "ynT_ready3", "l_ready3", "l_taken3"))
        isx_ready, counted, cnt_taken, ranked, placed, staged = (sem(k + "3") for k in (
            "isx_ready", "counted", "cnt_taken", "ranked", "placed", "staged"))
        scattered = [sem(f"scattered3{n}") for n in range(2)]
        chain = sem("chain4")
        with nc.Block() as block:
            @block.sync
            def _(sp):
                for dst, src in ((rw[:, :, :], rwT.rearrange("(k p) e -> p k e", p=P)), (rbr[:, :], rb.to_broadcast([P, EXP])),
                                 (e1[:, 0, :, :], E1[:, 0:P, :].rearrange("e p h -> p e h")),
                                 (e1[:, 1, :, :], E1[:, P:2 * P, :].rearrange("e p h -> p e h")),
                                 (e1b[:, :, :].rearrange("o e h -> o (e h)"), b1),
                                 (e2[0:EH, :, :], E2.rearrange("(e h) c -> h e c", h=EH)),
                                 (e2[EH:EH + 1, :, :].rearrange("o e c -> o (e c)"), b2)):
                    sp.dma_start(dst, src).then_inc(w3_in, 16)
                sp.wait_ge(const3, 3)
                sp.dma_start(eslots.rearrange("(p s) o -> p (s o)", p=P), empty[:, :]).then_inc(empty_out, 16)
                with sp.Fori(0, (TOK + 1) // 2) as i:
                    for n in range(2):
                        sp.wait_ge(yn_ready, i * 2 + n + 1)
                        sp.dma_start(normal[bass.ds((i * 2 + n) * P, P), :], yn[n][:, 0, :]).then_inc(yn_sent[n], 16)
                for n in range(2):
                    sp.wait_ge(yn_sent[n], 16 * ((TOK + 1) // 2))
                sp.wait_ge(w3_in, 16 * 7)

            @block.gpsimd
            def _(pool):
                pool.iota(empty[:, :], [[P, ST]], base=NP, channel_multiplier=1).then_inc(const3, 1)
                pool.iota(node[:, :], [[P, TOK]], base=0, channel_multiplier=1).then_inc(const3, 1)
                pool.iota(siota[:, :], [[1, ST]], base=0, channel_multiplier=0,
                          allow_small_or_imprecise_dtypes=True).then_inc(const3, 1)
                pool.memset(before[:, :], 1.0).then_inc(const3, 1)
                pool.wait_ge(const3, 4)
                pool.affine_select(out=before[:, :], in_=before[:, :], compare_op=ALU.is_gt, fill=0.0, base=0,
                                   pattern=[[1, P]], channel_multiplier=-1).then_inc(const3, 1)
                pool.wait_ge(empty_out, 16)
                pool.wait_ge(placed, 1)
                pool.sem_inc(pause["pool"], 1)

                def turn(i, n, wait):
                    if wait:
                        pool.wait_ge(scattered[n], i * (16 * SG))
                        pool.sem_inc(pause["pool"], 1)
                    cols = bass.ds(i * (2 * SG) + n * SG, SG)
                    pool.tensor_copy(node_s[n][:, :], node[:, cols]).then_inc(staged, 1)
                    pool.tensor_copy(pl_s[n][:, :], pl_i[:, cols]).then_inc(staged, 1)
                    pool.wait_ge(staged, i * 4 + 2 * n + 2)
                    pool.sem_inc(pause["pool"], 1)
                    for k in range(SG):
                        pool.indirect_dma_start(eslots, bass.IndirectOffsetOnAxis(ap=pl_s[n][:, k:k + 1].bitcast(u32), axis=0),
                                                node_s[n][:, k:k + 1], None).then_inc(scattered[n], 16)

                for n in range(2):
                    turn(0, n, False)
                with pool.Fori(1, TOK // (2 * SG)) as i:
                    for n in range(2):
                        turn(i, n, True)
                turn(TOK // (2 * SG), 0, True)
                for n in range(2):
                    pool.wait_ge(scattered[n], 16 * SG * (TOK // (2 * SG) + 1 - n))

            @block.scalar
            def _(act):
                with act.Fori(0, (TOK + 1) // 2) as i:
                    for n in range(2):
                        act.wait_ge(yT_ready, i * 2 + n + 3)
                        act.wait_ge(l_ready, i * 2 + n + 1)
                        nc.scalar.copy(ynT[n][:, :, :], psT[n][:, :, :]).then_inc(ynT_ready, 1)

            @block.vector
            def _(dve):
                V = nc.vector
                link = Link(dve, chain, pause["dve"])
                for s_ in (yT_ready, ynT_ready, l_ready, l_taken):
                    dve.sem_inc(s_, 2)
                link(V.memset(mvs[:, TOK:, :], 1.0))
                spreads(V, dve, link, x2, st, mv, mvs, rstd, rt)

                def normed(t, n, nth):
                    if nth is not None:
                        dve.wait_ge(yn_sent[n], nth * 16)
                    dve.wait_ge(yT_ready, t + 1)
                    xi = x2[:, bass.ds(t, 1), :]
                    link.put(V.tensor_scalar(yn[n][:, :, :], xi, mvs[:, bass.ds(t, 1), 0], rstd[:, bass.ds(t, 1)],
                                             ALU.subtract, ALU.mult), yn_ready, t + 1)

                def taken(t, n):
                    dve.wait_ge(l_ready, t + 3)
                    link.put(V.tensor_copy(lg[:, bass.ds(t, 1), :], psl[n][:, 0:EXP].unsqueeze(1)), l_taken, t + 3)

                for n in range(2):
                    normed(n, n, None)
                with dve.Fori(0, TOK // 2) as i:
                    for n in range(2):
                        normed(i * 2 + n + 2, n, i + 1)
                        taken(i * 2 + n, n)
                for n in range(2):
                    taken(TOK - 1 + n, n)
                link.need()
                lt = lg[:, 0:TOK, :]

                def over_e(a):
                    return a.unsqueeze(2).to_broadcast([P, TOK, EXP])

                def over_t(a):
                    return a.unsqueeze(2).to_broadcast([P, EXP, TOK])

                dve.wait_ge(w3_in, 16 * 7)
                link(V.tensor_tensor(lt, lt, rbr[:, :].unsqueeze(1).to_broadcast([P, TOK, EXP]), ALU.add))
                link(V.tensor_reduce(most[:, :], lt, AX.X, ALU.max))
                link(V.tensor_tensor(score[:, :, :], lt, over_e(most[:, :]), ALU.is_ge))
                link(V.tensor_scalar(late[:, :], iota_f[:, 0:EXP], -1.0, float(EXP), ALU.mult, ALU.add))
                link(V.tensor_tensor(score[:, :, :], score[:, :, :], late[:, :].unsqueeze(1).to_broadcast([P, TOK, EXP]), ALU.mult))
                link(V.tensor_reduce(most[:, :], score[:, :, :], AX.X, ALU.max))
                link(V.tensor_tensor(isx[:, :, :].rearrange("p e t -> p t e"), score[:, :, :], over_e(most[:, :]), ALU.is_equal),
                     isx_ready, 1)
                dve.wait_ge(counted, 1)
                link(V.tensor_copy(cnt[:, :, :].rearrange("p (a b) t -> p a (b t)", a=4), psc[:, :, 0:EQ * TOK]), cnt_taken, 1)
                flat = [a[:, :, :].rearrange("p e t -> p (e t)") for a in (cum, cnt)]
                link(V.tensor_tensor_scan(flat[0], ones[:, 0:1].to_broadcast([P, EXP * TOK]), flat[1], 0.0, ALU.mult, ALU.add))
                link(V.tensor_tensor(flat[0], flat[0], flat[1], ALU.subtract))
                link(V.tensor_reduce(tot[:, :], cnt[:, :, :], AX.X, ALU.add))
                link(V.tensor_tensor_scan(start[:, :], ones[:, 0:EXP], tot[:, :], 0.0, ALU.mult, ALU.add))
                link(V.tensor_tensor(start[:, :], start[:, :], tot[:, :], ALU.subtract))
                link(V.tensor_scalar(tiles_i[:, :], tot[:, :], float(P - 1), None, ALU.add))
                link(V.tensor_scalar(tiles_i[:, :], tiles_i[:, :], P.bit_length() - 1, None, ALU.arith_shift_right))
                link(V.tensor_copy(tiles[:, :], tiles_i[:, :]))
                link(V.tensor_tensor_scan(ends[:, :], ones[:, 0:EXP], tiles[:, :], 0.0, ALU.mult, ALU.add))
                link(V.tensor_tensor(tiles[:, :], ends[:, :], tiles[:, :], ALU.subtract))
                link(V.scalar_tensor_tensor(start[:, :], tiles[:, :], float(P), start[:, :], ALU.mult, ALU.subtract))
                link(V.tensor_tensor(cum[:, :, :], cum[:, :, :], over_t(start[:, :]), ALU.add))
                dve.wait_ge(ranked, 1)
                link(V.tensor_tensor(cum[:, :, :].rearrange("p (a b) t -> p a (b t)", a=4),
                                     cum[:, :, :].rearrange("p (a b) t -> p a (b t)", a=4), psc[:, :, 0:EQ * TOK], ALU.add))
                link(V.tensor_tensor(cum[:, :, :], cum[:, :, :], isx[:, :, :], ALU.mult))
                link(V.tensor_reduce(place[:, :], cum[:, :, :].rearrange("p e t -> p t e"), AX.X, ALU.add))
                link(V.tensor_copy(pl_i[:, :], place[:, :]))
                link(V.tensor_scalar(hi_i[:, :], pl_i[:, :], P.bit_length() - 1, None, ALU.arith_shift_right))
                link(V.tensor_scalar(pl_i[:, :], pl_i[:, :], P - 1, None, ALU.bitwise_and))
                link(V.scalar_tensor_tensor(pl_i[:, :], pl_i[:, :], float(ST), hi_i[:, :], ALU.mult, ALU.add), placed, 1)
                dve.wait_ge(const3, 5)
                link(V.tensor_tensor(past[:, :, :], siota[:, :].unsqueeze(2).to_broadcast([1, ST, EXP]),
                                     ends[0:1, :].unsqueeze(1).to_broadcast([1, ST, EXP]), ALU.is_ge))
                link(V.tensor_reduce(eidf[:, :], past[:, :, :], AX.X, ALU.add))
                link(V.tensor_scalar(eidf[:, :], eidf[:, :], float(EXP - 1), None, ALU.min))
                link(V.memset(eid_i[:, :], 0))
                link(V.tensor_copy(eid_i[:, LAG:LAG + ST], eidf[:, :]))
                link.settle()

            @block.tensor
            def _(pe):
                T = nc.tensor
                pe.wait_ge(w3_in, 16 * 7)

                def turn(t, n):
                    pe.wait_ge(yn_ready, t + 1)
                    pe.wait_ge(ynT_ready, t + 1)
                    for k in range(2):
                        last = T.transpose(psT[n][:, k, :], yn[n][:, 0, k * P:(k + 1) * P], ident[:, :])
                    last.then_inc(yT_ready, 1)

                def logits(t, n):
                    pe.wait_ge(ynT_ready, t + 3)
                    pe.wait_ge(l_taken, t + 1)
                    for k in range(2):
                        last = T.matmul(psl[n][:, 0:EXP], ynT[n][:, k, :], rw[:, k, :], start=(k == 0), stop=(k == 1))
                    last.then_inc(l_ready, 1)

                turn(0, 0)
                with pe.Fori(0, TOK // 2) as i:
                    for n in range(2):
                        turn(i * 2 + n + 1, 1 - n)
                        logits(i * 2 + n, n)
                turn(TOK, 1)
                logits(TOK - 1, 0)
                logits(TOK, 1)
                pe.wait_ge(isx_ready, 1)
                pe.wait_ge(const3, 5)
                flat = isx[:, :, :].rearrange("p (a b) t -> p a (b t)", a=4)
                for q in range(4):
                    last = T.matmul(psc[:, q, 0:EQ * TOK], ones[:, :], flat[:, q, :], start=True, stop=True)
                last.then_inc(counted, 1)
                pe.wait_ge(cnt_taken, 1)
                for q in range(4):
                    last = T.matmul(psc[:, q, 0:EQ * TOK], before[:, :], flat[:, q, :], start=True, stop=True)
                last.then_inc(ranked, 1)


def experts(nc, v, sb_, ps_, e1, e1b, e2, eid_i, normal, added, eslots):
    ident, ones = v["ident"], v["ones"]
    pause, sem = v["pause"], v["sem"]
    ctx = ExitStack()
    with ctx:
        def sb(name, shape, dt):
            return sb_(name, shape, dt, ctx)

        def ps(name, shape):
            return ps_(name, shape, ctx)

        nodes = sb("nodes", [P, ST], i32)
        rows = sb("rows", [P, ST], i32)
        ixg = [sb(f"ixg{n}", [P, 1], i32) for n in range(PLACES)]
        ixy = [sb(f"ixy{n}", [P, 1], i32) for n in range(PLACES)]
        g = [sb(f"g{n}", [P, C], fp32) for n in range(PLACES)]
        gT = [sb(f"gT{n}", [P, 2, P], fp32) for n in range(2)]
        h = [sb(f"h{n}", [P, P], fp32) for n in range(2)]
        hT = [sb(f"hT3{n}", [EH + 1, P], fp32) for n in range(2)]
        y = [sb(f"y{n}", [P, C], fp32) for n in range(PLACES)]
        psg = [ps(f"psg{n}", [P, 2, P]) for n in range(2)]
        psh = [ps(f"psh{n}", [P, 512]) for n in range(2)]
        psht = [ps(f"psht{n}", [P, 512]) for n in range(2)]
        psy = [ps(f"psy{n}", [P, 512]) for n in range(2)]

        nodes_in, at, gathered4 = sem("nodes_in"), sem("at"), [sem(f"gathered4{n}") for n in range(PLACES)]
        h_set, rows_ready = sem("h_set"), sem("rows_ready")
        g_turned = sem("g_turned")
        g_copied, h_ready, h_copied, h_turned, hT_copied, y_ready, y_copied = (sem(k + "4") for k in (
            "g_copied", "h_ready", "h_copied", "h_turned", "hT_copied", "y_ready", "y_copied"))
        y_sent = [sem(f"y_sent{n}") for n in range(PLACES)]
        with nc.Block() as block:
            def steps(eng, step):
                for i in range(2):
                    for k in range(PLACES):
                        step(i * PLACES + k, k, i, 0, ST)
                with eng.Fori(2, ST // PLACES) as i:
                    for k in range(PLACES):
                        step(i * PLACES + k, k, i, None, None)
                for k in range(LAG):
                    step(ST + k, k, ST // PLACES, 0, ST)

            def there(s, lag, low, high):
                return low is None or low <= s - lag < high

            @block.sync
            def _(sp):
                sp.dma_start(nodes[:, :], eslots.rearrange("(p s) o -> p (s o)", p=P)).then_inc(nodes_in, 16)

            @block.gpsimd
            def _(pool):
                pool.wait_ge(rows_ready, 1)
                pool.sem_inc(pause["pool"], 1)

                def gather(t, k, count):
                    if not isinstance(t, int) or t >= PLACES:
                        pool.wait_ge(g_turned, t - PLACES + 2)
                        pool.sem_inc(pause["pool"], 1)
                    pool.tensor_copy(ixg[k][:, :], rows[:, bass.ds(t, 1)]).then_inc(at, 1)
                    pool.wait_ge(at, count)
                    pool.sem_inc(pause["pool"], 1)
                    pool.indirect_dma_start(g[k][:, :], None, normal, bass.IndirectOffsetOnAxis(
                        ap=ixg[k][:, :].bitcast(u32), axis=0)).then_inc(gathered4[k], 16)

                def scatter(t, k, nth, count):
                    if nth is not None:
                        pool.wait_ge(y_sent[k], nth * 16)
                        pool.sem_inc(pause["pool"], 1)
                    pool.tensor_copy(ixy[k][:, :], nodes[:, bass.ds(t, 1)]).then_inc(at, 1)
                    pool.wait_ge(at, count)
                    pool.wait_ge(y_copied, t + 3)
                    pool.sem_inc(pause["pool"], 1)
                    pool.indirect_dma_start(added, bass.IndirectOffsetOnAxis(ap=ixy[k][:, :].bitcast(u32), axis=0),
                                            y[k][:, :], None).then_inc(y_sent[k], 16)

                for k in range(PLACES):
                    gather(k, k, k + 1)

                def turn(i, nth):
                    for k in range(PLACES):
                        t = i * PLACES + k
                        scatter(t, k, nth, t * 2 + PLACES + 1)
                        gather(t + PLACES, k, t * 2 + PLACES + 2)

                turn(0, None)
                with pool.Fori(1, ST // PLACES - 1) as i:
                    turn(i, i)
                for k in range(PLACES):
                    t = ST - PLACES + k
                    scatter(t, k, ST // PLACES - 1, 2 * (ST - PLACES) + PLACES + k + 1)
                for k in range(PLACES):
                    pool.wait_ge(y_sent[k], 16 * (ST // PLACES))

            @block.scalar
            def _(act):
                def step(s, k, i, low, high):
                    n = k % 2
                    if there(s, 0, low, high):
                        act.wait_ge(g_turned, s + 2)
                        act.wait_ge(h_ready, s + 1)
                        nc.scalar.copy(gT[n][:, :, :], psg[n][:, :, :]).then_inc(g_copied, 1)
                    if there(s, 1, low, high):
                        act.wait_ge(h_ready, s + 2)
                        act.wait_ge(h_turned, s)
                        nc.scalar.activation(h[1 - n][:, 0:EH], psh[1 - n][:, 0:EH], ACT.Relu).then_inc(h_copied, 1)

                act.wait_ge(h_set, 2)
                steps(act, step)

            @block.vector
            def _(dve):
                V = nc.vector
                dve.wait_ge(nodes_in, 16)
                V.tensor_scalar(rows[:, :], nodes[:, :], float(NP), None, ALU.min).then_inc(rows_ready, 1)
                dve.sem_inc(g_turned, 1)
                for s_ in (g_copied, h_ready, h_copied, h_turned, y_ready, y_copied):
                    dve.sem_inc(s_, 2)
                dve.sem_inc(hT_copied, 2)
                for n in range(2):
                    V.memset(h[n][:, 0:EH], 0.0)
                    V.memset(h[n][:, EH:EH + 1], 1.0)
                    V.memset(h[n][:, EH + 1:], 0.0).then_inc(h_set, 1)

                def step(s, k, i, low, high):
                    n = k % 2
                    if there(s, 2, low, high):
                        dve.wait_ge(h_turned, s + 1)
                        dve.wait_ge(y_ready, s - 1)
                        V.tensor_copy(hT[n][:, :], psht[n][0:EH + 1, 0:P]).then_inc(hT_copied, 1)
                    if there(s, LAG, low, high):
                        nth = i if k >= LAG else i - 1
                        dve.wait_ge(y_ready, s - LAG + 3)
                        if not isinstance(nth, int) or nth > 0:
                            dve.wait_ge(y_sent[(k - LAG) % PLACES], nth * 16)
                        V.tensor_scalar(y[(k - LAG) % PLACES][:, :], psy[1 - n][:, 0:C], 0.0, None, ALU.max).then_inc(y_copied, 1)

                steps(dve, step)

            @block.tensor
            def _(pe):
                T = nc.tensor
                eids = []

                def load(i):
                    eids[:] = nc.values_load_multi_w_load_instructions(
                        eid_i[0:1, bass.ds(i * PLACES, PLACES + LAG)], engines=[mybir.EngineType.PE], min_val=0,
                        max_val=EXP - 1,
                        skip_runtime_bounds_check_because="route clamps the experts to 0..EXP - 1")[1]

                def step(s, k, i, low, high):
                    n = k % 2
                    if k == 0:
                        load(i)
                    if there(s, 0, low, high):
                        pe.wait_ge(gathered4[k], i * 16 + 16)
                        pe.wait_ge(g_copied, s + 1)
                        for c in range(2):
                            last = T.transpose(psg[n][:, c, :], g[k][:, c * P:(c + 1) * P], ident[:, :])
                        last.then_inc(g_turned, 1)
                    if there(s, 1, low, high):
                        w_ = bass.ds(eids[k + LAG - 1], 1)
                        pe.wait_ge(g_copied, s + 2)
                        pe.wait_ge(h_copied, s)
                        for c in range(2):
                            T.matmul(psh[1 - n][:, 0:EH], gT[1 - n][:, c, :], e1[:, c, w_, :].rearrange("p e h -> p (e h)"),
                                     start=(c == 0), stop=False)
                        T.matmul(psh[1 - n][:, 0:EH], ones[0:1, :], e1b[:, w_, :].rearrange("p e h -> p (e h)"),
                                 start=False, stop=True).then_inc(h_ready, 1)
                    if there(s, 2, low, high):
                        pe.wait_ge(h_copied, s + 1)
                        pe.wait_ge(hT_copied, s - 1)
                        T.transpose(psht[n][:, 0:P], h[n][:, :], ident[:, :]).then_inc(h_turned, 1)
                    if there(s, LAG, low, high):
                        w_ = bass.ds(eids[k], 1)
                        pe.wait_ge(hT_copied, s - LAG + 3)
                        pe.wait_ge(y_copied, s - LAG + 1)
                        T.matmul(psy[1 - n][:, 0:C], hT[1 - n][:, :], e2[:, w_, :].rearrange("p e c -> p (e c)"),
                                 start=True, stop=True).then_inc(y_ready, 1)

                steps(pe, step)


_INS = ["x", "row", "col", "W", "WT", "b", "a", "Wqkv", "Wm", "W1", "W2", "lnp", "rwT", "rb", "E1", "b1", "E2", "b2"]


def kernel(**inputs):
    import numpy as _np
    import concourse.bacc as _bacc
    from concourse import mybir as _mybir
    from concourse.bass_utils import run_bass_kernel_spmd as _run

    g = {k: _np.asarray(v) for k, v in inputs.items()}

    def edges(v, fill):
        return _np.concatenate([v, _np.full(P * EC - E, fill, v.dtype)]).reshape(P, EC)

    host = {
        "x": _np.concatenate([g["x"], _np.zeros((NP - N, C), g["x"].dtype)]),
        "row": edges(g["src"], NP - 1), "col": edges(g["dst"], 0),
        "W": g["L0_gnn_W"], "WT": g["L0_gnn_W"].T, "b": g["L0_gnn_b"].reshape(DOUT, 1),
        "a": _np.concatenate([g["L0_gnn_a_dst"], g["L0_gnn_a_src"]]).T,
        "Wqkv": _np.concatenate([g["L0_mix_Wq"], g["L0_mix_Wk"], g["L0_mix_Wv"]], axis=1),
        "Wm": g["L0_mix_Wm"], "W1": g["L0_mix_W1"], "W2": g["L0_mix_W2"],
        "lnp": _np.stack([g["L0_mix_g1"], g["L0_mix_b1"], g["L0_mix_g2"], g["L0_mix_b2"]]),
        "rwT": g["L0_ffn_router_w"].T, "rb": g["L0_ffn_router_b"].reshape(1, EXP),
        "E1": g["L0_ffn_W1"], "b1": g["L0_ffn_b1"].reshape(1, EXP * EH),
        "E2": g["L0_ffn_W2"].reshape(EXP * EH, C), "b2": g["L0_ffn_b2"].reshape(1, EXP * C),
    }
    nc = _bacc.Bacc("TRN2", target_bir_lowering=False, num_devices=1)
    arrays, args = {}, []
    for name in _INS:
        arr = _np.ascontiguousarray(host[name])
        arrays[f"in_{name}_dram"] = arr
        args.append(nc.dram_tensor(f"in_{name}_dram", arr.shape, _mybir.dt.from_np(arr.dtype), kind="ExternalInput").ap())
    args.append(nc.dram_tensor("out_0_dram", (NP, C), fp32, kind="ExternalOutput").ap())
    build(nc, *args)
    r = _run(nc, [arrays], core_ids=[0])
    return r.results[0]["out_0_dram"][:N]
```
